# Optimizing a Trainium2 kernel written in Bass

```python
import numpy as np
import jax
import jax.numpy as jnp

def _softmax(x, axis=-1):
    return jax.nn.softmax(x, axis=axis)

def _gelu(x):
    return jax.nn.gelu(x, approximate=True)

def _silu(x):
    return jax.nn.silu(x)

def _sigmoid(x):
    return jax.nn.sigmoid(x)

def _layernorm(x, axis=-1, eps=1e-05):
    m = jnp.mean(x, axis=axis, keepdims=True)
    v = jnp.var(x, axis=axis, keepdims=True)
    return (x - m) / jnp.sqrt(v + eps)

def _scatter_add(tgt, idx, src, axis=0):
    return tgt.at[idx].add(src)

def _segment_sum(src, seg, n):
    return jax.ops.segment_sum(src, seg, n)
kernel_name = 'mk_gnn_preln_d2_gnn_r64_205209'

def setup_inputs(seed: int=0):
    np.random.seed(seed)
    _w = jnp.asarray

    def _rec_inputs():
        import jax
        import jax.numpy as jnp
        _gk = jax.random.key(seed)
        x = -0.0005121 + 1.001 * jax.random.normal(jax.random.fold_in(_gk, 1), (50000, 64), jnp.float32)
        src = jax.random.randint(jax.random.fold_in(_gk, 2), (25000,), 0, 50000, jnp.int32)
        dst = jnp.minimum((50000 * jax.random.uniform(jax.random.fold_in(_gk, 3), (25000,)) ** 2.0).astype(jnp.int32), 49999)
        _o = jnp.argsort(dst, stable=True)
        src = src[_o]
        dst = dst[_o]
        edge_attr_64 = -9.77346e-05 + 0.999888 * jax.random.normal(jax.random.fold_in(_gk, 12), (25000, 64), jnp.float32)
        edge_type_4 = jax.random.randint(jax.random.fold_in(_gk, 13), (25000,), 0, 4, jnp.int32)
        return (x, src, dst, edge_attr_64, edge_type_4)
    x, src, dst, edge_attr_64, edge_type_4 = _rec_inputs()

    def _L0_gnn_setup():
        import jax, jax.numpy as jnp
        import numpy as np
        N_NODES = 50000
        N_EDGES = 12500
        NDIM_IN = 64
        EDIMS = 64
        NDIM_OUT = 64
        key = jax.random.key(seed)
        ks = jax.random.split(key, 8)
        nfeats = jax.random.normal(ks[0], (N_NODES, NDIM_IN), dtype=jnp.float32)
        efeats = jax.random.normal(ks[1], (N_EDGES, EDIMS), dtype=jnp.float32)
        src = jax.random.randint(ks[2], (N_EDGES,), 0, N_NODES, dtype=jnp.int64 if jax.config.jax_enable_x64 else jnp.int32)
        dst = jax.random.randint(ks[3], (N_EDGES,), 0, N_NODES, dtype=jnp.int64 if jax.config.jax_enable_x64 else jnp.int32)
        scale_msg = 1.0 / np.sqrt(NDIM_IN + EDIMS)
        scale_app = 1.0 / np.sqrt(NDIM_IN + NDIM_OUT)
        W_msg_w = jax.random.normal(ks[4], (NDIM_OUT, NDIM_IN + EDIMS), dtype=jnp.float32) * scale_msg
        W_msg_b = jax.random.normal(ks[5], (NDIM_OUT,), dtype=jnp.float32) * scale_msg
        W_apply_w = jax.random.normal(ks[6], (NDIM_OUT, NDIM_IN + NDIM_OUT), dtype=jnp.float32) * scale_app
        W_apply_b = jax.random.normal(ks[7], (NDIM_OUT,), dtype=jnp.float32) * scale_app
        return {'nfeats': nfeats, 'efeats': efeats, 'src': src, 'dst': dst, 'W_msg_w': W_msg_w, 'W_msg_b': W_msg_b, 'W_apply_w': W_apply_w, 'W_apply_b': W_apply_b}
    _L0_gnn_all = _L0_gnn_setup()
    _L0_gnn_in = {k: v for k, v in _L0_gnn_all.items() if k in ('W_msg_w', 'W_msg_b', 'W_apply_w', 'W_apply_b')}
    del _L0_gnn_all

    def _L1_gnn_setup():
        import jax, jax.numpy as jnp
        import numpy as np
        N_NODES = 50000
        N_EDGES = 12500
        DIM = 64
        N_ETYPES = 4
        N_STEPS = 5

        def _gru_cell(a, h, w_ih, w_hh, b_ih, b_hh):
            gi = a @ w_ih.T + b_ih
            gh = h @ w_hh.T + b_hh
            i_r, i_z, i_n = jnp.split(gi, 3, axis=-1)
            h_r, h_z, h_n = jnp.split(gh, 3, axis=-1)
            r = jax.nn.sigmoid(i_r + h_r)
            z = jax.nn.sigmoid(i_z + h_z)
            n = jnp.tanh(i_n + r * h_n)
            return (1.0 - z) * n + z * h
        key = jax.random.key(seed)
        ks = jax.random.split(key, 10)
        feat = jax.random.normal(ks[0], (N_NODES, DIM), dtype=jnp.float32)
        src = jax.random.randint(ks[1], (N_EDGES,), 0, N_NODES, dtype=jnp.int32)
        dst = jax.random.randint(ks[2], (N_EDGES,), 0, N_NODES, dtype=jnp.int32)
        etypes = jax.random.randint(ks[3], (N_EDGES,), 0, N_ETYPES, dtype=jnp.int32)
        gain = float(np.sqrt(2.0))
        std = gain * float(np.sqrt(2.0 / (DIM + DIM)))
        W = jax.random.normal(ks[4], (N_ETYPES, DIM, DIM), dtype=jnp.float32) * std
        b = jnp.zeros((N_ETYPES, DIM), dtype=jnp.float32)
        bound = 1.0 / float(np.sqrt(DIM))
        w_ih = jax.random.uniform(ks[5], (3 * DIM, DIM), minval=-bound, maxval=bound, dtype=jnp.float32)
        w_hh = jax.random.uniform(ks[6], (3 * DIM, DIM), minval=-bound, maxval=bound, dtype=jnp.float32)
        b_ih = jax.random.uniform(ks[7], (3 * DIM,), minval=-bound, maxval=bound, dtype=jnp.float32)
        b_hh = jax.random.uniform(ks[8], (3 * DIM,), minval=-bound, maxval=bound, dtype=jnp.float32)
        return {'feat': feat, 'W': W, 'b': b, 'w_ih': w_ih, 'w_hh': w_hh, 'b_ih': b_ih, 'b_hh': b_hh, 'src': src, 'dst': dst, 'etypes': etypes}
    _L1_gnn_all = _L1_gnn_setup()
    _L1_gnn_in = {k: v for k, v in _L1_gnn_all.items() if k in ('W', 'b', 'w_ih', 'w_hh', 'b_ih', 'b_hh')}
    del _L1_gnn_all
    return {'x': x, 'src': src, 'dst': dst, 'edge_attr_64': edge_attr_64, 'edge_type_4': edge_type_4, 'L0_gnn_W_msg_w': _L0_gnn_in['W_msg_w'], 'L0_gnn_W_msg_b': _L0_gnn_in['W_msg_b'], 'L0_gnn_W_apply_w': _L0_gnn_in['W_apply_w'], 'L0_gnn_W_apply_b': _L0_gnn_in['W_apply_b'], 'L1_gnn_W': _L1_gnn_in['W'], 'L1_gnn_b': _L1_gnn_in['b'], 'L1_gnn_w_ih': _L1_gnn_in['w_ih'], 'L1_gnn_w_hh': _L1_gnn_in['w_hh'], 'L1_gnn_b_ih': _L1_gnn_in['b_ih'], 'L1_gnn_b_hh': _L1_gnn_in['b_hh']}

def reference(x, src, dst, edge_attr_64, edge_type_4, L0_gnn_W_msg_w, L0_gnn_W_msg_b, L0_gnn_W_apply_w, L0_gnn_W_apply_b, L1_gnn_W, L1_gnn_b, L1_gnn_w_ih, L1_gnn_w_hh, L1_gnn_b_ih, L1_gnn_b_hh):
    import jax
    import jax.numpy as jnp

    def _L0_gnn_ref(nfeats, efeats, src, dst, W_msg_w, W_msg_b, W_apply_w, W_apply_b):
        import jax, jax.numpy as jnp
        import numpy as np
        N_NODES = 50000
        N_EDGES = 12500
        NDIM_IN = 64
        EDIMS = 64
        NDIM_OUT = 64
        src_h = nfeats[src]
        msg_in = jnp.concatenate([src_h, efeats], axis=1)
        m = msg_in @ W_msg_w.T + W_msg_b
        agg = jax.ops.segment_sum(m, dst, num_segments=N_NODES)
        deg = jax.ops.segment_sum(jnp.ones((m.shape[0],), m.dtype), dst, num_segments=N_NODES)
        h_neigh = agg / jnp.maximum(deg, 1.0)[:, None]
        apply_in = jnp.concatenate([nfeats, h_neigh], axis=1)
        return jax.nn.relu(apply_in @ W_apply_w.T + W_apply_b)

    def _L1_gnn_ref(feat, W, b, w_ih, w_hh, b_ih, b_hh, src, dst, etypes):
        import jax, jax.numpy as jnp
        import numpy as np
        N_NODES = 50000
        N_EDGES = 12500
        DIM = 64
        N_ETYPES = 4
        N_STEPS = 5

        def _gru_cell(a, h, w_ih, w_hh, b_ih, b_hh):
            gi = a @ w_ih.T + b_ih
            gh = h @ w_hh.T + b_hh
            i_r, i_z, i_n = jnp.split(gi, 3, axis=-1)
            h_r, h_z, h_n = jnp.split(gh, 3, axis=-1)
            r = jax.nn.sigmoid(i_r + h_r)
            z = jax.nn.sigmoid(i_z + h_z)
            n = jnp.tanh(i_n + r * h_n)
            return (1.0 - z) * n + z * h
        n_nodes = feat.shape[0]
        h = feat
        for _ in range(N_STEPS):
            h_all = jnp.einsum('nd,ted->nte', h, W) + b
            m = h_all[src, etypes]
            a = jax.ops.segment_sum(m, dst, num_segments=n_nodes)
            h = _gru_cell(a, h, w_ih, w_hh, b_ih, b_hh)
        return h
    h = jnp.maximum(_layernorm(x, axis=-1), 0.0)
    x = x + _L0_gnn_ref(h, edge_attr_64, src, dst, L0_gnn_W_msg_w, L0_gnn_W_msg_b, L0_gnn_W_apply_w, L0_gnn_W_apply_b)
    h = jnp.maximum(_layernorm(x, axis=-1), 0.0)
    x = x + _L1_gnn_ref(h, L1_gnn_W, L1_gnn_b, L1_gnn_w_ih, L1_gnn_w_hh, L1_gnn_b_ih, L1_gnn_b_hh, src, dst, edge_type_4)
    return x

_drawn_inputs = setup_inputs


def setup_inputs(seed=0):
    import zlib

    import numpy as np

    out = dict(_drawn_inputs(seed))
    spreads = {'L1_gnn_b': (0.0, 0.1)}
    factors = {}
    for name, (base, spread) in spreads.items():
        noise = np.random.default_rng([zlib.crc32(name.encode()), seed]).standard_normal(out[name].shape)
        drawn = base * np.exp(spread * noise) if base else spread * noise
        out[name] = jnp.asarray(drawn.astype(out[name].dtype))
    for name, factor in factors.items():
        out[name] = (out[name] * factor).astype(out[name].dtype)
    return out
```

```python
import concourse.bass as bass
from concourse import mybir
from contextlib import ExitStack

F32 = mybir.dt.float32
I32 = mybir.dt.int32
BF16 = mybir.dt.bfloat16
U8 = mybir.dt.uint8
ALU = mybir.AluOpType
ACT = mybir.ActivationFunctionType
AX = mybir.AxisListType

P = 128
N = 50000
E = 25000
D = 64
NT = 4
STEPS = 5
EPS = 1e-5
ET = -(-E // P)
Q = 4
NQ = ET // Q
R = 7
NR = NQ // R
BT = N // P
NB = P * BT
TAIL = N - NB
G = 6
NG = BT // G
ROWS = NB + P * ET
SKIP = 1000000
TAIL_P = E % P


def flat(ap):
    return ap.rearrange("p a b -> p (a b)")


def pipeline(eng, n, lags, back=2):
    deep = max(lag for lag, _ in lags)
    for s in range(deep + back):
        for lag, body in lags:
            if s >= lag:
                body(s - lag)
    with eng.Fori(deep + back, n) as s:
        for lag, body in lags:
            body(s - lag)
    for s in range(n, n + deep):
        for lag, body in lags:
            if s - lag < n:
                body(s - lag)


class Steps:

    def __init__(self, sem, per):
        self.sem, self.per = sem, per

    def begin(self, eng, it):
        self.eng, self.it, self.done = eng, it, 0

    def mark(self, ins):
        self.done += 1
        assert self.done <= self.per
        ins.then_inc(self.sem, 1)

    def link(self, ins):
        self.mark(ins)
        self.eng.wait_ge(self.sem, self.per * self.it + self.done)

    def end(self):
        assert self.done == self.per, (self.done, self.per)

    def wait(self, eng, it, k=None):
        if isinstance(it, int) and it < 0:
            return
        eng.wait_ge(self.sem, self.per * it + (self.per if k is None else k))


def program(nc, x, edge_attr, dst_col, dst_next, dst_row, prev_last, src_col, slot_node, type_col,
            wm_t, bm, wa_t, ba, wl_t, bl, wih_t, whh_t, bih, bhh, out):
    ctx = ExitStack()
    with ctx:
        def sb(name, shape, dt=F32):
            return ctx.enter_context(nc.sbuf_tensor(name, shape, dt))

        def sem(name):
            return ctx.enter_context(nc.semaphore(name))

        node_row = nc.dram_tensor("node_row", [N, 1], I32, kind="Internal").ap()
        h0_tab = nc.dram_tensor("h0_tab", [N, D], F32, kind="Internal").ap()
        x1_tab = nc.dram_tensor("x1_tab", [ROWS, D], F32, kind="Internal").ap()
        state = [nc.dram_tensor(f"state{k}", [ROWS, D], F32, kind="Internal").ap() for k in range(STEPS)]

        def node_part(tab):
            return tab[0:NB, :].rearrange("(p t) d -> p (t d)", t=BT)

        def slot_part(tab):
            return tab[NB:ROWS, :].rearrange("(p t) d -> p (t d)", t=ET)

        ident = sb("ident", [P, P])
        eps = sb("eps", [P, 1])
        wm = sb("wm", [P, D])
        bm_all = sb("bm_all", [P, D])
        wa1 = sb("wa1", [D + 1, D])
        wa2 = sb("wa2", [D + 1, D + 1])
        wl = sb("wl", [D + 1, NT * D])
        wg = sb("wg", [P, 4 * D])
        wh = sb("wh", [D + 1, 4 * D])
        h_slot = sb("h_slot", [P, ET * D])
        brow_i = h_slot[0:D + 1, 0:4 * D]
        brow_h = h_slot[0:D + 1, 4 * D:8 * D]
        b3f = h_slot[0:3, 8 * D:16 * D].rearrange("p (a b) -> p a b", b=4 * D)
        b3acc = h_slot[0:3, 16 * D:24 * D].rearrange("p (a b) -> p a b", b=4 * D)
        b3part = h_slot[0:3, 24 * D:28 * D].bitcast(BF16).rearrange("p (a b) -> p a b", b=4 * D)
        last_f = h_slot[:, 32 * D:32 * D + ET]
        dstn_i = h_slot[:, 36 * D:36 * D + ET].bitcast(I32)
        bias3 = sb("bias3", [3, 4 * D], BF16)
        ones3 = sb("ones3", [3, P], BF16)
        dst_i = sb("dst_i", [P, ET], I32)
        src_i = sb("src_i", [P, ET], I32)
        slot_i = sb("slot_i", [P, ET], I32)
        type_i = sb("type_i", [P, ET], I32)
        prev_i = sb("prev_i", [D + 1, ET], I32)
        dst_f = sb("dst_f", [P, ET])
        prev_f = sb("prev_f", [D + 1, ET])
        own_idx = sb("own_idx", [P, ET], I32)
        slot_row = sb("slot_row", [P, ET], I32)
        node_ids = sb("node_ids", [P, BT], I32)
        tail_rows = sb("tail_rows", [TAIL, 1], I32)
        tail_now = sb("tail_now", [P, 1], I32)
        tail_f = sb("tail_f", [P, 4])
        cand = sb("cand", [P, 1], I32)
        src_row = sb("src_row", [P, ET], I32)
        tmask = sb("tmask", [P, 3, ET], I32)
        tm_st = sb("tm_st", [P, 3, Q], I32)
        same = sb("same", [P, ET * P], BF16)
        cont = sb("cont", [D + 1, ET * P], U8)
        idx_st = sb("idx_st", [P, 2, R * Q], I32)
        val_st = sb("val_st", [P, R * Q], I32)
        rings = sb("rings", [P, 2 * R * Q * D])
        ring, xring = rings[:, 0:R * Q * D], rings[:, R * Q * D:2 * R * Q * D]
        drow = rings[:, :].bitcast(I32)
        nring = sb("nring", [P, 4 * G * D])
        nring2 = sb("nring2", [P, 4 * G * D])
        assert R * Q * P == 2 * R * Q * D
        stage = sb("stage", [P, G, D])
        stage2 = sb("stage2", [P, Q, D])
        he = sb("he", [P, Q, 2 * D])
        hT = sb("hT", [D + 1, G * P])
        heT = sb("heT", [P, Q * P])
        m = sb("m", [P, Q, D])
        mres = sb("mres", [P, Q, D])
        parts = sb("parts", [P, 3, Q, D + 1], BF16)
        stack = sb("stack", [P, Q * P])
        aggT = sb("aggT", [D + 1, Q * P])
        rz = sb("rz", [P, G, 2 * D])
        pre = sb("pre", [P, G, D])
        cn = sb("cn", [P, G, D])
        blend = sb("blend", [P, G, D])
        hnew = sb("hnew", [P, G, D])
        x1b = sb("x1b", [P, G, D])
        fin = sb("fin", [P, G, D])
        ln_c = nring2[:, 0:2 * G * D].rearrange("p (u a b) -> p u a b", u=2, b=D)
        ln_q = nring2[:, 2 * G * D:4 * G * D].rearrange("p (u a b) -> p u a b", u=2, b=D)
        ln_s = sb("ln_s", [P, 2, 5, G])
        rdeg = sb("rdeg", [P, 2, Q])
        ps = ctx.enter_context(nc.psum_tensor("ps", [P, 8, 512], F32))
        psf = ps[:, :, :].rearrange("p a b -> p (a b)")

        s_const = sem("s_const")
        s_setup = sem("s_setup")
        s_prep = sem("s_prep")
        s_tail = sem("s_tail")
        s_tailc = sem("s_tailc")
        s_minit = sem("s_minit")
        s_mset = sem("s_mset")
        s_mget = sem("s_mget")
        s_pool = sem("s_pool")
        s_tailnow = sem("s_tailnow")
        s_drow = sem("s_drow")
        s_same = sem("s_same")
        b0_ld, b0_sth, b0_stx, b0_sts = sem("b0_ld"), sem("b0_sth"), sem("b0_stx"), sem("b0_sts")
        b0_v1, b0_v2 = Steps(sem("b0_v1"), 7), Steps(sem("b0_v2"), 8)
        b0_a1, b0_a2 = Steps(sem("b0_a1"), 1), Steps(sem("b0_a2"), 3)
        b0_p = Steps(sem("b0_p"), 2)
        a0_ea, a0_stx, a0_sts = sem("a0_ea"), sem("a0_stx"), sem("a0_sts")
        a0_g = [sem(f"a0_g{q}") for q in range(R)]
        a0_quad = sem("a0_quad")
        a0_a0, a0_a1, a0_a2, a0_a3 = Steps(sem("a0_a0"), 3), Steps(sem("a0_a1"), 3), Steps(sem("a0_a2"), 1), Steps(sem("a0_a3"), 1)
        a0_v1, a0_v2, a0_v3 = Steps(sem("a0_v1"), 10), Steps(sem("a0_v2"), Q), Steps(sem("a0_v3"), 12)
        a0_p0, a0_p1, a0_p2, a0_p3 = (Steps(sem(f"a0_p{j}"), n) for j, n in enumerate((1, 1, 2, 1)))
        b_ld, b_ld1, b_st = sem("b_ld"), sem("b_ld1"), sem("b_st")
        b_a0, b_a1, b_a2 = Steps(sem("b_a0"), 1), Steps(sem("b_a1"), 2), Steps(sem("b_a2"), 2)
        b_v = Steps(sem("b_v"), 5)
        b_p0, b_p1 = Steps(sem("b_p0"), 1), Steps(sem("b_p1"), 1)
        b_fin = sem("b_fin")
        a_g = [sem(f"a_g{q}") for q in range(R)]
        a_quad, a_st = sem("a_quad"), sem("a_st")
        a_a0, a_a1, a_a2s, a_a2, a_a3 = (Steps(sem(f"a_a{j}"), n) for j, n in enumerate((2, 1, 3, 1, 2)))
        a_v1, a_v2, a_v2s, a_v3t, a_v3 = (Steps(sem(f"a_v{j}"), n) for j, n in enumerate((4, 2, Q, 2, 3)))
        a_p0, a_p1, a_p2, a_p3 = (Steps(sem(f"a_p{j}"), n) for j, n in enumerate((1, 1, 2, 1)))
        f_ld = sem("f_ld")
        f_v = sem("f_v")
        f_sc = [sem(f"f_sc{q}") for q in range(R)]

        s_held = sem("s_held")

        def hold(eng):
            eng.sem_inc(s_held, 1)

        block = ctx.enter_context(nc.Block())
        consts = []

        @block.sync
        def _(sp):
            def load(dst, src):
                consts.append(1)
                sp.dma_start(dst, src).then_inc(s_const, 16)

            load(wm[:, :], wm_t)
            load(bm_all[:, :], bm.rearrange("(a d) -> a d", a=1).to_broadcast([P, D]))
            load(wa1[0:D, :], wa_t[0:D, :])
            load(wa1[D:D + 1, :], ba.rearrange("(a d) -> a d", a=1))
            load(wl[0:D, :], wl_t)
            load(wl[D:D + 1, :], bl.rearrange("(a t) d -> a (t d)", a=1))
            load(dst_i[:, :], dst_col)
            load(dstn_i[:, :], dst_next)
            load(src_i[:, :], src_col)
            load(slot_i[:, :], slot_node)
            load(type_i[:, :], type_col)
            load(prev_i[:, :], prev_last.to_broadcast([D + 1, ET]))
            sp.wait_ge(s_setup, 12)
            load(wa2[0:D, 0:D], wa_t[D:2 * D, :])
            load(wg[0:D, 0:2 * D], wih_t[:, 0:2 * D])
            load(wg[0:D, 3 * D:4 * D], wih_t[:, 2 * D:3 * D])
            load(wg[D:2 * D, 0:3 * D], whh_t)
            load(wh[0:D, 0:3 * D], whh_t)
            row = lambda v: v.rearrange("(a d) -> a d", a=1)
            load(brow_i[D:D + 1, 0:2 * D], row(bih[0:2 * D]))
            load(brow_i[D:D + 1, 3 * D:4 * D], row(bih[2 * D:3 * D]))
            load(brow_h[D:D + 1, 0:3 * D], row(bhh))
            load(b3f[:, 0, 0:2 * D], row(bih[0:2 * D]).to_broadcast([3, 2 * D]))
            load(b3f[:, 0, 3 * D:4 * D], row(bih[2 * D:3 * D]).to_broadcast([3, D]))
            load(b3f[:, 1, 0:3 * D], row(bhh).to_broadcast([3, 3 * D]))

            sp.wait_ge(s_setup, 15)
            sp.dma_start(node_row[0:NB, :].rearrange("(p t) a -> p (t a)", t=BT), node_ids[:, :]).then_inc(s_minit, 16)
            sp.dma_start(node_row[NB:N, :], tail_rows[:, :]).then_inc(s_minit, 16)
            sp.dma_start(x1b[0:TAIL, 0, :], x[NB:N, :]).then_inc(s_tail, 16)
            sp.wait_ge(s_prep, 7)
            sp.dma_start(h0_tab[NB:N, :], hnew[0:TAIL, 0, :]).then_inc(s_tail, 16)
            sp.wait_ge(s_tail, 32)

            W = G * D
            x_v, h0_v = node_part(x), node_part(h0_tab)

            def b0_load(i):
                b0_v2.wait(sp, i - 4)
                sp.dma_start(nring[:, bass.ds((i % 4) * W, W)], x_v[:, bass.ds(i * W, W)]).then_inc(b0_ld, 16)
                sp.wait_ge(b0_ld, 16 * (i + 1))
                hold(sp)

            def b0_store(i):
                b0_v1.wait(sp, i)
                sp.dma_start(h0_v[:, bass.ds(i * W, W)], flat(stage[:, :, :])).then_inc(b0_sth, 16)
                b0_v2.wait(sp, i)
                sp.dma_start(node_part(x1_tab)[:, bass.ds(i * W, W)], flat(x1b[:, :, :])).then_inc(b0_stx, 16)
                sp.dma_start(node_part(state[0])[:, bass.ds(i * W, W)], flat(hnew[:, :, :])).then_inc(b0_sts, 16)
                sp.wait_ge(b0_sts, 16 * (i + 1))
                hold(sp)

            pipeline(sp, NG, [(0, b0_load), (2, b0_store)], back=5)

            C = R * Q * P

            def rows_in(r):
                if not isinstance(r, int) or r > 0:
                    sp.wait_ge(s_same, 2 * R * Q * r)
                sp.dma_start(drow[:, :], dst_row[:, bass.ds(r * C, C)].to_broadcast([P, C])).then_inc(s_drow, 16)

            rows_in(0)
            with sp.Fori(1, NR) as r:
                rows_in(r)

            V = Q * D

            def a0_load(i):
                a0_a0.wait(sp, i - 4)
                sp.dma_start(nring[:, bass.ds((i % 4) * V, V)], edge_attr[:, bass.ds(i * V, V)]).then_inc(a0_ea, 16)
                sp.wait_ge(a0_ea, 16 * (i + 1))
                hold(sp)

            def a0_store(i):
                a0_v3.wait(sp, i)
                sp.dma_start(slot_part(x1_tab)[:, bass.ds(i * V, V)], flat(x1b[:, 0:Q, :])).then_inc(a0_stx, 16)
                sp.dma_start(slot_part(state[0])[:, bass.ds(i * V, V)], h_slot[:, bass.ds(i * V, V)]).then_inc(a0_sts, 16)
                sp.wait_ge(a0_sts, 16 * (i + 1))
                sp.wait_ge(a0_stx, 16 * (i + 1))
                hold(sp)

            sp.wait_ge(b0_sth, 16 * NG)
            pipeline(sp, NQ, [(0, a0_load), (4, a0_store)], back=5)

            for k in range(STEPS):
                last = k == STEPS - 1
                src_t = node_part(state[k])
                dst_t = node_part(out if last else state[k + 1])

                def b_load(i):
                    it = i + k * NG
                    b_v.wait(sp, it - 4)
                    if last:
                        hold(sp)
                        sp.wait_ge(b_fin, max(i - 3, 0) if isinstance(i, int) else i - 3)
                    sp.dma_start(nring[:, bass.ds((i % 4) * W, W)], src_t[:, bass.ds(i * W, W)]).then_inc(b_ld, 16)
                    if last:
                        sp.dma_start(nring2[:, bass.ds((i % 4) * W, W)],
                                     node_part(x1_tab)[:, bass.ds(i * W, W)]).then_inc(b_ld1, 16)
                        sp.wait_ge(b_ld1, 16 * (i + 1))
                    sp.wait_ge(b_ld, 16 * (it + 1))
                    hold(sp)

                def b_store(i):
                    it = i + k * NG
                    if last:
                        sp.wait_ge(b_fin, i + 1)
                    else:
                        b_v.wait(sp, it)
                    sp.dma_start(dst_t[:, bass.ds(i * W, W)], flat((fin if last else hnew)[:, :, :])).then_inc(b_st, 16)
                    sp.wait_ge(b_st, 16 * (it + 1))
                    hold(sp)

                pipeline(sp, NG, [(0, b_load), (3, b_store)], back=5)
                if not last:
                    def a_store(i):
                        it = i + k * NQ
                        a_v3.wait(sp, it)
                        sp.dma_start(slot_part(state[k + 1])[:, bass.ds(i * V, V)],
                                     h_slot[:, bass.ds(i * V, V)]).then_inc(a_st, 16)
                        sp.wait_ge(a_st, 16 * (it + 1))
                        hold(sp)

                    pipeline(sp, NQ, [(0, a_store)])

            def f_load(i):
                if not isinstance(i, int):
                    sp.wait_ge(f_v, i - 3)
                sp.dma_start(nring2[:, bass.ds((i % 4) * V, V)], slot_part(x1_tab)[:, bass.ds(i * V, V)]).then_inc(f_ld, 16)
                sp.wait_ge(f_ld, 16 * (i + 1))
                hold(sp)

            for i in range(4):
                f_load(i)
            with sp.Fori(4, NQ) as i:
                f_load(i)
            for q in range(R):
                sp.wait_ge(f_sc[q], 16 * Q * NR)

        @block.gpsimd
        def _(pool):
            setup = [0]

            def mark(ins):
                setup[0] += 1
                ins.then_inc(s_setup, 1)
                pool.wait_ge(s_setup, setup[0])

            mark(pool.memset(ident[:, :], 0.0))
            mark(pool.memset(eps[:, :], EPS))
            mark(pool.memset(wa2[:, :], 0.0))
            mark(pool.memset(wg[:, :], 0.0))
            mark(pool.memset(wh[:, :], 0.0))
            mark(pool.memset(brow_i[:, :], 0.0))
            mark(pool.memset(brow_h[:, :], 0.0))
            mark(pool.memset(b3f[:, :, :], 0.0))
            mark(pool.memset(ones3[:, :], 1.0))
            mark(pool.memset(hT[D:D + 1, :], 1.0))
            mark(pool.memset(parts[:, :, :, :], 0.0))
            mark(pool.memset(tail_now[:, :], 0))
            mark(pool.iota(slot_row[:, :], pattern=[[1, ET]], base=NB, channel_multiplier=ET))
            mark(pool.iota(node_ids[:, :], pattern=[[1, BT]], base=0, channel_multiplier=BT))
            mark(pool.iota(tail_rows[:, :], pattern=[[0, 1]], base=NB + TAIL_P * ET + ET - 1, channel_multiplier=ET))
            mark(pool.iota(cand[:, :], pattern=[[0, 1]], base=NB - TAIL_P, channel_multiplier=1))
            mark(pool.affine_select(out=ident[:, :], in_=ident[:, :], compare_op=ALU.not_equal, fill=1.0,
                                    base=0, pattern=[[-1, P]], channel_multiplier=1))
            mark(pool.memset(wa2[D:D + 1, D:D + 1], 1.0))
            mark(pool.memset(parts[:, 0, :, D:D + 1], 1.0))

            T = R * Q
            pool.wait_ge(s_prep, 9)
            pool.wait_ge(s_minit, 32)

            def step(ins):
                ins.then_inc(s_pool, 1)

            with pool.Fori(0, NR) as r:
                step(pool.tensor_copy(idx_st[:, 0, :], own_idx[:, bass.ds(r * T, T)]))
                step(pool.tensor_copy(val_st[:, :], slot_row[:, bass.ds(r * T, T)]))
                pool.wait_ge(s_pool, 2 * r + 2)
                hold(pool)
                for t in range(T):
                    pool.indirect_dma_start(out=node_row[:, :],
                                            out_offset=bass.IndirectOffsetOnAxis(ap=idx_st[:, 0, t:t + 1], axis=0),
                                            in_=val_st[:, t:t + 1], in_offset=None,
                                            bounds_check=N - 1, oob_is_err=False).then_inc(s_mset, 16)
                pool.wait_ge(s_mset, 16 * T * (r + 1))
                hold(pool)
            with pool.Fori(0, NR) as r:
                step(pool.tensor_copy(idx_st[:, 0, :], src_i[:, bass.ds(r * T, T)]))
                pool.wait_ge(s_pool, 2 * NR + 2 * r + 1)
                hold(pool)
                for t in range(T):
                    pool.indirect_dma_start(out=val_st[:, t:t + 1], out_offset=None, in_=node_row[:, :],
                                            in_offset=bass.IndirectOffsetOnAxis(ap=idx_st[:, 0, t:t + 1], axis=0)
                                            ).then_inc(s_mget, 16)
                pool.wait_ge(s_mget, 16 * T * (r + 1))
                step(pool.tensor_copy(src_row[:, bass.ds(r * T, T)], val_st[:, :]))
                pool.wait_ge(s_pool, 2 * NR + 2 * r + 2)
                hold(pool)
            pool.dma_start(tail_now[TAIL_P:TAIL_P + TAIL, :], node_row[NB:N, :]).then_inc(s_tailnow, 16)

            pool.wait_ge(b0_sth, 16 * NG)
            pool.wait_ge(s_tail, 32)
            pool.wait_ge(s_same, 2 * ET)
            done = 4 * NR

            def a0_quad_in(r, q):
                i = r * R + q
                for j in range(Q):
                    t = q * Q + j
                    pool.indirect_dma_start(out=xring[:, t * D:(t + 1) * D], out_offset=None, in_=x[:, :],
                                            in_offset=bass.IndirectOffsetOnAxis(ap=idx_st[:, 0, t:t + 1], axis=0)
                                            ).then_inc(a0_g[q], 16)
                    pool.indirect_dma_start(out=ring[:, t * D:(t + 1) * D], out_offset=None, in_=h0_tab[:, :],
                                            in_offset=bass.IndirectOffsetOnAxis(ap=idx_st[:, 1, t:t + 1], axis=0)
                                            ).then_inc(a0_g[q], 16)

            def forward(sems, q, r, per, quad_sem):
                pool.wait_ge(sems[q], per * (r + 1))
                pool.sem_inc(quad_sem, 1)

            def a0_round(r):
                step(pool.tensor_copy(idx_st[:, 0, :], slot_i[:, bass.ds(r * T, T)]))
                step(pool.tensor_copy(idx_st[:, 1, :], src_i[:, bass.ds(r * T, T)]))
                pool.wait_ge(s_pool, done + 2 * r + 2)
                hold(pool)
                for q in range(R):
                    if not isinstance(r, int):
                        a0_v3.wait(pool, (r - 1) * R + q)
                        hold(pool)
                    a0_quad_in(r, q)
                    if q:
                        forward(a0_g, q - 1, r, 32 * Q, a0_quad)
                forward(a0_g, R - 1, r, 32 * Q, a0_quad)

            a0_round(0)
            with pool.Fori(1, NR) as r:
                a0_round(r)
            done += 2 * NR

            pool.wait_ge(b0_sts, 16 * NG)
            for k in range(STEPS):
                if k == 0:
                    pool.wait_ge(a0_sts, 16 * NQ)
                else:
                    pool.wait_ge(a_st, 16 * NQ * k)
                    pool.wait_ge(b_st, 16 * NG * k)

                def a_round(r):
                    step(pool.tensor_copy(idx_st[:, 0, :], src_row[:, bass.ds(r * T, T)]))
                    pool.wait_ge(s_pool, done + r + 1)
                    for q in range(R):
                        it = r * R + q + k * NQ
                        a_a0.wait(pool, it - R, 1)
                        hold(pool)
                        for j in range(Q):
                            t = q * Q + j
                            pool.indirect_dma_start(out=ring[:, t * D:(t + 1) * D], out_offset=None, in_=state[k][:, :],
                                                    in_offset=bass.IndirectOffsetOnAxis(ap=idx_st[:, 0, t:t + 1], axis=0)
                                                    ).then_inc(a_g[q], 16)
                        if q:
                            forward(a_g, q - 1, r + k * NR, 16 * Q, a_quad)
                    forward(a_g, R - 1, r + k * NR, 16 * Q, a_quad)

                a_round(0)
                with pool.Fori(1, NR) as r:
                    a_round(r)
                done += NR

            pool.wait_ge(b_st, 16 * NG * STEPS)

            def f_round(r):
                step(pool.tensor_copy(idx_st[:, 0, :], own_idx[:, bass.ds(r * T, T)]))
                pool.wait_ge(s_pool, done + r + 1)
                for q in range(R):
                    pool.wait_ge(f_v, r * R + q + 1)
                    hold(pool)
                    for j in range(Q):
                        t = q * Q + j
                        pool.indirect_dma_start(out=out[:, :],
                                                out_offset=bass.IndirectOffsetOnAxis(ap=idx_st[:, 0, t:t + 1], axis=0),
                                                in_=ring[:, t * D:(t + 1) * D], in_offset=None,
                                                bounds_check=N - 1, oob_is_err=False).then_inc(f_sc[q], 16)

            f_round(0)
            with pool.Fori(1, NR) as r:
                for q in range(R):
                    pool.wait_ge(f_sc[q], 16 * Q * r)
                f_round(r)
            for q in range(R):
                pool.wait_ge(f_sc[q], 16 * Q * NR)

        @block.scalar
        def _(act):
            def copy(out_, in_):
                return nc.scalar.activation(out_, in_, ACT.Copy)

            def root(u, n, p=P):
                return nc.scalar.activation(ln_s[0:p, u, 3, 0:n], ln_s[0:p, u, 2, 0:n], ACT.Sqrt,
                                            bias=eps[0:p, :], scale=1.0 / D)

            act.wait_ge(s_setup, 19)
            act.wait_ge(s_prep, 5)
            root(0, 1, TAIL).then_inc(s_tailc, 1)

            def b0_root1(i):
                b0_a1.begin(act, i)
                b0_v1.wait(act, i, 5)
                b0_a1.mark(root(0, G))
                b0_a1.end()

            def b0_rest(i):
                b0_a2.begin(act, i)
                b0_p.wait(act, i, 1)
                b0_p.wait(act, i - 1)
                b0_a2.mark(copy(hT[0:D, 0:3 * P], ps[0:D, 0, 0:3 * P]))
                b0_a2.mark(copy(hT[0:D, 3 * P:6 * P], ps[0:D, 1, 0:3 * P]))
                b0_v2.wait(act, i, 6)
                b0_a2.mark(root(1, G))
                b0_a2.end()

            pipeline(act, NG, [(1, b0_rest), (0, b0_root1)])

            b0_v2.wait(act, NG - 1)
            def a0_0(i):
                a0_a0.begin(act, i)
                act.wait_ge(a0_quad, i + 1)
                a0_p0.wait(act, i - 1)
                a0_a0.mark(copy(he[:, :, 0:D], ring[:, bass.ds((i % R) * Q * D, Q * D)].rearrange("p (a b) -> p a b", b=D)))
                act.wait_ge(a0_ea, 16 * (i + 1))
                a0_a0.mark(copy(he[:, :, D:2 * D], nring[:, bass.ds((i % 4) * Q * D, Q * D)].rearrange("p (a b) -> p a b", b=D)))
                a0_p0.wait(act, i)
                a0_p1.wait(act, i - 1)
                a0_a0.mark(copy(heT[:, :], ps[:, 0, :]))
                a0_a0.end()

            def a0_1(i):
                a0_a1.begin(act, i)
                a0_v1.wait(act, i, 1)
                a0_p2.wait(act, i - 1)
                a0_a1.mark(copy(parts[:, 0, :, 0:D], m[:, :, :]))
                a0_v1.wait(act, i, 2)
                a0_a1.mark(copy(parts[:, 1, :, 0:D], mres[:, :, :]))
                a0_v1.wait(act, i, 8)
                a0_a1.mark(root(0, Q))
                a0_a1.end()

            def a0_2(i):
                a0_a2.begin(act, i)
                a0_p2.wait(act, i)
                a0_p3.wait(act, i - 1)
                a0_a2.mark(copy(hT[0:D, 0:Q * P], ps[0:D, 1, :]))
                a0_a2.end()

            def a0_3(i):
                a0_a3.begin(act, i)
                a0_v3.wait(act, i, 10)
                a0_a3.mark(root(1, Q))
                a0_a3.end()

            pipeline(act, NQ, [(3, a0_3), (2, a0_2), (1, a0_1), (0, a0_0)])

            for k in range(STEPS):
                if k == 0:
                    a0_v3.wait(act, NQ - 1)
                else:
                    a_v3.wait(act, NQ * k - 1)

                def b_0(i):
                    it = i + k * NG
                    b_a0.begin(act, it)
                    act.wait_ge(b_ld, 16 * (it + 1))
                    b_p0.wait(act, it - 1)
                    b_a0.mark(copy(flat(stage[:, :, :]), nring[:, bass.ds((i % 4) * G * D, G * D)]))
                    b_a0.end()

                def b_1(i):
                    it = i + k * NG
                    b_a1.begin(act, it)
                    b_p0.wait(act, it)
                    b_p1.wait(act, it - 1)
                    b_a1.mark(copy(hT[0:D, 0:3 * P], ps[0:D, 0, 0:3 * P]))
                    b_a1.mark(copy(hT[0:D, 3 * P:6 * P], ps[0:D, 1, 0:3 * P]))
                    b_a1.end()

                def gates(i):
                    return psf[:, bass.ds(1024 + (i % 2) * 1536, 1536)].rearrange("p (t c) -> p t c", c=4 * D)

                def b_2(i):
                    it = i + k * NG
                    b_a2.begin(act, it)
                    b_p1.wait(act, it)
                    b_v.wait(act, it - 1)
                    b_a2.mark(nc.scalar.activation(rz[:, :, :], gates(i)[:, :, 0:2 * D], ACT.Sigmoid))
                    b_v.wait(act, it, 2)
                    b_a2.mark(nc.scalar.activation(flat(cn[:, :, :]), flat(pre[:, :, :]), ACT.Tanh))
                    b_a2.end()

                pipeline(act, NG, [(0, b_0), (2, b_2), (0, b_1)])

                b_v.wait(act, NG * (k + 1) - 1)

                def a_0(i):
                    it = i + k * NQ
                    a_a0.begin(act, it)
                    act.wait_ge(a_quad, it + 1)
                    a_p0.wait(act, it - 1)
                    a_a0.mark(copy(flat(stage[:, 0:Q, :]), ring[:, bass.ds((i % R) * Q * D, Q * D)]))

                def a_0b(i):
                    it = i + k * NQ
                    a_p0.wait(act, it)
                    a_p1.wait(act, it - 1)
                    a_a0.mark(copy(hT[0:D, 0:Q * P], ps[0:D, 0, :]))
                    a_a0.end()

                def a_1(i):
                    it = i + k * NQ
                    a_a1.begin(act, it)
                    a_p1.wait(act, it)
                    a_v2.wait(act, it - 1)
                    a_a1.mark(copy(m[:, :, :], psf[:, 1024:2048].rearrange("p (a t d) -> p a t d", t=NT, d=D)[:, :, 0, :]))
                    a_a1.end()

                def a_2s(i):
                    it = i + k * NQ
                    a_a2s.begin(act, it)
                    a_p2.wait(act, it - 1, 2)
                    a_a2s.mark(copy(flat(stage2[:, :, :]), h_slot[:, bass.ds(i * Q * D, Q * D)]))
                    a_v1.wait(act, it)
                    a_a2s.mark(copy(parts[:, 0, :, 0:D], m[:, :, :]))
                    a_v2.wait(act, it, 1)
                    a_a2s.mark(copy(parts[:, 1, :, 0:D], mres[:, :, :]))
                    a_a2s.end()

                def a_2(i):
                    it = i + k * NQ
                    a_a2.begin(act, it)
                    a_p2.wait(act, it)
                    a_p3.wait(act, it - 1)
                    a_a2.mark(copy(stack[D:2 * D, :], ps[0:D, 1, :]))
                    a_a2.end()

                sg = ps[:, 5:7, :].rearrange("p a (t c) -> p (a t) c", c=4 * D)

                def a_3(i):
                    it = i + k * NQ
                    a_a3.begin(act, it)
                    a_p3.wait(act, it)
                    a_v3.wait(act, it - 1)
                    a_a3.mark(nc.scalar.activation(rz[:, 0:Q, :], sg[:, :, 0:2 * D], ACT.Sigmoid))

                def a_3b(i):
                    it = i + k * NQ
                    a_v3t.wait(act, it)
                    a_a3.mark(nc.scalar.activation(flat(cn[:, 0:Q, :]), flat(pre[:, 0:Q, :]), ACT.Tanh))
                    a_a3.end()

                pipeline(act, NQ, [(0, a_0), (2, a_2s), (3, a_3), (2, a_2), (3, a_3b), (1, a_1), (0, a_0b)])

        @block.vector
        def _(dve):
            count = [0]

            def link(ins):
                count[0] += 1
                ins.then_inc(s_prep, 1)
                dve.wait_ge(s_prep, count[0])

            def ln_head(st, u, src, n, p=P):
                wide = lambda a: a.rearrange("p (n o) -> p n o", o=1).to_broadcast([p, n, D])
                st(nc.vector.tensor_reduce(ln_s[0:p, u, 0, 0:n], src, axis=AX.X, op=ALU.add))
                st(nc.vector.tensor_scalar(ln_s[0:p, u, 1, 0:n], ln_s[0:p, u, 0, 0:n], -1.0 / D, None, ALU.mult))
                st(nc.vector.tensor_tensor(ln_c[0:p, u, 0:n, :], src, wide(ln_s[0:p, u, 1, 0:n]), ALU.add))
                st(nc.vector.tensor_tensor(ln_q[0:p, u, 0:n, :], ln_c[0:p, u, 0:n, :], ln_c[0:p, u, 0:n, :], ALU.mult))

            def ln_sum(u, n, p=P):
                return nc.vector.tensor_reduce(ln_s[0:p, u, 2, 0:n], ln_q[0:p, u, 0:n, :], axis=AX.X, op=ALU.add)

            def ln_inv(u, n, p=P):
                return nc.vector.reciprocal(ln_s[0:p, u, 4, 0:n], ln_s[0:p, u, 3, 0:n])

            def ln_out(u, dst, n, p=P):
                wide = ln_s[0:p, u, 4, 0:n].rearrange("p (n o) -> p n o", o=1).to_broadcast([p, n, D])
                return nc.vector.scalar_tensor_tensor(dst, ln_c[0:p, u, 0:n, :], 0.0, wide, ALU.max, ALU.mult)

            dve.wait_ge(s_tail, 16)
            ln_head(link, 0, x1b[0:TAIL, 0:1, :], 1, TAIL)
            link(ln_sum(0, 1, TAIL))
            dve.wait_ge(s_tailc, 1)
            link(ln_inv(0, 1, TAIL))
            link(ln_out(0, hnew[0:TAIL, 0:1, :], 1, TAIL))
            dve.wait_ge(s_const, 16 * len(consts))
            link(nc.vector.tensor_tensor(last_f[:, :], dst_i[:, :], dstn_i[:, :], ALU.is_equal))
            link(nc.vector.scalar_tensor_tensor(own_idx[:, :], last_f[:, :], float(SKIP), dst_i[:, :], ALU.mult, ALU.add))
            link(nc.vector.tensor_copy(dst_f[:, :], dst_i[:, :]))
            link(nc.vector.tensor_copy(prev_f[:, :], prev_i[:, :]))
            for t in range(3):
                link(nc.vector.tensor_scalar(tmask[:, t, :], type_i[:, :], float(t + 1), None, ALU.is_equal))
            dve.wait_ge(s_setup, 19)
            link(nc.vector.tensor_tensor(wh[D:D + 1, :], brow_i[D:D + 1, :], brow_h[D:D + 1, :], ALU.add))
            link(nc.vector.tensor_tensor(b3acc[:, 0, :], b3f[:, 0, :], b3f[:, 1, :], ALU.add))
            link(nc.vector.tensor_copy(b3part[:, 0, :], b3acc[:, 0, :]))
            link(nc.vector.tensor_tensor(b3acc[:, 1, :], b3acc[:, 0, :], b3part[:, 0, :], ALU.subtract))
            link(nc.vector.tensor_copy(b3part[:, 1, :], b3acc[:, 1, :]))
            link(nc.vector.tensor_tensor(b3acc[:, 0, :], b3acc[:, 1, :], b3part[:, 1, :], ALU.subtract))
            link(nc.vector.tensor_scalar(b3acc[:, 1, :], b3part[:, 0, :], ident[0:3, 0:1], None, ALU.mult))
            link(nc.vector.scalar_tensor_tensor(b3acc[:, 1, :], b3part[:, 1, :], ident[0:3, 1:2], b3acc[:, 1, :], ALU.mult, ALU.add))
            link(nc.vector.scalar_tensor_tensor(bias3[:, :], b3acc[:, 0, :], ident[0:3, 2:3], b3acc[:, 1, :], ALU.mult, ALU.add))
            dve.wait_ge(s_tail, 32)

            W = G * D

            def xs(i):
                return nring[:, bass.ds((i % 4) * W, W)].rearrange("p (a b) -> p a b", b=D)

            def b0_1(i):
                b0_v1.begin(dve, i)
                dve.wait_ge(b0_ld, 16 * (i + 1))
                ln_head(b0_v1.link, 0, xs(i), G)
                b0_v1.mark(ln_sum(0, G))
                b0_a1.wait(dve, i)
                b0_v1.link(ln_inv(0, G))
                b0_p.wait(dve, i - 1, 1)
                if not isinstance(i, int) or i > 0:
                    dve.wait_ge(b0_sth, 16 * i)
                b0_v1.mark(ln_out(0, stage[:, :, :], G))
                b0_v1.end()

            def b0_2(i):
                b0_v2.begin(dve, i)
                b0_p.wait(dve, i)
                if not isinstance(i, int) or i > 0:
                    dve.wait_ge(b0_stx, 16 * i)
                b0_v2.link(nc.vector.scalar_tensor_tensor(
                    x1b[:, :, :], ps[:, 2, 0:W].rearrange("p (a b) -> p a b", b=D), 0.0, xs(i), ALU.max, ALU.add))
                ln_head(b0_v2.link, 1, x1b[:, :, :], G)
                b0_v2.mark(ln_sum(1, G))
                b0_a2.wait(dve, i)
                b0_v2.link(ln_inv(1, G))
                if not isinstance(i, int) or i > 0:
                    dve.wait_ge(b0_sts, 16 * i)
                b0_v2.mark(ln_out(1, hnew[:, :, :], G))
                b0_v2.end()

            pipeline(dve, NG, [(1, b0_2), (0, b0_1)])

            T = R * Q
            with dve.Fori(0, NR) as r:
                dve.wait_ge(s_drow, 16 * (r + 1))
                hold(dve)
                with dve.Fori(0, T) as t:
                    g = r * T + t
                    nc.vector.tensor_scalar(same[:, bass.ds(g * P, P)], drow[:, bass.ds(t * P, P)],
                                            dst_f[:, bass.ds(g, 1)], None, ALU.is_equal).then_inc(s_same, 1)
                    nc.vector.tensor_scalar(cont[:, bass.ds(g * P, P)], drow[0:D + 1, bass.ds(t * P, P)],
                                            prev_f[:, bass.ds(g, 1)], None, ALU.is_equal).then_inc(s_same, 1)
            dve.wait_ge(s_same, 2 * ET)

            def a0_1(i):
                a0_v1.begin(dve, i)
                a0_p1.wait(dve, i)
                a0_a1.wait(dve, i - 1, 1)
                bias = bm_all[:, :].rearrange("p (o d) -> p o d", o=1).to_broadcast([P, Q, D])
                a0_v1.link(nc.vector.tensor_tensor(m[:, :, :], ps[:, 2, 0:Q * D].rearrange("p (a b) -> p a b", b=D), bias, ALU.add))
                a0_a1.wait(dve, i, 1)
                a0_v1.link(nc.vector.tensor_tensor(mres[:, :, :], m[:, :, :], parts[:, 0, :, 0:D], ALU.subtract))
                a0_a1.wait(dve, i, 2)
                a0_v1.mark(nc.vector.tensor_tensor(parts[:, 2, :, 0:D], mres[:, :, :], parts[:, 1, :, 0:D], ALU.subtract))
                xq = xring[:, bass.ds((i % R) * Q * D, Q * D)].rearrange("p (a b) -> p a b", b=D)
                ln_head(a0_v1.link, 0, xq, Q)
                a0_v1.mark(ln_sum(0, Q))
                a0_a1.wait(dve, i, 3)
                a0_v1.link(ln_inv(0, Q))
                a0_p2.wait(dve, i - 1)
                a0_v1.mark(ln_out(0, stage[:, 0:Q, :], Q))
                a0_v1.end()

            def a0_2(i):
                a0_v2.begin(dve, i)
                a0_p2.wait(dve, i, 1)
                a0_p3.wait(dve, i - 1)
                for j in range(Q):
                    before = (j + Q - 1) % Q * P + P - 1
                    c = slice(j * P, (j + 1) * P)
                    a0_v2.link(nc.vector.scalar_tensor_tensor(
                        aggT[:, c], cont[:, bass.ds((i * Q + j) * P, P)], aggT[:, before:before + 1],
                        ps[0:D + 1, 4, c], ALU.mult, ALU.add))
                a0_v2.end()

            def a0_3(i):
                a0_v3.begin(dve, i)
                a0_p3.wait(dve, i)
                agg = ps[:, 5, 0:Q * (D + 1)].rearrange("p (a b) -> p a b", b=D + 1)
                a0_v3.link(nc.vector.tensor_scalar(rdeg[:, 0, :], agg[:, :, D], 1.0, None, ALU.max))
                a0_v3.link(nc.vector.reciprocal(rdeg[:, 1, :], rdeg[:, 0, :]))
                wide = rdeg[:, 1, :].rearrange("p (n o) -> p n o", o=1).to_broadcast([P, Q, D])
                a0_v3.link(nc.vector.tensor_tensor(fin[:, 0:Q, :], agg[:, :, 0:D], wide, ALU.mult))
                a0_v3.link(nc.vector.tensor_tensor(fin[:, 0:Q, :], ps[:, 6, 0:Q * D].rearrange("p (a b) -> p a b", b=D),
                                                   fin[:, 0:Q, :], ALU.add))
                if not isinstance(i, int) or i > 0:
                    dve.wait_ge(a0_stx, 16 * i)
                xq = xring[:, bass.ds((i % R) * Q * D, Q * D)].rearrange("p (a b) -> p a b", b=D)
                a0_v3.link(nc.vector.scalar_tensor_tensor(x1b[:, 0:Q, :], fin[:, 0:Q, :], 0.0, xq, ALU.max, ALU.add))
                ln_head(a0_v3.link, 1, x1b[:, 0:Q, :], Q)
                a0_v3.mark(ln_sum(1, Q))
                a0_a3.wait(dve, i)
                a0_v3.link(ln_inv(1, Q))
                a0_v3.mark(ln_out(1, h_slot[:, bass.ds(i * Q * D, Q * D)].rearrange("p (a b) -> p a b", b=D), Q))
                a0_v3.end()

            link(nc.vector.memset(aggT[:, :], 0.0))
            link(nc.vector.memset(stack[:, :], 0.0))
            pipeline(dve, NQ, [(3, a0_3), (2, a0_2), (1, a0_1)])

            dve.wait_ge(s_tailnow, 16)
            link(nc.vector.tensor_tensor(tail_f[:, 0:1], tail_now[:, :], slot_row[:, ET - 1:ET], ALU.is_equal))
            link(nc.vector.tensor_scalar(tail_f[:, 1:2], cand[:, :], -float(SKIP), None, ALU.add))
            link(nc.vector.tensor_tensor(tail_f[:, 2:3], tail_f[:, 0:1], tail_f[:, 1:2], ALU.mult))
            link(nc.vector.tensor_scalar(tail_f[:, 3:4], tail_f[:, 2:3], float(SKIP), None, ALU.add))
            link(nc.vector.tensor_tensor(own_idx[:, ET - 1:ET], own_idx[:, ET - 1:ET], tail_f[:, 3:4], ALU.min))

            for k in range(STEPS):
                last = k == STEPS - 1

                def b_2(i):
                    it = i + k * NG
                    b_v.begin(dve, it)
                    gates = psf[:, bass.ds(1024 + (i % 2) * 1536, 1536)].rearrange("p (t c) -> p t c", c=4 * D)
                    h = nring[:, bass.ds((i % 4) * W, W)].rearrange("p (a b) -> p a b", b=D)
                    b_a2.wait(dve, it, 1)
                    b_v.link(nc.vector.tensor_tensor(pre[:, :, :], gates[:, :, 2 * D:3 * D], rz[:, :, 0:D], ALU.mult))
                    b_v.mark(nc.vector.tensor_tensor(pre[:, :, :], gates[:, :, 3 * D:4 * D], pre[:, :, :], ALU.add))
                    b_a2.wait(dve, it)
                    b_v.link(nc.vector.tensor_tensor(blend[:, :, :], h, cn[:, :, :], ALU.subtract))
                    b_v.link(nc.vector.tensor_tensor(blend[:, :, :], blend[:, :, :], rz[:, :, D:2 * D], ALU.mult))
                    if not isinstance(it, int) or it > 0:
                        dve.wait_ge(b_st, 16 * it)
                    if last:
                        b_v.link(nc.vector.tensor_tensor(hnew[:, :, :], blend[:, :, :], cn[:, :, :], ALU.add))
                        dve.wait_ge(b_ld1, 16 * (i + 1))
                        x1 = nring2[:, bass.ds((i % 4) * W, W)].rearrange("p (a b) -> p a b", b=D)
                        nc.vector.tensor_tensor(fin[:, :, :], hnew[:, :, :], x1, ALU.add).then_inc(b_fin, 1)
                    else:
                        b_v.mark(nc.vector.tensor_tensor(hnew[:, :, :], blend[:, :, :], cn[:, :, :], ALU.add))
                    b_v.end()

                pipeline(dve, NG, [(2, b_2)] if False else [(0, b_2)])

                link(nc.vector.memset(stack[0:D, Q * P - 1:Q * P], 0.0))

                def a_1(i):
                    it = i + k * NQ
                    a_v1.begin(dve, it)
                    if not isinstance(it, int) or it > 0:
                        a_v1.mark(nc.vector.tensor_copy(tm_st[:, :, :], tmask[:, :, bass.ds(i * Q, Q)]))
                    else:
                        a_v1.mark(nc.vector.tensor_copy(tm_st[:, :, :], tmask[:, :, 0:Q]))
                    a_v1.eng.wait_ge(a_v1.sem, a_v1.per * it + 1)
                    a_a1.wait(dve, it)
                    all_t = psf[:, 1024:2048].rearrange("p (a t d) -> p a t d", t=NT, d=D)
                    for t in range(1, NT):
                        hold(dve)
                        mask = tm_st[:, t - 1, :].rearrange("p (n o) -> p n o", o=1).to_broadcast([P, Q, D])
                        a_v1.link(nc.vector.copy_predicated(m[:, :, :], mask, all_t[:, :, t, :]))
                    a_v1.end()

                def a_2s(i):
                    it = i + k * NQ
                    a_v2.begin(dve, it)
                    a_a2s.wait(dve, it, 2)
                    a_v2.link(nc.vector.tensor_tensor(mres[:, :, :], m[:, :, :], parts[:, 0, :, 0:D], ALU.subtract))
                    a_a2s.wait(dve, it, 3)
                    a_v2.mark(nc.vector.tensor_tensor(parts[:, 2, :, 0:D], mres[:, :, :], parts[:, 1, :, 0:D], ALU.subtract))
                    a_v2.end()

                def a_2(i):
                    it = i + k * NQ
                    a_v2s.begin(dve, it)
                    a_p2.wait(dve, it, 1)
                    a_p3.wait(dve, it - 1)
                    for j in range(Q):
                        before = (j + Q - 1) % Q * P + P - 1
                        c = slice(j * P, (j + 1) * P)
                        a_v2s.link(nc.vector.scalar_tensor_tensor(
                            stack[0:D, c], cont[0:D, bass.ds((i * Q + j) * P, P)], stack[0:D, before:before + 1],
                            ps[0:D, 4, c], ALU.mult, ALU.add))
                    a_v2s.end()

                sg = ps[:, 5:7, :].rearrange("p a (t c) -> p (a t) c", c=4 * D)

                def a_3t(i):
                    it = i + k * NQ
                    a_v3t.begin(dve, it)
                    a_a3.wait(dve, it, 1)
                    a_v3t.link(nc.vector.tensor_tensor(pre[:, 0:Q, :], sg[:, :, 2 * D:3 * D], rz[:, 0:Q, 0:D], ALU.mult))
                    a_v3t.mark(nc.vector.tensor_tensor(pre[:, 0:Q, :], sg[:, :, 3 * D:4 * D], pre[:, 0:Q, :], ALU.add))
                    a_v3t.end()

                def a_3(i):
                    it = i + k * NQ
                    a_v3.begin(dve, it)
                    h = h_slot[:, bass.ds(i * Q * D, Q * D)].rearrange("p (a b) -> p a b", b=D)
                    a_a3.wait(dve, it)
                    a_v3.link(nc.vector.tensor_tensor(blend[:, 0:Q, :], h, cn[:, 0:Q, :], ALU.subtract))
                    a_v3.link(nc.vector.tensor_tensor(blend[:, 0:Q, :], blend[:, 0:Q, :], rz[:, 0:Q, D:2 * D], ALU.mult))
                    a_v3.mark(nc.vector.tensor_tensor(h, blend[:, 0:Q, :], cn[:, 0:Q, :], ALU.add))
                    a_v3.end()

                pipeline(dve, NQ, [(2, a_2s), (3, a_3t), (2, a_2), (3, a_3), (1, a_1)])

            def f_add(i, ring_free):
                dve.wait_ge(f_ld, 16 * (i + 1))
                V = Q * D
                slot = (i % R) * V
                nc.vector.tensor_tensor(ring[:, bass.ds(slot, V)], h_slot[:, bass.ds(i * V, V)],
                                        nring2[:, bass.ds((i % 4) * V, V)], ALU.add).then_inc(f_v, 1)

            a_v3.wait(dve, NQ * STEPS - 1)
            for q in range(R):
                f_add(q, None)
            with dve.Fori(1, NR) as r:
                for q in range(R):
                    dve.wait_ge(f_sc[q], 16 * Q * r)
                    f_add(r * R + q, None)

        @block.tensor
        def _(pe):
            pe.wait_ge(s_setup, 19)
            pe.wait_ge(s_const, 16 * len(consts))
            pe.wait_ge(s_prep, 23)

            def transposes(src, n, bank):
                hold(pe)
                for j in range(n):
                    b, c = (bank + j // 3, j % 3) if n == G else (bank, j)
                    last = nc.tensor.transpose(ps[0:D, b, c * P:(c + 1) * P], src[:, j, :], ident[:, :])
                return last

            def b0(i):
                b0_p.begin(pe, i)
                b0_v1.wait(pe, i)
                b0_a2.wait(pe, i - 1, 2)
                b0_p.mark(transposes(stage, G, 0))
                b0_a2.wait(pe, i, 2)
                b0_v2.wait(pe, i - 1, 1)
                for j in range(G):
                    last = nc.tensor.matmul(ps[:, 2, j * D:(j + 1) * D], hT[:, j * P:(j + 1) * P], wa1[:, :], start=True, stop=True)
                b0_p.mark(last)
                b0_p.end()

            pipeline(pe, NG, [(0, b0)])

            def a0_0(i):
                a0_p0.begin(pe, i)
                a0_a0.wait(pe, i, 2)
                for j in range(Q):
                    last = nc.tensor.transpose(ps[:, 0, j * P:(j + 1) * P], he[:, j, :], ident[:, :])
                a0_p0.mark(last)

            def a0_1(i):
                a0_p1.begin(pe, i)
                a0_a0.wait(pe, i)
                a0_v1.wait(pe, i - 1, 1)
                for j in range(Q):
                    last = nc.tensor.matmul(ps[:, 2, j * D:(j + 1) * D], heT[:, j * P:(j + 1) * P], wm[:, :], start=True, stop=True)
                a0_p1.mark(last)

            def sums(i, wide):
                for j in range(Q):
                    for part in range(3):
                        last = nc.tensor.matmul(ps[0:wide, 4, j * P:(j + 1) * P], parts[:, part, j, 0:wide],
                                                same[:, bass.ds((i * Q + j) * P, P)], start=part == 0, stop=part == 2)
                return last

            def a0_2(i):
                a0_p2.begin(pe, i)
                a0_v1.wait(pe, i)
                a0_v2.wait(pe, i - 1)
                a0_p2.mark(sums(i, D + 1))
                a0_a2.wait(pe, i - 1)
                a0_p2.mark(transposes(stage, Q, 1))

            def a0_3(i):
                a0_p3.begin(pe, i)
                a0_v2.wait(pe, i)
                a0_a2.wait(pe, i)
                a0_v3.wait(pe, i - 1, 4)
                for j in range(Q):
                    nc.tensor.matmul(ps[:, 5, j * (D + 1):(j + 1) * (D + 1)], aggT[:, j * P:(j + 1) * P], wa2[:, :], start=True, stop=True)
                for j in range(Q):
                    last = nc.tensor.matmul(ps[:, 6, j * D:(j + 1) * D], hT[:, j * P:(j + 1) * P], wa1[:, :], start=True, stop=True)
                a0_p3.mark(last)

            pe.wait_ge(s_same, 2 * ET)
            pipeline(pe, NQ, [(3, a0_3), (2, a0_2), (1, a0_1), (0, a0_0)])

            for k in range(STEPS):
                if k == 0:
                    a0_v3.wait(pe, NQ - 1)
                else:
                    a_v3.wait(pe, NQ * k - 1)

                def b_0(i):
                    it = i + k * NG
                    b_p0.begin(pe, it)
                    b_a0.wait(pe, it)
                    b_a1.wait(pe, it - 1)
                    b_p0.mark(transposes(stage, G, 0))

                def b_1(i):
                    it = i + k * NG
                    b_p1.begin(pe, it)
                    b_a1.wait(pe, it)
                    b_v.wait(pe, it - 2, 2)
                    for j in range(G):
                        last = nc.tensor.matmul(psf[:, bass.ds(1024 + (i % 2) * 1536 + j * 4 * D, 4 * D)],
                                                hT[:, j * P:(j + 1) * P], wh[:, :], start=True, stop=True)
                    b_p1.mark(last)

                pipeline(pe, NG, [(1, b_1), (0, b_0)], back=3)
                b_v.wait(pe, NG * (k + 1) - 1)

                def a_0(i):
                    it = i + k * NQ
                    a_p0.begin(pe, it)
                    a_a0.wait(pe, it, 1)
                    a_p0.mark(transposes(stage, Q, 0))

                def a_1(i):
                    it = i + k * NQ
                    a_p1.begin(pe, it)
                    a_a0.wait(pe, it)
                    a_v1.wait(pe, it - 1)
                    for j in range(Q):
                        last = nc.tensor.matmul(psf[:, 1024 + j * 256:1280 + j * 256], hT[:, j * P:(j + 1) * P], wl[:, :],
                                                start=True, stop=True)
                    a_p1.mark(last)

                def a_2(i):
                    it = i + k * NQ
                    a_p2.begin(pe, it)
                    a_v2.wait(pe, it)
                    a_v2s.wait(pe, it - 1)
                    a_p2.mark(sums(i, D))
                    a_a2s.wait(pe, it, 1)
                    a_a2.wait(pe, it - 1)
                    a_p2.mark(transposes(stage2, Q, 1))

                def a_3(i):
                    it = i + k * NQ
                    a_p3.begin(pe, it)
                    a_v2s.wait(pe, it)
                    a_a2.wait(pe, it)
                    a_v3t.wait(pe, it - 1)
                    for j in range(Q):
                        o = ps[:, 5 + j // 2, (j % 2) * 256:(j % 2) * 256 + 256]
                        nc.tensor.matmul(o, stack[:, j * P:(j + 1) * P], wg[:, :], start=True, stop=False)
                        last = nc.tensor.matmul(o, ones3[:, :], bias3[:, :], start=False, stop=True)
                    a_p3.mark(last)

                pipeline(pe, NQ, [(3, a_3), (2, a_2), (1, a_1), (0, a_0)])


def kernel(x, src, dst, edge_attr_64, edge_type_4, L0_gnn_W_msg_w, L0_gnn_W_msg_b, L0_gnn_W_apply_w,
           L0_gnn_W_apply_b, L1_gnn_W, L1_gnn_b, L1_gnn_w_ih, L1_gnn_w_hh, L1_gnn_b_ih, L1_gnn_b_hh):
    import numpy as np
    import concourse.bacc as bacc
    from concourse.bass_utils import run_bass_kernel_spmd

    slots = P * ET
    pads = slots - E

    def columns(v, pad):
        v = np.concatenate([np.asarray(v), np.asarray(pad, np.int32)])
        return np.ascontiguousarray(v.reshape(ET, P).T)

    dst, src, kind = np.asarray(dst), np.asarray(src), np.asarray(edge_type_4)
    none = np.full(pads, -1, np.int32)
    tail = np.concatenate([np.arange(NB, N, dtype=np.int32), np.zeros(pads - TAIL, np.int32)])
    ea = np.concatenate([np.asarray(edge_attr_64), np.zeros((pads, D), np.float32)])
    arrays = {
        "x": np.asarray(x),
        "edge_attr": np.ascontiguousarray(ea.reshape(ET, P, D).transpose(1, 0, 2).reshape(P, ET * D)),
        "dst_col": columns(dst, none),
        "dst_next": columns(dst[1:], np.full(pads + 1, -1, np.int32)),
        "dst_row": np.concatenate([dst, np.full(pads, -2, np.int32)]).reshape(1, slots),
        "prev_last": np.concatenate([np.full(1, -3, np.int32), dst[P - 1::P][:ET - 1]]).reshape(1, ET),
        "src_col": columns(src, np.zeros(pads, np.int32)),
        "slot_node": columns(dst, tail),
        "type_col": columns(kind, np.zeros(pads, np.int32)),
        "wm_t": np.ascontiguousarray(np.asarray(L0_gnn_W_msg_w).T),
        "bm": np.asarray(L0_gnn_W_msg_b),
        "wa_t": np.ascontiguousarray(np.asarray(L0_gnn_W_apply_w).T),
        "ba": np.asarray(L0_gnn_W_apply_b),
        "wl_t": np.ascontiguousarray(np.asarray(L1_gnn_W).transpose(2, 0, 1).reshape(D, NT * D)),
        "bl": np.asarray(L1_gnn_b),
        "wih_t": np.ascontiguousarray(np.asarray(L1_gnn_w_ih).T),
        "whh_t": np.ascontiguousarray(np.asarray(L1_gnn_w_hh).T),
        "bih": np.asarray(L1_gnn_b_ih),
        "bhh": np.asarray(L1_gnn_b_hh),
    }
    nc = bacc.Bacc("TRN2", target_bir_lowering=False, num_devices=1)
    args = [nc.dram_tensor(f"in_{name}", a.shape, mybir.dt.from_np(a.dtype), kind="ExternalInput").ap()
            for name, a in arrays.items()]
    out = nc.dram_tensor("out", [N, D], F32, kind="ExternalOutput").ap()
    program(nc, *args, out)
    r = run_bass_kernel_spmd(nc, [{f"in_{name}": a for name, a in arrays.items()}], core_ids=[0])
    return r.results[0]["out"]
```

```python
import concourse.bass as bass
from concourse import mybir
from contextlib import ExitStack

F32 = mybir.dt.float32
I32 = mybir.dt.int32
BF16 = mybir.dt.bfloat16
U8 = mybir.dt.uint8
ALU = mybir.AluOpType
ACT = mybir.ActivationFunctionType
AX = mybir.AxisListType

P = 128
N = 50000
E = 25000
D = 64
NT = 4
STEPS = 5
EPS = 1e-5
ET = -(-E // P)
Q = 4
NQ = ET // Q
R = 7
NR = NQ // R
BT = N // P
NB = P * BT
TAIL = N - NB
G = 6
NG = BT // G
H = 2 * Q
HL = BT - H * (NQ - 1)
CH = 2 * R
X_RING = 5
ROWS = NB + P * ET
SKIP = 1000000
TAIL_P = E % P


def flat(ap):
    return ap.rearrange("p a b -> p (a b)")


def pipeline(eng, n, lags, back=2, tail=0):
    deep = max(lag for lag, _ in lags)
    for s in range(deep + back):
        for lag, body in lags:
            if s >= lag:
                body(s - lag)
    with eng.Fori(deep + back, n - tail) as s:
        for lag, body in lags:
            body(s - lag)
    for s in range(n - tail, n + deep):
        for lag, body in lags:
            if s - lag < n:
                body(s - lag)


class Steps:

    def __init__(self, sem, per):
        self.sem, self.per = sem, per

    def begin(self, eng, it):
        self.eng, self.it, self.done = eng, it, 0

    def mark(self, ins):
        self.done += 1
        assert self.done <= self.per
        ins.then_inc(self.sem, 1)

    def link(self, ins):
        self.mark(ins)
        self.eng.wait_ge(self.sem, self.per * self.it + self.done)

    def end(self):
        assert self.done == self.per, (self.done, self.per)

    def wait(self, eng, it, k=None):
        if isinstance(it, int) and it < 0:
            return
        eng.wait_ge(self.sem, self.per * it + (self.per if k is None else k))


def program(nc, x, edge_attr, dst_col, dst_next, dst_row, prev_last, src_col, slot_node, type_col,
            wm_t, bm, wa_t, ba, wl_t, bl, wih_t, whh_t, bih, bhh, out):
    ctx = ExitStack()
    with ctx:
        def sb(name, shape, dt=F32):
            return ctx.enter_context(nc.sbuf_tensor(name, shape, dt))

        def sem(name):
            return ctx.enter_context(nc.semaphore(name))

        node_row = nc.dram_tensor("node_row", [N, 1], I32, kind="Internal").ap()
        h0_tab = nc.dram_tensor("h0_tab", [N, D], F32, kind="Internal").ap()
        x1_tab = nc.dram_tensor("x1_tab", [ROWS, D], F32, kind="Internal").ap()
        state = [nc.dram_tensor(f"state{k}", [ROWS, D], F32, kind="Internal").ap() for k in range(STEPS)]

        def node_part(tab):
            return tab[0:NB, :].rearrange("(p t) d -> p (t d)", t=BT)

        def slot_part(tab):
            return tab[NB:ROWS, :].rearrange("(p t) d -> p (t d)", t=ET)

        ident = sb("ident", [P, P])
        eps = sb("eps", [P, 1])
        wm = sb("wm", [P, D])
        bm_all = sb("bm_all", [P, D])
        wa1 = sb("wa1", [P, D])
        wa2 = sb("wa2", [P, D + 1])
        wl = sb("wl", [P, NT * D])
        wg = sb("wg", [P, 4 * D])
        wh = sb("wh", [P, 3 * D])
        bin_all = sb("bin_all", [P, D])
        h_slot = sb("h_slot", [P, ET * D])
        brow_i = h_slot[0:D + 1, 0:4 * D]
        brow_h = h_slot[0:D + 1, 4 * D:8 * D]
        b3f = h_slot[0:3, 8 * D:16 * D].rearrange("p (a b) -> p a b", b=4 * D)
        b3acc = h_slot[0:3, 16 * D:24 * D].rearrange("p (a b) -> p a b", b=4 * D)
        b3part = h_slot[0:3, 24 * D:28 * D].bitcast(BF16).rearrange("p (a b) -> p a b", b=4 * D)
        last_f = h_slot[:, 32 * D:32 * D + ET]
        dstn_i = h_slot[:, 36 * D:36 * D + ET].bitcast(I32)
        bias3 = sb("bias3", [P, 4 * D], BF16)
        ones3 = sb("ones3", [P, P], BF16)
        dst_i = sb("dst_i", [P, ET], I32)
        src_i = sb("src_i", [P, ET], I32)
        slot_i = sb("slot_i", [P, ET], I32)
        type_i = sb("type_i", [P, ET], I32)
        prev_i = sb("prev_i", [D + 1, ET], I32)
        dst_f = sb("dst_f", [P, ET])
        prev_f = sb("prev_f", [D + 1, ET])
        own_idx = sb("own_idx", [P, ET], I32)
        slot_row = sb("slot_row", [P, ET], I32)
        node_ids = sb("node_ids", [P, BT], I32)
        tail_rows = sb("tail_rows", [TAIL, 1], I32)
        tail_now = sb("tail_now", [P, 1], I32)
        tail_f = sb("tail_f", [P, 4])
        cand = sb("cand", [P, 1], I32)
        src_row = sb("src_row", [P, ET], I32)
        tmask = sb("tmask", [P, 3, ET], I32)
        tm_st = sb("tm_st", [P, 3, Q], I32)
        same = sb("same", [P, ET * P], BF16)
        cont = sb("cont", [D + 1, ET * P], U8)
        idx_st = sb("idx_st", [P, 2, R * Q], I32)
        val_st = sb("val_st", [P, R * Q], I32)
        rings = sb("rings", [P, 2 * R * Q * D])
        ring, xring = rings[:, 0:R * Q * D], rings[:, R * Q * D:2 * R * Q * D]
        drow = rings[:, :].bitcast(I32)
        assert R * Q * P == 2 * R * Q * D
        nring = sb("nring", [P, 4 * H * D])
        stage = sb("stage", [P, G, D])
        stage2 = sb("stage2", [P, Q, D])
        hT = sb("hT", [P, G * P])
        m = sb("m", [P, Q, D])
        mres = sb("mres", [P, Q, D])
        parts = sb("parts", [P, 3, Q, D + 1], BF16)
        stack = sb("stack", [P, Q * P])
        rz = sb("rz", [P, Q, 2 * D])
        pre = sb("pre", [P, Q, D])
        cn = sb("cn", [P, Q, D])
        blend = sb("blend", [P, Q, D])
        blend_b = sb("blend_b", [P, H, D])
        hnew = sb("hnew", [P, H, D])
        fin = sb("fin", [P, H, D])
        rdeg = sb("rdeg", [P, 2, Q])
        ln_s = sb("ln_s", [P, 2, 5, G])
        shared = sb("shared", [P, 88 * D])

        def carve(at, width):
            return shared[:, at * D:(at + width) * D]

        def tiles(ap, n):
            return ap.rearrange("p (n d) -> p n d", n=n)

        he, heT, aggT = tiles(carve(0, 2 * Q), Q), carve(8, 2 * Q), carve(16, 2 * Q)
        x1b = tiles(carve(24, G), G)
        ln_c = carve(30, 2 * G).rearrange("p (u a b) -> p u a b", u=2, b=D)
        ln_q = carve(42, 2 * G).rearrange("p (u a b) -> p u a b", u=2, b=D)
        hT_b, stage_b = carve(0, 4 * Q), tiles(carve(16, H), H)
        rz_b, pre_b, cn_b = tiles(carve(24, 2 * H), H), tiles(carve(40, H), H), tiles(carve(48, H), H)
        xring_b = carve(56, 4 * H)
        ps = ctx.enter_context(nc.psum_tensor("ps", [P, 8, 512], F32))
        psf = ps[:, :, :].rearrange("p a b -> p (a b)")

        s_const = sem("s_const")
        s_setup = sem("s_setup")
        s_prep = sem("s_prep")
        s_tail = sem("s_tail")
        s_tailc = sem("s_tailc")
        s_minit = sem("s_minit")
        s_mset = sem("s_mset")
        s_mget = sem("s_mget")
        s_pool = sem("s_pool")
        s_tailnow = sem("s_tailnow")
        s_drow = sem("s_drow")
        s_ones = sem("s_ones")
        s_same = sem("s_same")
        b0_ld, b0_sth, b0_stx, b0_sts = sem("b0_ld"), sem("b0_sth"), sem("b0_stx"), sem("b0_sts")
        b0_va, b0_vb, b0_vc, b0_vd = Steps(sem("b0_va"), 3), Steps(sem("b0_vb"), 3), Steps(sem("b0_vc"), 4), Steps(sem("b0_vd"), 3)
        b0_sq0, b0_rt0, b0_ev, b0_sq1, b0_rt1 = (Steps(sem(f"b0_{n}"), c) for n, c in
                                                 (("sq0", 1), ("rt0", 1), ("ev", 2), ("sq1", 1), ("rt1", 1)))
        b0_tr, b0_mm = Steps(sem("b0_tr"), 1), Steps(sem("b0_mm"), 1)
        a0_ea, a0_stx, a0_sts = sem("a0_ea"), sem("a0_stx"), sem("a0_sts")
        a0_g = [sem(f"a0_g{q}") for q in range(R)]
        a0_quad = sem("a0_quad")
        a0_he, a0_ev, a0_cut, a0_evh = Steps(sem("a0_he"), 2), Steps(sem("a0_ev"), 1), Steps(sem("a0_cut"), 2), Steps(sem("a0_evh"), 1)
        a0_sq0, a0_rt0, a0_sq1, a0_rt1 = (Steps(sem(f"a0_{n}"), 1) for n in ("sq0", "rt0", "sq1", "rt1"))
        a0_msg, a0_va, a0_vb, a0_sum, a0_upd, a0_vd = (Steps(sem(f"a0_{n}"), c) for n, c in
                                                       (("msg", 3), ("va", 3), ("vb", 3), ("sum", Q), ("upd", 8), ("vd", 3)))
        a0_p0, a0_p1, a0_p2, a0_p3 = (Steps(sem(f"a0_p{j}"), n) for j, n in enumerate((1, 1, 2, 1)))
        b_ld, b_ld1, b_st = sem("b_ld"), sem("b_ld1"), sem("b_st")
        b_stg, b_ev, b_sig, b_tanh = Steps(sem("b_stg"), 1), Steps(sem("b_ev"), 2), Steps(sem("b_sig"), 2), Steps(sem("b_tanh"), 1)
        b_pre, b_new = Steps(sem("b_pre"), 4), Steps(sem("b_new"), 3)
        b_tr, b_gate = Steps(sem("b_tr"), 2), Steps(sem("b_gate"), 2)
        b_fin = sem("b_fin")
        a_g = [sem(f"a_g{q}") for q in range(R)]
        a_quad, a_st = sem("a_quad"), sem("a_st")
        a_stg, a_ev, a_m0, a_cut, a_stgh, a_evh, a_sig, a_tanh = (Steps(sem(f"a_{n}"), c) for n, c in (
            ("stg", 1), ("ev", 1), ("m0", 1), ("cut", 2), ("stgh", 1), ("evh", 1), ("sig", 1), ("tanh", 1)))
        a_msg, a_res, a_sum, a_pre, a_new = (Steps(sem(f"a_{n}"), c) for n, c in (
            ("msg", NT), ("res", 2), ("sum", Q), ("pre", 2), ("new", 3)))
        a_tr, a_trh, a_mm, a_agg, a_gate = (Steps(sem(f"a_{n}"), 1) for n in ("tr", "trh", "mm", "agg", "gate"))
        f_ld = sem("f_ld")
        f_v = sem("f_v")
        f_sc = [sem(f"f_sc{q}") for q in range(R)]

        s_held = sem("s_held")

        def hold(eng):
            eng.sem_inc(s_held, 1)

        def gates_a():
            return ps[:, 4:6, :].rearrange("p a (t c) -> p (a t) c", c=4 * D)

        def gates_b():
            return ps[:, 6:8, :].rearrange("p a (t c) -> p (a t) c", c=4 * D)

        block = ctx.enter_context(nc.Block())
        consts = []

        @block.sync
        def _(sp):
            def load(dst, src):
                consts.append(1)
                sp.dma_start(dst, src).then_inc(s_const, 16)

            load(wm[:, :], wm_t)
            load(bm_all[:, :], bm.rearrange("(a d) -> a d", a=1).to_broadcast([P, D]))
            load(bin_all[:, :], bih[2 * D:3 * D].rearrange("(a d) -> a d", a=1).to_broadcast([P, D]))
            load(dst_i[:, :], dst_col)
            load(dstn_i[:, :], dst_next)
            load(src_i[:, :], src_col)
            load(slot_i[:, :], slot_node)
            load(type_i[:, :], type_col)
            load(prev_i[:, :], prev_last.to_broadcast([D + 1, ET]))
            sp.wait_ge(s_setup, 17)
            load(wa1[0:D, :], wa_t[0:D, :])
            load(wa1[D:D + 1, :], ba.rearrange("(a d) -> a d", a=1))
            load(wa2[0:D, 0:D], wa_t[D:2 * D, :])
            load(wl[0:D, :], wl_t)
            load(wl[D:D + 1, :], bl.rearrange("(a t) d -> a (t d)", a=1))
            load(wg[0:D, 0:2 * D], wih_t[:, 0:2 * D])
            load(wg[0:D, 3 * D:4 * D], wih_t[:, 2 * D:3 * D])
            load(wg[D:2 * D, 0:3 * D], whh_t)
            load(wh[0:D, 0:3 * D], whh_t)
            row = lambda v: v.rearrange("(a d) -> a d", a=1)
            load(brow_i[D:D + 1, 0:2 * D], row(bih[0:2 * D]))
            load(brow_i[D:D + 1, 3 * D:4 * D], row(bih[2 * D:3 * D]))
            load(brow_h[D:D + 1, 0:3 * D], row(bhh))
            load(b3f[:, 0, 0:2 * D], row(bih[0:2 * D]).to_broadcast([3, 2 * D]))
            load(b3f[:, 0, 3 * D:4 * D], row(bih[2 * D:3 * D]).to_broadcast([3, D]))
            load(b3f[:, 1, 0:3 * D], row(bhh).to_broadcast([3, 3 * D]))

            sp.wait_ge(s_setup, 20)
            sp.dma_start(node_row[0:NB, :].rearrange("(p t) a -> p (t a)", t=BT), node_ids[:, :]).then_inc(s_minit, 16)
            sp.dma_start(node_row[NB:N, :], tail_rows[:, :]).then_inc(s_minit, 16)
            sp.dma_start(x1b[0:TAIL, 0, :], x[NB:N, :]).then_inc(s_tail, 16)
            sp.wait_ge(s_prep, 7)
            sp.dma_start(h0_tab[NB:N, :], hnew[0:TAIL, 0, :]).then_inc(s_tail, 16)
            sp.wait_ge(s_tail, 32)

            W = G * D
            x_v, h0_v = node_part(x), node_part(h0_tab)

            def b0_load(i):
                b0_vc.wait(sp, i - X_RING, 1)
                sp.dma_start(nring[:, bass.ds((i % X_RING) * W, W)], x_v[:, bass.ds(i * W, W)]).then_inc(b0_ld, 16)

            def b0_store_h0(i):
                b0_vb.wait(sp, i)
                sp.dma_start(h0_v[:, bass.ds(i * W, W)], flat(stage[:, :, :])).then_inc(b0_sth, 16)

            def b0_store_x1(i):
                b0_vc.wait(sp, i, 1)
                sp.dma_start(node_part(x1_tab)[:, bass.ds(i * W, W)], flat(x1b[:, :, :])).then_inc(b0_stx, 16)

            def b0_store_state(i):
                b0_vd.wait(sp, i)
                sp.dma_start(node_part(state[0])[:, bass.ds(i * W, W)], flat(hnew[:, 0:G, :])).then_inc(b0_sts, 16)

            def b0_arrived(s, n):
                if not isinstance(n, int) or n > 0:
                    sp.wait_ge(s, 16 * n)
                    hold(sp)

            pipeline(sp, NG, [(0, lambda i: b0_arrived(b0_ld, i)), (0, b0_load),
                              (2, lambda i: b0_arrived(b0_sth, i)), (2, b0_store_h0),
                              (4, lambda i: b0_arrived(b0_stx, i)), (4, b0_store_x1),
                              (5, lambda i: b0_arrived(b0_sts, i)), (5, b0_store_state)], back=7)

            C = CH * P

            def rows_in(r):
                if not isinstance(r, int) or r > 1:
                    sp.wait_ge(s_same, 2 * r - 2)
                sp.dma_start(drow[:, bass.ds((r % 2) * C, C)], dst_row[:, bass.ds(r * C, C)].to_broadcast([P, C])
                             ).then_inc(s_drow, 16)
                sp.wait_ge(s_drow, 16 * (r + 1))
                hold(sp)

            for r in range(2):
                rows_in(r)
            with sp.Fori(2, ET // CH) as r:
                rows_in(r)

            V = Q * D

            def a0_load(i):
                b0_arrived(a0_ea, i)
                a0_he.wait(sp, i - 4)
                sp.dma_start(nring[:, bass.ds((i % 4) * V, V)], edge_attr[:, bass.ds(i * V, V)]).then_inc(a0_ea, 16)

            def a0_store_x1(i):
                a0_upd.wait(sp, i, 5)
                sp.dma_start(slot_part(x1_tab)[:, bass.ds(i * V, V)], flat(x1b[:, 0:Q, :])).then_inc(a0_stx, 16)
                sp.wait_ge(a0_stx, 16 * (i + 1))
                hold(sp)

            def a0_store(i):
                a0_vd.wait(sp, i)
                sp.dma_start(slot_part(state[0])[:, bass.ds(i * V, V)], h_slot[:, bass.ds(i * V, V)]).then_inc(a0_sts, 16)
                sp.wait_ge(a0_sts, 16 * (i + 1))
                hold(sp)

            sp.wait_ge(b0_sth, 16 * NG)
            b0_vd.wait(sp, NG - 1)
            pipeline(sp, NQ, [(0, a0_load), (4, a0_store_x1), (5, a0_store)], back=5)

            for k in range(STEPS):
                last = k == STEPS - 1
                src_t = node_part(state[k])
                dst_t = node_part(out if last else state[k + 1])
                if k == 0:
                    a0_he.wait(sp, NQ - 1)
                    sp.wait_ge(b0_sts, 16 * NG)
                    sp.wait_ge(b0_stx, 16 * NG)

                def cols(i):
                    w = (HL if isinstance(i, int) and i == NQ - 1 else H) * D
                    return bass.ds(i * H * D, w), w

                def b_load(i):
                    it = i + k * NQ
                    b_new.wait(sp, it - 4)
                    hold(sp)
                    c, w = cols(i)
                    sp.dma_start(nring[:, bass.ds((it % 4) * H * D, w)], src_t[:, c]).then_inc(b_ld, 16)
                    if last:
                        if not isinstance(i, int) or i >= 4:
                            sp.wait_ge(b_fin, i - 3)
                        sp.dma_start(xring_b[:, bass.ds((it % 4) * H * D, w)], node_part(x1_tab)[:, c]).then_inc(b_ld1, 16)
                        sp.wait_ge(b_ld1, 16 * (i + 1))
                    sp.wait_ge(b_ld, 16 * (it + 1))
                    hold(sp)

                def b_store(i):
                    it = i + k * NQ
                    if last:
                        sp.wait_ge(b_fin, i + 1)
                    else:
                        b_new.wait(sp, it)
                    c, w = cols(i)
                    sp.dma_start(dst_t[:, c], flat((fin if last else hnew)[:, :, :])[:, 0:w]).then_inc(b_st, 16)
                    sp.wait_ge(b_st, 16 * (it + 1))
                    hold(sp)

                def a_store(i):
                    it = i + k * NQ
                    a_new.wait(sp, it)
                    sp.dma_start(slot_part(state[k + 1])[:, bass.ds(i * V, V)],
                                 h_slot[:, bass.ds(i * V, V)]).then_inc(a_st, 16)
                    sp.wait_ge(a_st, 16 * (it + 1))
                    hold(sp)

                pipeline(sp, NQ, [(0, b_load), (2, b_store)] + ([] if last else [(4, a_store)]), back=6, tail=1)

            def f_load(i):
                if not isinstance(i, int):
                    sp.wait_ge(f_v, i - 3)
                sp.dma_start(nring[:, bass.ds((i % 4) * V, V)], slot_part(x1_tab)[:, bass.ds(i * V, V)]).then_inc(f_ld, 16)
                sp.wait_ge(f_ld, 16 * (i + 1))
                hold(sp)

            for i in range(4):
                f_load(i)
            with sp.Fori(4, NQ) as i:
                f_load(i)
            for q in range(R):
                sp.wait_ge(f_sc[q], 16 * Q * NR)

        @block.gpsimd
        def _(pool):
            setup = [0]

            def mark(ins):
                setup[0] += 1
                ins.then_inc(s_setup, 1)
                pool.wait_ge(s_setup, setup[0])

            mark(pool.memset(ident[:, :], 0.0))
            mark(pool.memset(eps[:, :], EPS))
            mark(pool.memset(wa2[:, :], 0.0))
            mark(pool.memset(wg[:, :], 0.0))
            mark(pool.memset(wh[:, :], 0.0))
            mark(pool.memset(wa1[:, :], 0.0))
            mark(pool.memset(wl[:, :], 0.0))
            mark(pool.memset(bias3[:, :], 0.0))
            mark(pool.memset(hT[D:2 * D, :], 0.0))
            mark(pool.memset(brow_i[:, :], 0.0))
            mark(pool.memset(brow_h[:, :], 0.0))
            mark(pool.memset(b3f[:, :, :], 0.0))
            mark(pool.memset(ones3[:, :], 0.0))
            mark(pool.memset(ones3[0:3, :], 1.0))
            mark(pool.memset(hT[D:D + 1, :], 1.0))
            mark(pool.memset(parts[:, :, :, :], 0.0))
            mark(pool.memset(tail_now[:, :], 0))
            mark(pool.iota(slot_row[:, :], pattern=[[1, ET]], base=NB, channel_multiplier=ET))
            mark(pool.iota(node_ids[:, :], pattern=[[1, BT]], base=0, channel_multiplier=BT))
            mark(pool.iota(tail_rows[:, :], pattern=[[0, 1]], base=NB + TAIL_P * ET + ET - 1, channel_multiplier=ET))
            mark(pool.iota(cand[:, :], pattern=[[0, 1]], base=NB - TAIL_P, channel_multiplier=1))
            mark(pool.affine_select(out=ident[:, :], in_=ident[:, :], compare_op=ALU.not_equal, fill=1.0,
                                    base=0, pattern=[[-1, P]], channel_multiplier=1))
            mark(pool.memset(wa2[D:D + 1, D:D + 1], 1.0))
            mark(pool.memset(parts[:, 0, :, D:D + 1], 1.0))

            T = R * Q
            pool.wait_ge(s_prep, 9)
            pool.wait_ge(s_minit, 32)

            def step(ins):
                ins.then_inc(s_pool, 1)

            with pool.Fori(0, NR) as r:
                step(pool.tensor_copy(idx_st[:, 0, :], own_idx[:, bass.ds(r * T, T)]))
                step(pool.tensor_copy(val_st[:, :], slot_row[:, bass.ds(r * T, T)]))
                pool.wait_ge(s_pool, 2 * r + 2)
                hold(pool)
                for t in range(T):
                    pool.indirect_dma_start(out=node_row[:, :],
                                            out_offset=bass.IndirectOffsetOnAxis(ap=idx_st[:, 0, t:t + 1], axis=0),
                                            in_=val_st[:, t:t + 1], in_offset=None,
                                            bounds_check=N - 1, oob_is_err=False).then_inc(s_mset, 16)
                pool.wait_ge(s_mset, 16 * T * (r + 1))
                hold(pool)
            with pool.Fori(0, NR) as r:
                step(pool.tensor_copy(idx_st[:, 0, :], src_i[:, bass.ds(r * T, T)]))
                pool.wait_ge(s_pool, 2 * NR + 2 * r + 1)
                hold(pool)
                for t in range(T):
                    pool.indirect_dma_start(out=val_st[:, t:t + 1], out_offset=None, in_=node_row[:, :],
                                            in_offset=bass.IndirectOffsetOnAxis(ap=idx_st[:, 0, t:t + 1], axis=0)
                                            ).then_inc(s_mget, 16)
                pool.wait_ge(s_mget, 16 * T * (r + 1))
                step(pool.tensor_copy(src_row[:, bass.ds(r * T, T)], val_st[:, :]))
                pool.wait_ge(s_pool, 2 * NR + 2 * r + 2)
                hold(pool)
            pool.dma_start(tail_now[TAIL_P:TAIL_P + TAIL, :], node_row[NB:N, :]).then_inc(s_tailnow, 16)

            pool.wait_ge(b0_sth, 16 * NG)
            pool.wait_ge(s_tail, 32)
            pool.wait_ge(s_same, 2 * ET // CH)
            done = 4 * NR

            def a0_quad_in(r, q):
                i = r * R + q
                for j in range(Q):
                    t = q * Q + j
                    pool.indirect_dma_start(out=xring[:, t * D:(t + 1) * D], out_offset=None, in_=x[:, :],
                                            in_offset=bass.IndirectOffsetOnAxis(ap=idx_st[:, 0, t:t + 1], axis=0)
                                            ).then_inc(a0_g[q], 16)
                    pool.indirect_dma_start(out=ring[:, t * D:(t + 1) * D], out_offset=None, in_=h0_tab[:, :],
                                            in_offset=bass.IndirectOffsetOnAxis(ap=idx_st[:, 1, t:t + 1], axis=0)
                                            ).then_inc(a0_g[q], 16)

            def forward(sems, q, r, per, quad_sem):
                pool.wait_ge(sems[q], per * (r + 1))
                pool.sem_inc(quad_sem, 1)

            def a0_round(r):
                step(pool.tensor_copy(idx_st[:, 0, :], slot_i[:, bass.ds(r * T, T)]))
                step(pool.tensor_copy(idx_st[:, 1, :], src_i[:, bass.ds(r * T, T)]))
                pool.wait_ge(s_pool, done + 2 * r + 2)
                hold(pool)
                for q in range(R):
                    if not isinstance(r, int):
                        a0_upd.wait(pool, (r - 1) * R + q)
                        hold(pool)
                    a0_quad_in(r, q)
                    if q:
                        forward(a0_g, q - 1, r, 32 * Q, a0_quad)
                forward(a0_g, R - 1, r, 32 * Q, a0_quad)

            a0_round(0)
            with pool.Fori(1, NR) as r:
                a0_round(r)
            done += 2 * NR

            pool.wait_ge(b0_sts, 16 * NG)
            for k in range(STEPS):
                if k == 0:
                    pool.wait_ge(a0_sts, 16 * NQ)
                else:
                    pool.wait_ge(a_st, 16 * NQ * k)
                    pool.wait_ge(b_st, 16 * NQ * k)

                def a_round(r):
                    step(pool.tensor_copy(idx_st[:, 0, :], src_row[:, bass.ds(r * T, T)]))
                    pool.wait_ge(s_pool, done + r + 1)
                    for q in range(R):
                        it = r * R + q + k * NQ
                        a_stg.wait(pool, it - R)
                        hold(pool)
                        for j in range(Q):
                            t = q * Q + j
                            pool.indirect_dma_start(out=ring[:, t * D:(t + 1) * D], out_offset=None, in_=state[k][:, :],
                                                    in_offset=bass.IndirectOffsetOnAxis(ap=idx_st[:, 0, t:t + 1], axis=0)
                                                    ).then_inc(a_g[q], 16)
                        if q:
                            forward(a_g, q - 1, r + k * NR, 16 * Q, a_quad)
                    forward(a_g, R - 1, r + k * NR, 16 * Q, a_quad)

                a_round(0)
                with pool.Fori(1, NR) as r:
                    a_round(r)
                done += NR

            pool.wait_ge(b_st, 16 * NQ * STEPS)

            def f_round(r):
                step(pool.tensor_copy(idx_st[:, 0, :], own_idx[:, bass.ds(r * T, T)]))
                pool.wait_ge(s_pool, done + r + 1)
                for q in range(R):
                    pool.wait_ge(f_v, r * R + q + 1)
                    hold(pool)
                    for j in range(Q):
                        t = q * Q + j
                        pool.indirect_dma_start(out=out[:, :],
                                                out_offset=bass.IndirectOffsetOnAxis(ap=idx_st[:, 0, t:t + 1], axis=0),
                                                in_=ring[:, t * D:(t + 1) * D], in_offset=None,
                                                bounds_check=N - 1, oob_is_err=False).then_inc(f_sc[q], 16)

            f_round(0)
            with pool.Fori(1, NR) as r:
                for q in range(R):
                    pool.wait_ge(f_sc[q], 16 * Q * r)
                f_round(r)
            for q in range(R):
                pool.wait_ge(f_sc[q], 16 * Q * NR)

        @block.scalar
        def _(act):
            def copy(out_, in_):
                return nc.scalar.activation(out_, in_, ACT.Copy)

            def root(u, n, p=P):
                return nc.scalar.activation(ln_s[0:p, u, 3, 0:n], ln_s[0:p, u, 2, 0:n], ACT.Sqrt,
                                            bias=eps[0:p, :], scale=1.0 / D)

            act.wait_ge(s_setup, 24)
            act.wait_ge(s_prep, 5)
            root(0, 1, TAIL).then_inc(s_tailc, 1)

            def square(u, n):
                return nc.scalar.activation(ln_q[:, u, 0:n, :], ln_c[:, u, 0:n, :], ACT.Square)

            def one(steps, it, ins):
                steps.begin(act, it)
                steps.mark(ins())
                steps.end()

            def b0_root1(i):
                b0_vd.wait(act, i, 1)
                one(b0_rt1, i, lambda: root(1, G))

            def b0_root0(i):
                b0_vb.wait(act, i, 1)
                one(b0_rt0, i, lambda: root(0, G))

            def b0_copy(i):
                b0_tr.wait(act, i)
                b0_mm.wait(act, i - 1)
                b0_ev.begin(act, i)
                b0_ev.mark(copy(hT[0:D, 0:3 * P], ps[0:D, 0, 0:3 * P]))
                b0_ev.mark(copy(hT[0:D, 3 * P:6 * P], ps[0:D, 1, 0:3 * P]))
                b0_ev.end()

            def b0_square1(i):
                b0_vc.wait(act, i)
                b0_vd.wait(act, i - 1, 1)
                one(b0_sq1, i, lambda: square(1, G))

            def b0_square0(i):
                b0_va.wait(act, i)
                b0_vb.wait(act, i - 1, 1)
                one(b0_sq0, i, lambda: square(0, G))

            pipeline(act, NG, [(4, b0_root1), (1, b0_root0), (2, b0_copy), (3, b0_square1), (0, b0_square0)])

            b0_vd.wait(act, NG - 1)
            act.wait_ge(b0_stx, 16 * NG)
            V = Q * D

            def a0_he_in(i):
                a0_he.begin(act, i)
                act.wait_ge(a0_quad, i + 1)
                a0_p0.wait(act, i - 1)
                a0_he.mark(copy(he[:, :, 0:D], tiles(ring[:, bass.ds((i % R) * V, V)], Q)))
                act.wait_ge(a0_ea, 16 * (i + 1))
                a0_he.mark(copy(he[:, :, D:2 * D], tiles(nring[:, bass.ds((i % 4) * V, V)], Q)))
                a0_he.end()

            def a0_copy(i):
                a0_p0.wait(act, i)
                a0_p1.wait(act, i - 1)
                one(a0_ev, i, lambda: copy(heT, ps[:, 0, :]))

            def a0_hi(i):
                a0_msg.wait(act, i, 1)
                a0_p2.wait(act, i - 1)
                a0_cut.begin(act, i)
                a0_cut.mark(copy(parts[:, 0, :, 0:D], m[:, :, :]))

            def a0_mid(i):
                a0_msg.wait(act, i, 2)
                a0_cut.mark(copy(parts[:, 1, :, 0:D], mres[:, :, :]))
                a0_cut.end()

            def a0_root0(i):
                a0_vb.wait(act, i, 1)
                one(a0_rt0, i, lambda: root(0, Q))

            def a0_copy_h(i):
                a0_p2.wait(act, i, 1)
                a0_p3.wait(act, i - 1)
                one(a0_evh, i, lambda: copy(hT[0:D, 0:Q * P], ps[0:D, 1, :]))

            def a0_root1(i):
                a0_vd.wait(act, i, 1)
                one(a0_rt1, i, lambda: root(1, Q))

            def a0_square0(i):
                a0_va.wait(act, i)
                a0_vb.wait(act, i - 1, 1)
                one(a0_sq0, i, lambda: square(0, Q))

            def a0_square1(i):
                a0_upd.wait(act, i)
                a0_vd.wait(act, i - 1, 1)
                one(a0_sq1, i, lambda: square(1, Q))

            pipeline(act, NQ, [(0, a0_he_in), (1, a0_hi), (4, a0_root1), (1, a0_root0), (1, a0_mid), (0, a0_copy),
                               (0, a0_square0), (2, a0_copy_h), (3, a0_square1)])

            a0_vd.wait(act, NQ - 1)
            for k in range(STEPS):
                at = lambda i: i + k * NQ

                def stage_nodes(i):
                    act.wait_ge(b_ld, 16 * (at(i) + 1))
                    b_tr.wait(act, at(i) - 1)
                    one(b_stg, at(i), lambda: copy(flat(stage_b), nring[:, bass.ds((at(i) % 4) * H * D, H * D)]))

                def copy_nodes(u):
                    def body(i):
                        b_tr.wait(act, at(i), u + 1)
                        b_gate.wait(act, at(i) - 1, u + 1)
                        if u == 0:
                            b_ev.begin(act, at(i))
                        b_ev.mark(copy(hT_b[0:D, u * Q * P:(u + 1) * Q * P], ps[0:D, 0, :]))
                    return body

                def sigmoid_nodes(u):
                    def body(i):
                        b_gate.wait(act, at(i), u + 1)
                        if u == 0:
                            b_sig.begin(act, at(i))
                            b_new.wait(act, at(i) - 1)
                        b_sig.mark(nc.scalar.activation(rz_b[:, u * Q:(u + 1) * Q, :], gates_b()[:, :, 0:2 * D], ACT.Sigmoid))
                    return body

                def tanh_nodes(i):
                    b_pre.wait(act, at(i))
                    b_new.wait(act, at(i) - 1)
                    one(b_tanh, at(i), lambda: nc.scalar.activation(flat(cn_b), flat(pre_b), ACT.Tanh))

                def stage_src(i):
                    act.wait_ge(a_quad, at(i) + 1)
                    a_tr.wait(act, at(i) - 1)
                    one(a_stg, at(i), lambda: copy(flat(stage[:, 0:Q, :]), ring[:, bass.ds((i % R) * V, V)]))

                def copy_src(i):
                    a_tr.wait(act, at(i))
                    a_mm.wait(act, at(i) - 1)
                    one(a_ev, at(i), lambda: copy(hT[0:D, 0:Q * P], ps[0:D, 0, :]))

                def type0(i):
                    a_mm.wait(act, at(i))
                    a_res.wait(act, at(i) - 1)
                    one(a_m0, at(i), lambda: copy(m[:, :, :], psf[:, 512:1536].rearrange("p (a t d) -> p a t d", t=NT, d=D)[:, :, 0, :]))

                def hi(i):
                    a_msg.wait(act, at(i))
                    a_agg.wait(act, at(i) - 1)
                    a_cut.begin(act, at(i))
                    a_cut.mark(copy(parts[:, 0, :, 0:D], m[:, :, :]))

                def mid(i):
                    a_res.wait(act, at(i), 1)
                    a_cut.mark(copy(parts[:, 1, :, 0:D], mres[:, :, :]))
                    a_cut.end()

                def stage_slots(i):
                    a_trh.wait(act, at(i) - 1)
                    one(a_stgh, at(i), lambda: copy(flat(stage2[:, :, :]), h_slot[:, bass.ds(i * V, V)]))

                def copy_slots(i):
                    a_trh.wait(act, at(i))
                    a_gate.wait(act, at(i) - 1)
                    one(a_evh, at(i), lambda: copy(stack[D:2 * D, :], ps[0:D, 0, :]))

                def sigmoid_slots(i):
                    a_gate.wait(act, at(i))
                    a_new.wait(act, at(i) - 1)
                    one(a_sig, at(i), lambda: nc.scalar.activation(rz[:, :, :], gates_a()[:, :, 0:2 * D], ACT.Sigmoid))

                def tanh_slots(i):
                    a_pre.wait(act, at(i))
                    one(a_tanh, at(i), lambda: nc.scalar.activation(flat(cn[:, :, :]), flat(pre[:, :, :]), ACT.Tanh))

                pipeline(act, NQ, [(2, hi), (2, tanh_nodes), (2, mid), (2, stage_slots), (3, sigmoid_slots),
                                   (2, copy_slots), (3, tanh_slots), (0, stage_nodes), (1, sigmoid_nodes(0)),
                                   (0, copy_nodes(0)), (0, stage_src), (1, type0), (0, copy_src),
                                   (1, sigmoid_nodes(1)), (0, copy_nodes(1))])

        @block.vector
        def _(dve):
            count = [0]

            def link(ins):
                count[0] += 1
                ins.then_inc(s_prep, 1)
                dve.wait_ge(s_prep, count[0])

            def ln_head(st, u, src, n, p=P):
                wide = lambda a: a.rearrange("p (n o) -> p n o", o=1).to_broadcast([p, n, D])
                st(nc.vector.tensor_reduce(ln_s[0:p, u, 0, 0:n], src, axis=AX.X, op=ALU.add))
                st(nc.vector.tensor_scalar(ln_s[0:p, u, 1, 0:n], ln_s[0:p, u, 0, 0:n], -1.0 / D, None, ALU.mult))
                st(nc.vector.tensor_tensor(ln_c[0:p, u, 0:n, :], src, wide(ln_s[0:p, u, 1, 0:n]), ALU.add))
                st(nc.vector.tensor_tensor(ln_q[0:p, u, 0:n, :], ln_c[0:p, u, 0:n, :], ln_c[0:p, u, 0:n, :], ALU.mult))

            def ln_sum(u, n, p=P):
                return nc.vector.tensor_reduce(ln_s[0:p, u, 2, 0:n], ln_q[0:p, u, 0:n, :], axis=AX.X, op=ALU.add)

            def ln_inv(u, n, p=P):
                return nc.vector.reciprocal(ln_s[0:p, u, 4, 0:n], ln_s[0:p, u, 3, 0:n])

            def ln_out(u, dst, n, p=P):
                wide = ln_s[0:p, u, 4, 0:n].rearrange("p (n o) -> p n o", o=1).to_broadcast([p, n, D])
                return nc.vector.scalar_tensor_tensor(dst, ln_c[0:p, u, 0:n, :], 0.0, wide, ALU.max, ALU.mult)

            dve.wait_ge(s_tail, 16)
            ln_head(link, 0, x1b[0:TAIL, 0:1, :], 1, TAIL)
            link(ln_sum(0, 1, TAIL))
            dve.wait_ge(s_tailc, 1)
            link(ln_inv(0, 1, TAIL))
            link(ln_out(0, hnew[0:TAIL, 0:1, :], 1, TAIL))
            dve.wait_ge(s_const, 16 * len(consts))
            link(nc.vector.tensor_tensor(last_f[:, :], dst_i[:, :], dstn_i[:, :], ALU.is_equal))
            link(nc.vector.scalar_tensor_tensor(own_idx[:, :], last_f[:, :], float(SKIP), dst_i[:, :], ALU.mult, ALU.add))
            link(nc.vector.tensor_copy(dst_f[:, :], dst_i[:, :]))
            link(nc.vector.tensor_copy(prev_f[:, :], prev_i[:, :]))
            for t in range(3):
                link(nc.vector.tensor_scalar(tmask[:, t, :], type_i[:, :], float(t + 1), None, ALU.is_equal))
            dve.wait_ge(s_setup, 24)
            link(nc.vector.tensor_tensor(wh[D:D + 1, :], brow_i[D:D + 1, 0:3 * D], brow_h[D:D + 1, 0:3 * D], ALU.add))
            link(nc.vector.tensor_tensor(b3acc[:, 0, :], b3f[:, 0, :], b3f[:, 1, :], ALU.add))
            link(nc.vector.tensor_copy(b3part[:, 0, :], b3acc[:, 0, :]))
            link(nc.vector.tensor_tensor(b3acc[:, 1, :], b3acc[:, 0, :], b3part[:, 0, :], ALU.subtract))
            link(nc.vector.tensor_copy(b3part[:, 1, :], b3acc[:, 1, :]))
            link(nc.vector.tensor_tensor(b3acc[:, 0, :], b3acc[:, 1, :], b3part[:, 1, :], ALU.subtract))
            link(nc.vector.tensor_scalar(b3acc[:, 1, :], b3part[:, 0, :], ident[0:3, 0:1], None, ALU.mult))
            link(nc.vector.scalar_tensor_tensor(b3acc[:, 1, :], b3part[:, 1, :], ident[0:3, 1:2], b3acc[:, 1, :], ALU.mult, ALU.add))
            link(nc.vector.scalar_tensor_tensor(bias3[0:3, :], b3acc[:, 0, :], ident[0:3, 2:3], b3acc[:, 1, :], ALU.mult, ALU.add))
            dve.wait_ge(s_tail, 32)

            W = G * D

            def ln_centre(st, u, src, n):
                wide = ln_s[:, u, 1, 0:n].rearrange("p (n o) -> p n o", o=1).to_broadcast([P, n, D])
                st.link(nc.vector.tensor_reduce(ln_s[:, u, 0, 0:n], src, axis=AX.X, op=ALU.add))
                st.link(nc.vector.tensor_scalar(ln_s[:, u, 1, 0:n], ln_s[:, u, 0, 0:n], -1.0 / D, None, ALU.mult))
                st.mark(nc.vector.tensor_tensor(ln_c[:, u, 0:n, :], src, wide, ALU.add))

            def xs(i):
                return tiles(nring[:, bass.ds((i % X_RING) * W, W)], G)

            def stored(s, i):
                if not isinstance(i, int) or i > 0:
                    dve.wait_ge(s, 16 * i)

            def b0_sum1(i):
                b0_vd.begin(dve, i)
                b0_sq1.wait(dve, i)
                b0_vd.mark(ln_sum(1, G))

            def b0_sum0(i):
                b0_vb.begin(dve, i)
                b0_sq0.wait(dve, i)
                b0_vb.mark(ln_sum(0, G))

            def b0_x1(i):
                b0_vc.begin(dve, i)
                b0_mm.wait(dve, i)
                stored(b0_stx, i)
                b0_vc.link(nc.vector.scalar_tensor_tensor(x1b, tiles(ps[:, 2, 0:W], G), 0.0, xs(i), ALU.max, ALU.add))

            def b0_out1(i):
                b0_rt1.wait(dve, i)
                b0_vd.link(ln_inv(1, G))
                stored(b0_sts, i)
                b0_vd.mark(ln_out(1, hnew[:, 0:G, :], G))
                b0_vd.end()

            def b0_out0(i):
                b0_rt0.wait(dve, i)
                b0_vb.link(ln_inv(0, G))
                b0_tr.wait(dve, i - 1)
                stored(b0_sth, i)
                b0_vb.mark(ln_out(0, stage[:, :, :], G))
                b0_vb.end()

            def b0_centre1(i):
                b0_vd.wait(dve, i - 1)
                b0_sq1.wait(dve, i - 1)
                ln_centre(b0_vc, 1, x1b, G)
                b0_vc.end()

            def b0_centre0(i):
                b0_va.begin(dve, i)
                dve.wait_ge(b0_ld, 16 * (i + 1))
                b0_vb.wait(dve, i - 1)
                ln_centre(b0_va, 0, xs(i), G)
                b0_va.end()

            pipeline(dve, NG, [(4, b0_sum1), (1, b0_sum0), (3, b0_x1), (4, b0_out1), (1, b0_out0),
                               (3, b0_centre1), (0, b0_centre0)])

            with dve.Fori(0, ET // CH) as r:
                dve.wait_ge(s_drow, 16 * (r + 1))
                rows = drow[:, bass.ds((r % 2) * CH * P, CH * P)].rearrange("p (t e) -> p t e", e=P)

                def wide(v, p):
                    return v[:, bass.ds(r * CH, CH)].rearrange("p (t o) -> p t o", o=1).to_broadcast([p, CH, P])

                def tile_block(v):
                    return v[:, bass.ds(r * CH * P, CH * P)].rearrange("p (t e) -> p t e", e=P)

                nc.vector.tensor_tensor(tile_block(same), rows, wide(dst_f, P), ALU.is_equal).then_inc(s_same, 1)
                nc.vector.tensor_tensor(tile_block(cont), rows[0:D + 1], wide(prev_f, D + 1), ALU.is_equal).then_inc(s_same, 1)
            dve.wait_ge(s_same, 2 * ET // CH)

            V = Q * D
            dve.wait_ge(b0_stx, 16 * NG)
            dve.wait_ge(b0_sts, 16 * NG)
            link(nc.vector.memset(aggT, 0.0))
            link(nc.vector.memset(stack[:, :], 0.0))

            def xq(i):
                return tiles(xring[:, bass.ds((i % R) * V, V)], Q)

            def a0_sum1(i):
                a0_vd.begin(dve, i)
                a0_sq1.wait(dve, i)
                a0_vd.mark(ln_sum(1, Q))

            def a0_sum0(i):
                a0_vb.begin(dve, i)
                a0_sq0.wait(dve, i)
                a0_vb.mark(ln_sum(0, Q))

            def a0_m(i):
                a0_msg.begin(dve, i)
                a0_p1.wait(dve, i)
                a0_cut.wait(dve, i - 1)
                bias = bm_all[:, :].rearrange("p (o d) -> p o d", o=1).to_broadcast([P, Q, D])
                a0_msg.link(nc.vector.tensor_tensor(m[:, :, :], tiles(ps[:, 2, 0:V], Q), bias, ALU.add))

            def a0_out1(i):
                a0_rt1.wait(dve, i)
                a0_vd.link(ln_inv(1, Q))
                a0_vd.mark(ln_out(1, tiles(h_slot[:, bass.ds(i * V, V)], Q), Q))
                a0_vd.end()

            def a0_rest(i):
                a0_cut.wait(dve, i, 1)
                a0_msg.link(nc.vector.tensor_tensor(mres[:, :, :], m[:, :, :], parts[:, 0, :, 0:D], ALU.subtract))

            def a0_out0(i):
                a0_rt0.wait(dve, i)
                a0_vb.link(ln_inv(0, Q))
                a0_p2.wait(dve, i - 1, 1)
                a0_vb.mark(ln_out(0, stage[:, 0:Q, :], Q))
                a0_vb.end()

            def a0_low(i):
                a0_cut.wait(dve, i, 2)
                a0_msg.mark(nc.vector.tensor_tensor(parts[:, 2, :, 0:D], mres[:, :, :], parts[:, 1, :, 0:D], ALU.subtract))
                a0_msg.end()

            def a0_update(i):
                a0_upd.begin(dve, i)
                a0_p3.wait(dve, i)
                agg = ps[:, 5, 0:Q * (D + 1)].rearrange("p (a b) -> p a b", b=D + 1)
                a0_upd.link(nc.vector.tensor_scalar(rdeg[:, 0, :], agg[:, :, D], 1.0, None, ALU.max))
                a0_upd.link(nc.vector.reciprocal(rdeg[:, 1, :], rdeg[:, 0, :]))
                wide = rdeg[:, 1, :].rearrange("p (n o) -> p n o", o=1).to_broadcast([P, Q, D])
                a0_upd.link(nc.vector.tensor_tensor(fin[:, 0:Q, :], agg[:, :, 0:D], wide, ALU.mult))
                a0_upd.link(nc.vector.tensor_tensor(fin[:, 0:Q, :], tiles(ps[:, 6, 0:V], Q), fin[:, 0:Q, :], ALU.add))
                stored(a0_stx, i)
                a0_upd.link(nc.vector.scalar_tensor_tensor(x1b[:, 0:Q, :], fin[:, 0:Q, :], 0.0, xq(i), ALU.max, ALU.add))
                a0_vd.wait(dve, i - 1)
                ln_centre(a0_upd, 1, x1b[:, 0:Q, :], Q)
                a0_upd.end()

            def a0_sums(i):
                a0_sum.begin(dve, i)
                a0_p2.wait(dve, i)
                a0_p3.wait(dve, i - 1)
                for j in range(Q):
                    before = (j + Q - 1) % Q * P + P - 1
                    c = slice(j * P, (j + 1) * P)
                    a0_sum.link(nc.vector.scalar_tensor_tensor(
                        aggT[0:D + 1, c], cont[:, bass.ds((i * Q + j) * P, P)], aggT[0:D + 1, before:before + 1],
                        ps[0:D + 1, 4, c], ALU.mult, ALU.add))
                a0_sum.end()

            def a0_centre0(i):
                a0_va.begin(dve, i)
                dve.wait_ge(a0_quad, i + 1)
                a0_vb.wait(dve, i - 1)
                ln_centre(a0_va, 0, xq(i), Q)
                a0_va.end()

            pipeline(dve, NQ, [(1, a0_m), (4, a0_sum1), (1, a0_sum0), (1, a0_rest), (4, a0_out1), (1, a0_low),
                               (1, a0_out0), (0, a0_centre0), (3, a0_update), (2, a0_sums)])

            dve.wait_ge(s_tailnow, 16)
            link(nc.vector.tensor_tensor(tail_f[:, 0:1], tail_now[:, :], slot_row[:, ET - 1:ET], ALU.is_equal))
            link(nc.vector.tensor_scalar(tail_f[:, 1:2], cand[:, :], -float(SKIP), None, ALU.add))
            link(nc.vector.tensor_tensor(tail_f[:, 2:3], tail_f[:, 0:1], tail_f[:, 1:2], ALU.mult))
            link(nc.vector.tensor_scalar(tail_f[:, 3:4], tail_f[:, 2:3], float(SKIP), None, ALU.add))
            link(nc.vector.tensor_tensor(own_idx[:, ET - 1:ET], own_idx[:, ET - 1:ET], tail_f[:, 3:4], ALU.min))

            link(nc.vector.memset(hT_b[D:2 * D, :], 0.0))
            nc.vector.memset(hT_b[D:D + 1, :], 1.0).then_inc(s_ones, 1)
            for k in range(STEPS):
                last = k == STEPS - 1
                at = lambda i: i + k * NQ
                if k:
                    a_gate.wait(dve, k * NQ - 1)
                link(nc.vector.memset(stack[0:D, Q * P - 1:Q * P], 0.0))

                def rest(i):
                    a_res.begin(dve, at(i))
                    a_cut.wait(dve, at(i), 1)
                    a_res.link(nc.vector.tensor_tensor(mres[:, :, :], m[:, :, :], parts[:, 0, :, 0:D], ALU.subtract))

                def low(i):
                    a_cut.wait(dve, at(i), 2)
                    a_res.mark(nc.vector.tensor_tensor(parts[:, 2, :, 0:D], mres[:, :, :], parts[:, 1, :, 0:D], ALU.subtract))
                    a_res.end()

                def blend_nodes(i):
                    b_new.begin(dve, at(i))
                    h = tiles(nring[:, bass.ds((at(i) % 4) * H * D, H * D)], H)
                    b_tanh.wait(dve, at(i))
                    b_new.mark(nc.vector.tensor_tensor(blend_b[:, :, :], h, cn_b, ALU.subtract))

                def blend_nodes2(i):
                    b_new.wait(dve, at(i), 1)
                    b_new.link(nc.vector.tensor_tensor(blend_b[:, :, :], blend_b[:, :, :], rz_b[:, :, D:2 * D], ALU.mult))
                    stored(b_st, at(i))
                    b_new.mark(nc.vector.tensor_tensor(hnew[:, :, :], blend_b[:, :, :], cn_b, ALU.add))
                    b_new.end()
                    if last:
                        b_new.wait(dve, at(i))
                        dve.wait_ge(b_ld1, 16 * (i + 1))
                        x1 = tiles(xring_b[:, bass.ds((at(i) % 4) * H * D, H * D)], H)
                        nc.vector.tensor_tensor(fin[:, :, :], hnew[:, :, :], x1, ALU.add).then_inc(b_fin, 1)

                def pre_slots(i):
                    a_pre.begin(dve, at(i))
                    a_sig.wait(dve, at(i))
                    a_pre.link(nc.vector.tensor_tensor(pre[:, :, :], gates_a()[:, :, 2 * D:3 * D], rz[:, :, 0:D], ALU.mult))
                    a_pre.mark(nc.vector.tensor_tensor(pre[:, :, :], gates_a()[:, :, 3 * D:4 * D], pre[:, :, :], ALU.add))
                    a_pre.end()

                def run_sums(i):
                    a_sum.begin(dve, at(i))
                    a_agg.wait(dve, at(i))
                    a_gate.wait(dve, at(i) - 1)
                    for j in range(Q):
                        before = (j + Q - 1) % Q * P + P - 1
                        c = slice(j * P, (j + 1) * P)
                        a_sum.link(nc.vector.scalar_tensor_tensor(
                            stack[0:D, c], cont[0:D, bass.ds((i * Q + j) * P, P)], stack[0:D, before:before + 1],
                            ps[0:D, 3, c], ALU.mult, ALU.add))
                    a_sum.end()

                def blend_slots(i):
                    a_new.begin(dve, at(i))
                    h = tiles(h_slot[:, bass.ds(i * V, V)], Q)
                    a_tanh.wait(dve, at(i))
                    a_new.link(nc.vector.tensor_tensor(blend[:, :, :], h, cn[:, :, :], ALU.subtract))
                    a_new.link(nc.vector.tensor_tensor(blend[:, :, :], blend[:, :, :], rz[:, :, D:2 * D], ALU.mult))
                    a_new.mark(nc.vector.tensor_tensor(h, blend[:, :, :], cn[:, :, :], ALU.add))
                    a_new.end()

                def pre_nodes(u):
                    def body(i):
                        if u == 0:
                            b_pre.begin(dve, at(i))
                        half = slice(u * Q, (u + 1) * Q)
                        b_sig.wait(dve, at(i), u + 1)
                        b_tanh.wait(dve, at(i) - 1)
                        b_pre.link(nc.vector.tensor_tensor(pre_b[:, half, :], gates_b()[:, :, 2 * D:3 * D],
                                                           rz_b[:, half, 0:D], ALU.mult))
                        b_pre.mark(nc.vector.tensor_tensor(pre_b[:, half, :], pre_b[:, half, :],
                                                           bin_all[:, :].rearrange("p (o d) -> p o d", o=1).to_broadcast([P, Q, D]), ALU.add))
                    return body

                def by_type(i):
                    a_msg.begin(dve, at(i))
                    a_msg.link(nc.vector.tensor_copy(tm_st[:, :, :], tmask[:, :, bass.ds(i * Q, Q)]))
                    a_m0.wait(dve, at(i))
                    all_t = psf[:, 512:1536].rearrange("p (a t d) -> p a t d", t=NT, d=D)
                    for t in range(1, NT):
                        hold(dve)
                        mask = tm_st[:, t - 1, :].rearrange("p (n o) -> p n o", o=1).to_broadcast([P, Q, D])
                        a_msg.link(nc.vector.copy_predicated(m[:, :, :], mask, all_t[:, :, t, :]))
                    a_msg.end()

                pipeline(dve, NQ, [(2, rest), (2, blend_nodes), (2, low), (2, blend_nodes2), (3, pre_slots), (2, run_sums),
                                   (3, blend_slots), (1, pre_nodes(0)), (1, by_type), (1, pre_nodes(1))])

            def f_add(i, ring_free):
                dve.wait_ge(f_ld, 16 * (i + 1))
                slot = (i % R) * V
                nc.vector.tensor_tensor(ring[:, bass.ds(slot, V)], h_slot[:, bass.ds(i * V, V)],
                                        nring[:, bass.ds((i % 4) * V, V)], ALU.add).then_inc(f_v, 1)

            a_new.wait(dve, NQ * STEPS - 1)
            a_stg.wait(dve, NQ * STEPS - 1)
            for q in range(R):
                f_add(q, None)
            with dve.Fori(1, NR) as r:
                for q in range(R):
                    dve.wait_ge(f_sc[q], 16 * Q * r)
                    f_add(r * R + q, None)

        @block.tensor
        def _(pe):
            pe.wait_ge(s_setup, 24)
            pe.wait_ge(s_const, 16 * len(consts))
            pe.wait_ge(s_prep, 23)

            def transposes(src, n, bank):
                hold(pe)
                for j in range(n):
                    b, c = (bank + j // 3, j % 3) if n == G else (bank, j)
                    last = nc.tensor.transpose(ps[0:D, b, c * P:(c + 1) * P], src[:, j, :], ident[:, :])
                return last

            def b0_transpose(i):
                b0_vb.wait(pe, i)
                b0_ev.wait(pe, i - 1)
                b0_tr.begin(pe, i)
                b0_tr.mark(transposes(stage, G, 0))

            def b0_own(i):
                b0_ev.wait(pe, i)
                b0_vc.wait(pe, i - 1, 1)
                for j in range(G):
                    last = nc.tensor.matmul(ps[:, 2, j * D:(j + 1) * D], hT[:, j * P:(j + 1) * P], wa1[:, :], start=True, stop=True)
                b0_mm.begin(pe, i)
                b0_mm.mark(last)

            pipeline(pe, NG, [(3, b0_own), (2, b0_transpose)])

            def a0_0(i):
                a0_p0.begin(pe, i)
                a0_he.wait(pe, i)
                a0_ev.wait(pe, i - 1)
                for j in range(Q):
                    last = nc.tensor.transpose(ps[:, 0, j * P:(j + 1) * P], he[:, j, :], ident[:, :])
                a0_p0.mark(last)

            def a0_1(i):
                a0_p1.begin(pe, i)
                a0_ev.wait(pe, i)
                a0_msg.wait(pe, i - 1, 1)
                for j in range(Q):
                    last = nc.tensor.matmul(ps[:, 2, j * D:(j + 1) * D], heT[:, j * P:(j + 1) * P], wm[:, :], start=True, stop=True)
                a0_p1.mark(last)

            def sums(i, wide, bank):
                for j in range(Q):
                    for part in range(3):
                        last = nc.tensor.matmul(ps[0:wide, bank, j * P:(j + 1) * P], parts[:, part, j, 0:wide],
                                                same[:, bass.ds((i * Q + j) * P, P)], start=part == 0, stop=part == 2)
                return last

            def a0_2(i):
                a0_p2.begin(pe, i)
                a0_vb.wait(pe, i)
                a0_evh.wait(pe, i - 1)
                a0_p2.mark(transposes(stage, Q, 1))

            def a0_2s(i):
                a0_msg.wait(pe, i)
                a0_sum.wait(pe, i - 1)
                a0_p2.mark(sums(i, D + 1, 4))
                a0_p2.end()

            def a0_3(i):
                a0_p3.begin(pe, i)
                a0_sum.wait(pe, i)
                a0_evh.wait(pe, i)
                a0_upd.wait(pe, i - 1, 4)
                for j in range(Q):
                    nc.tensor.matmul(ps[:, 5, j * (D + 1):(j + 1) * (D + 1)], aggT[:, j * P:(j + 1) * P], wa2[:, :], start=True, stop=True)
                for j in range(Q):
                    last = nc.tensor.matmul(ps[:, 6, j * D:(j + 1) * D], hT[:, j * P:(j + 1) * P], wa1[:, :], start=True, stop=True)
                a0_p3.mark(last)

            pe.wait_ge(s_same, 2 * ET // CH)
            pipeline(pe, NQ, [(1, a0_1), (2, a0_2), (2, a0_2s), (3, a0_3), (0, a0_0)])

            a0_vd.wait(pe, NQ - 1)
            pe.wait_ge(s_ones, 1)
            for k in range(STEPS):
                at = lambda i: i + k * NQ

                def one(steps, it, last):
                    steps.begin(pe, it)
                    steps.mark(last)

                def transpose_slots(i):
                    a_stgh.wait(pe, at(i))
                    if isinstance(i, int) and i == NQ - 1:
                        a_evh.wait(pe, at(i) - 1)
                    else:
                        b_ev.wait(pe, at(i) + 1)
                    one(a_trh, at(i), transposes(stage2, Q, 0))

                def transpose_nodes(u):
                    def body(i):
                        if u == 0:
                            b_stg.wait(pe, at(i))
                            a_evh.wait(pe, at(i) - 2)
                            if isinstance(i, int) and i == 1:
                                b_ev.wait(pe, at(0))
                            b_tr.begin(pe, at(i))
                        else:
                            a_ev.wait(pe, at(i))
                        b_tr.mark(transposes(stage_b[:, u * Q:(u + 1) * Q, :], Q, 0))
                    return body

                def transpose_src(i):
                    a_stg.wait(pe, at(i))
                    b_ev.wait(pe, at(i), 1)
                    one(a_tr, at(i), transposes(stage, Q, 0))

                def messages(i):
                    a_ev.wait(pe, at(i))
                    a_msg.wait(pe, at(i) - 1)
                    for j in range(Q):
                        last = nc.tensor.matmul(psf[:, 512 + j * 256:768 + j * 256], hT[:, j * P:(j + 1) * P], wl[:, :],
                                                start=True, stop=True)
                    one(a_mm, at(i), last)

                def tile_sums(i):
                    a_res.wait(pe, at(i))
                    a_sum.wait(pe, at(i) - 1)
                    one(a_agg, at(i), sums(i, D, 3))

                def gates_slots(i):
                    a_sum.wait(pe, at(i))
                    a_evh.wait(pe, at(i))
                    a_pre.wait(pe, at(i) - 1)
                    for j in range(Q):
                        o = gates_a()[:, j, :]
                        nc.tensor.matmul(o, stack[:, j * P:(j + 1) * P], wg[:, :], start=True, stop=False)
                        last = nc.tensor.matmul(o, ones3[:, :], bias3[:, :], start=False, stop=True)
                    one(a_gate, at(i), last)

                def gates_nodes(u):
                    def body(i):
                        b_ev.wait(pe, at(i), u + 1)
                        if u == 0:
                            b_pre.wait(pe, at(i) - 1)
                            b_gate.begin(pe, at(i))
                        else:
                            b_pre.wait(pe, at(i), 1)
                        for j in range(Q):
                            last = nc.tensor.matmul(gates_b()[:, j, 0:3 * D], hT_b[:, (u * Q + j) * P:(u * Q + j + 1) * P],
                                                    wh[:, :], start=True, stop=True)
                        b_gate.mark(last)
                    return body

                pipeline(pe, NQ, [(3, gates_slots), (2, transpose_slots), (2, tile_sums), (1, gates_nodes(0)),
                                  (0, transpose_nodes(0)), (1, messages), (0, transpose_src),
                                  (1, gates_nodes(1)), (0, transpose_nodes(1))], back=3)


def kernel(x, src, dst, edge_attr_64, edge_type_4, L0_gnn_W_msg_w, L0_gnn_W_msg_b, L0_gnn_W_apply_w,
           L0_gnn_W_apply_b, L1_gnn_W, L1_gnn_b, L1_gnn_w_ih, L1_gnn_w_hh, L1_gnn_b_ih, L1_gnn_b_hh):
    import numpy as np
    import concourse.bacc as bacc
    from concourse.bass_utils import run_bass_kernel_spmd

    slots = P * ET
    pads = slots - E

    def columns(v, pad):
        v = np.concatenate([np.asarray(v), np.asarray(pad, np.int32)])
        return np.ascontiguousarray(v.reshape(ET, P).T)

    dst, src, kind = np.asarray(dst), np.asarray(src), np.asarray(edge_type_4)
    none = np.full(pads, -1, np.int32)
    tail = np.concatenate([np.arange(NB, N, dtype=np.int32), np.zeros(pads - TAIL, np.int32)])
    ea = np.concatenate([np.asarray(edge_attr_64), np.zeros((pads, D), np.float32)])
    arrays = {
        "x": np.asarray(x),
        "edge_attr": np.ascontiguousarray(ea.reshape(ET, P, D).transpose(1, 0, 2).reshape(P, ET * D)),
        "dst_col": columns(dst, none),
        "dst_next": columns(dst[1:], np.full(pads + 1, -1, np.int32)),
        "dst_row": np.concatenate([dst, np.full(pads, -2, np.int32)]).reshape(1, slots),
        "prev_last": np.concatenate([np.full(1, -3, np.int32), dst[P - 1::P][:ET - 1]]).reshape(1, ET),
        "src_col": columns(src, np.zeros(pads, np.int32)),
        "slot_node": columns(dst, tail),
        "type_col": columns(kind, np.zeros(pads, np.int32)),
        "wm_t": np.ascontiguousarray(np.asarray(L0_gnn_W_msg_w).T),
        "bm": np.asarray(L0_gnn_W_msg_b),
        "wa_t": np.ascontiguousarray(np.asarray(L0_gnn_W_apply_w).T),
        "ba": np.asarray(L0_gnn_W_apply_b),
        "wl_t": np.ascontiguousarray(np.asarray(L1_gnn_W).transpose(2, 0, 1).reshape(D, NT * D)),
        "bl": np.asarray(L1_gnn_b),
        "wih_t": np.ascontiguousarray(np.asarray(L1_gnn_w_ih).T),
        "whh_t": np.ascontiguousarray(np.asarray(L1_gnn_w_hh).T),
        "bih": np.asarray(L1_gnn_b_ih),
        "bhh": np.asarray(L1_gnn_b_hh),
    }
    nc = bacc.Bacc("TRN2", target_bir_lowering=False, num_devices=1)
    args = [nc.dram_tensor(f"in_{name}", a.shape, mybir.dt.from_np(a.dtype), kind="ExternalInput").ap()
            for name, a in arrays.items()]
    out = nc.dram_tensor("out", [N, D], F32, kind="ExternalOutput").ap()
    program(nc, *args, out)
    r = run_bass_kernel_spmd(nc, [{f"in_{name}": a for name, a in arrays.items()}], core_ids=[0])
    return r.results[0]["out"]
```

```python
import concourse.bass as bass
from concourse import mybir
from contextlib import ExitStack

F32 = mybir.dt.float32
I32 = mybir.dt.int32
BF16 = mybir.dt.bfloat16
U8 = mybir.dt.uint8
ALU = mybir.AluOpType
ACT = mybir.ActivationFunctionType
AX = mybir.AxisListType

P = 128
N = 50000
E = 25000
D = 64
NT = 4
STEPS = 5
EPS = 1e-5
ET = -(-E // P)
Q = 4
NQ = ET // Q
R = 7
NR = NQ // R
BT = N // P
NB = P * BT
TAIL = N - NB
G = 6
NG = BT // G
H = 2 * Q
HL = BT - H * (NQ - 1)
CH = 2 * R
EARLY = 4
DR = 5
X_RING = 5
ROWS = NB + P * ET
SKIP = 1000000
TAIL_P = E % P


def flat(ap):
    return ap.rearrange("p a b -> p (a b)")


def pipeline(eng, n, lags, back=2, tail=0):
    deep = max(lag for lag, _ in lags)
    for s in range(deep + back):
        for lag, body in lags:
            if s >= lag:
                body(s - lag)
    with eng.Fori(deep + back, n - tail) as s:
        for lag, body in lags:
            body(s - lag)
    for s in range(n - tail, n + deep):
        for lag, body in lags:
            if s - lag < n:
                body(s - lag)


class Steps:

    def __init__(self, sem, per):
        self.sem, self.per = sem, per

    def begin(self, eng, it):
        self.eng, self.it, self.done = eng, it, 0

    def mark(self, ins):
        self.done += 1
        assert self.done <= self.per
        ins.then_inc(self.sem, 1)

    def link(self, ins):
        self.mark(ins)
        self.eng.wait_ge(self.sem, self.per * self.it + self.done)

    def end(self):
        assert self.done == self.per, (self.done, self.per)

    def wait(self, eng, it, k=None):
        if isinstance(it, int) and it < 0:
            return
        eng.wait_ge(self.sem, self.per * it + (self.per if k is None else k))


def program(nc, x, edge_attr, dst_col, dst_next, dst_row, prev_last, src_col, slot_node, type_col,
            wm_t, bm, wa_t, ba, wl_t, bl, wih_t, whh_t, bih, bhh, out):
    ctx = ExitStack()
    with ctx:
        def sb(name, shape, dt=F32):
            return ctx.enter_context(nc.sbuf_tensor(name, shape, dt))

        def sem(name):
            return ctx.enter_context(nc.semaphore(name))

        node_row = nc.dram_tensor("node_row", [N, 1], I32, kind="Internal").ap()
        h0_tab = nc.dram_tensor("h0_tab", [N, D], F32, kind="Internal").ap()
        x1_tab = nc.dram_tensor("x1_tab", [ROWS, D], F32, kind="Internal").ap()
        state = [nc.dram_tensor(f"state{k}", [ROWS, D], F32, kind="Internal").ap() for k in range(STEPS)]

        def node_part(tab):
            return tab[0:NB, :].rearrange("(p t) d -> p (t d)", t=BT)

        def slot_part(tab):
            return tab[NB:ROWS, :].rearrange("(p t) d -> p (t d)", t=ET)

        ident = sb("ident", [P, P])
        eps = sb("eps", [P, 1])
        wm = sb("wm", [P, D])
        bm_all = sb("bm_all", [P, D])
        wa1 = sb("wa1", [P, D])
        wa2 = sb("wa2", [P, D + 1])
        wl = sb("wl", [P, NT * D])
        wg = sb("wg", [P, 4 * D])
        wh = sb("wh", [P, 3 * D])
        bin_all = sb("bin_all", [P, D])
        h_slot = sb("h_slot", [P, ET * D])
        brow_i = h_slot[0:D + 1, 0:4 * D]
        brow_h = h_slot[0:D + 1, 4 * D:8 * D]
        b3f = h_slot[0:3, 8 * D:16 * D].rearrange("p (a b) -> p a b", b=4 * D)
        b3acc = h_slot[0:3, 16 * D:24 * D].rearrange("p (a b) -> p a b", b=4 * D)
        b3part = h_slot[0:3, 24 * D:28 * D].bitcast(BF16).rearrange("p (a b) -> p a b", b=4 * D)
        last_f = h_slot[:, 32 * D:32 * D + ET]
        dstn_i = h_slot[:, 36 * D:36 * D + ET].bitcast(I32)
        bias3 = sb("bias3", [P, 4 * D], BF16)
        ones3 = sb("ones3", [P, P], BF16)
        dst_i = sb("dst_i", [P, ET], I32)
        src_i = sb("src_i", [P, ET], I32)
        slot_i = sb("slot_i", [P, ET], I32)
        type_i = sb("type_i", [P, ET], I32)
        prev_i = sb("prev_i", [D + 1, ET], I32)
        dst_f = sb("dst_f", [P, ET])
        prev_f = sb("prev_f", [D + 1, ET])
        own_idx = sb("own_idx", [P, ET], I32)
        slot_row = sb("slot_row", [P, ET], I32)
        node_ids = sb("node_ids", [P, BT], I32)
        tail_rows = sb("tail_rows", [TAIL, 1], I32)
        tail_now = sb("tail_now", [P, 1], I32)
        tail_f = sb("tail_f", [P, 4])
        cand = sb("cand", [P, 1], I32)
        src_row = sb("src_row", [P, ET], I32)
        tmask = sb("tmask", [P, 3, ET], I32)
        tm_st = sb("tm_st", [P, 3, Q], I32)
        same = sb("same", [P, ET * P], BF16)
        cont = sb("cont", [D + 1, ET * P], U8)
        idx_st = sb("idx_st", [P, 2, R * Q], I32)
        val_st = sb("val_st", [P, R * Q], I32)
        rings = sb("rings", [P, 2 * R * Q * D])
        ring, xring = rings[:, 0:R * Q * D], rings[:, R * Q * D:2 * R * Q * D]
        drow = h_slot[:, 40 * D:40 * D + DR * CH * P].bitcast(I32)
        nring = sb("nring", [P, 4 * H * D])
        stage = sb("stage", [P, G, D])
        stage2 = sb("stage2", [P, Q, D])
        hT = sb("hT", [P, G * P])
        m = sb("m", [P, Q, D])
        mres = sb("mres", [P, Q, D])
        parts = sb("parts", [P, 3, Q, D + 1], BF16)
        stack = sb("stack", [P, Q * P])
        rz = sb("rz", [P, Q, 2 * D])
        pre = sb("pre", [P, Q, D])
        cn = sb("cn", [P, Q, D])
        blend = sb("blend", [P, Q, D])
        blend_b = sb("blend_b", [P, H, D])
        hnew = sb("hnew", [P, H, D])
        fin = sb("fin", [P, H, D])
        rdeg = sb("rdeg", [P, 2, Q])
        ln_s = sb("ln_s", [P, 2, 5, G])
        shared = sb("shared", [P, 88 * D])

        def carve(at, width):
            return shared[:, at * D:(at + width) * D]

        def tiles(ap, n):
            return ap.rearrange("p (n d) -> p n d", n=n)

        he, heT, aggT = tiles(carve(0, 2 * Q), Q), carve(8, 2 * Q), carve(16, 2 * Q)
        x1b = tiles(carve(24, G), G)
        ln_c = carve(30, 2 * G).rearrange("p (u a b) -> p u a b", u=2, b=D)
        ln_q = carve(42, 2 * G).rearrange("p (u a b) -> p u a b", u=2, b=D)
        hT_b, stage_b = carve(0, 4 * Q), tiles(carve(16, H), H)
        rz_b, pre_b, cn_b = tiles(carve(24, 2 * H), H), tiles(carve(40, H), H), tiles(carve(48, H), H)
        xring_b = carve(56, 4 * H)
        ps = ctx.enter_context(nc.psum_tensor("ps", [P, 8, 512], F32))
        psf = ps[:, :, :].rearrange("p a b -> p (a b)")

        s_const = sem("s_const")
        s_setup = sem("s_setup")
        s_prep = sem("s_prep")
        s_tail = sem("s_tail")
        s_tailc = sem("s_tailc")
        s_minit = sem("s_minit")
        s_mset = sem("s_mset")
        s_mget = sem("s_mget")
        s_pool = sem("s_pool")
        s_tailnow = sem("s_tailnow")
        s_drow0 = sem("s_drow0")
        s_drow = sem("s_drow")
        s_ones = sem("s_ones")
        s_same = sem("s_same")
        b0_ld, b0_sth, b0_stx, b0_sts = sem("b0_ld"), sem("b0_sth"), sem("b0_stx"), sem("b0_sts")
        b0_va, b0_vb, b0_vc, b0_vd = Steps(sem("b0_va"), 3), Steps(sem("b0_vb"), 3), Steps(sem("b0_vc"), 4), Steps(sem("b0_vd"), 3)
        b0_sq0, b0_rt0, b0_ev, b0_sq1, b0_rt1 = (Steps(sem(f"b0_{n}"), c) for n, c in
                                                 (("sq0", 1), ("rt0", 1), ("ev", 2), ("sq1", 1), ("rt1", 1)))
        b0_tr, b0_mm = Steps(sem("b0_tr"), 1), Steps(sem("b0_mm"), 1)
        a0_ea, a0_stx, a0_sts = sem("a0_ea"), sem("a0_stx"), sem("a0_sts")
        a0_g = [sem(f"a0_g{q}") for q in range(R)]
        a0_quad = sem("a0_quad")
        a0_he, a0_ev, a0_cut, a0_evh = Steps(sem("a0_he"), 2), Steps(sem("a0_ev"), 1), Steps(sem("a0_cut"), 2), Steps(sem("a0_evh"), 1)
        a0_sq0, a0_rt0, a0_sq1, a0_rt1 = (Steps(sem(f"a0_{n}"), 1) for n in ("sq0", "rt0", "sq1", "rt1"))
        a0_msg, a0_va, a0_vb, a0_sum, a0_upd, a0_vd = (Steps(sem(f"a0_{n}"), c) for n, c in
                                                       (("msg", 3), ("va", 3), ("vb", 3), ("sum", Q), ("upd", 8), ("vd", 3)))
        a0_p0, a0_p1, a0_p2, a0_p3 = (Steps(sem(f"a0_p{j}"), n) for j, n in enumerate((1, 1, 2, 1)))
        b_ld, b_ld1, b_st = sem("b_ld"), sem("b_ld1"), sem("b_st")
        b_stg, b_ev, b_sig, b_tanh = Steps(sem("b_stg"), 1), Steps(sem("b_ev"), 2), Steps(sem("b_sig"), 2), Steps(sem("b_tanh"), 1)
        b_pre, b_new = Steps(sem("b_pre"), 4), Steps(sem("b_new"), 3)
        b_tr, b_gate = Steps(sem("b_tr"), 2), Steps(sem("b_gate"), 2)
        b_fin = sem("b_fin")
        a_g = [sem(f"a_g{q}") for q in range(R)]
        a_quad, a_st = sem("a_quad"), sem("a_st")
        a_stg, a_ev, a_m0, a_cut, a_stgh, a_evh, a_sig, a_tanh = (Steps(sem(f"a_{n}"), c) for n, c in (
            ("stg", 1), ("ev", 1), ("m0", 1), ("cut", 2), ("stgh", 1), ("evh", 1), ("sig", 1), ("tanh", 1)))
        a_msg, a_res, a_sum, a_pre, a_new = (Steps(sem(f"a_{n}"), c) for n, c in (
            ("msg", NT), ("res", 2), ("sum", Q), ("pre", 2), ("new", 3)))
        a_tr, a_trh, a_mm, a_agg, a_gate = (Steps(sem(f"a_{n}"), 1) for n in ("tr", "trh", "mm", "agg", "gate"))
        f_ld = sem("f_ld")
        f_v = sem("f_v")
        f_sc = [sem(f"f_sc{q}") for q in range(R)]

        s_held = sem("s_held")

        def hold(eng):
            eng.sem_inc(s_held, 1)

        def gates_a():
            return ps[:, 4:6, :].rearrange("p a (t c) -> p (a t) c", c=4 * D)

        def gates_b():
            return ps[:, 6:8, :].rearrange("p a (t c) -> p (a t) c", c=4 * D)

        block = ctx.enter_context(nc.Block())
        consts = []

        @block.sync
        def _(sp):
            def load(dst, src):
                consts.append(1)
                sp.dma_start(dst, src).then_inc(s_const, 16)

            load(wm[:, :], wm_t)
            load(bm_all[:, :], bm.rearrange("(a d) -> a d", a=1).to_broadcast([P, D]))
            load(bin_all[:, :], bih[2 * D:3 * D].rearrange("(a d) -> a d", a=1).to_broadcast([P, D]))
            load(dst_i[:, :], dst_col)
            load(dstn_i[:, :], dst_next)
            load(src_i[:, :], src_col)
            load(slot_i[:, :], slot_node)
            load(type_i[:, :], type_col)
            load(prev_i[:, :], prev_last.to_broadcast([D + 1, ET]))
            sp.wait_ge(s_setup, 17)
            load(wa1[0:D, :], wa_t[0:D, :])
            load(wa1[D:D + 1, :], ba.rearrange("(a d) -> a d", a=1))
            load(wa2[0:D, 0:D], wa_t[D:2 * D, :])
            load(wl[0:D, :], wl_t)
            load(wl[D:D + 1, :], bl.rearrange("(a t) d -> a (t d)", a=1))
            load(wg[0:D, 0:2 * D], wih_t[:, 0:2 * D])
            load(wg[0:D, 3 * D:4 * D], wih_t[:, 2 * D:3 * D])
            load(wg[D:2 * D, 0:3 * D], whh_t)
            load(wh[0:D, 0:3 * D], whh_t)
            row = lambda v: v.rearrange("(a d) -> a d", a=1)
            load(brow_i[D:D + 1, 0:2 * D], row(bih[0:2 * D]))
            load(brow_i[D:D + 1, 3 * D:4 * D], row(bih[2 * D:3 * D]))
            load(brow_h[D:D + 1, 0:3 * D], row(bhh))
            load(b3f[:, 0, 0:2 * D], row(bih[0:2 * D]).to_broadcast([3, 2 * D]))
            load(b3f[:, 0, 3 * D:4 * D], row(bih[2 * D:3 * D]).to_broadcast([3, D]))
            load(b3f[:, 1, 0:3 * D], row(bhh).to_broadcast([3, 3 * D]))

            sp.wait_ge(s_setup, 20)
            sp.dma_start(node_row[0:NB, :].rearrange("(p t) a -> p (t a)", t=BT), node_ids[:, :]).then_inc(s_minit, 16)
            sp.dma_start(node_row[NB:N, :], tail_rows[:, :]).then_inc(s_minit, 16)
            sp.dma_start(x1b[0:TAIL, 0, :], x[NB:N, :]).then_inc(s_tail, 16)
            sp.wait_ge(s_prep, 7)
            sp.dma_start(h0_tab[NB:N, :], hnew[0:TAIL, 0, :]).then_inc(s_tail, 16)
            sp.wait_ge(s_tail, 32)

            W = G * D
            x_v, h0_v = node_part(x), node_part(h0_tab)

            C = CH * P

            def rows_in(r):
                return sp.dma_start(drow[:, bass.ds((r % DR) * C, C)],
                                    dst_row[:, bass.ds(r * C, C)].to_broadcast([P, C]))

            def b0_load(i):
                b0_vc.wait(sp, i - X_RING, 1)
                sp.dma_start(nring[:, bass.ds((i % X_RING) * W, W)], x_v[:, bass.ds(i * W, W)]).then_inc(b0_ld, 16)
                if isinstance(i, int) and X_RING <= i < X_RING + DR:
                    rows_in(i - X_RING).then_inc(s_drow0, 16)

            def b0_store_h0(i):
                b0_vb.wait(sp, i)
                sp.dma_start(h0_v[:, bass.ds(i * W, W)], flat(stage[:, :, :])).then_inc(b0_sth, 16)

            def b0_store_x1(i):
                b0_vc.wait(sp, i, 1)
                sp.dma_start(node_part(x1_tab)[:, bass.ds(i * W, W)], flat(x1b[:, :, :])).then_inc(b0_stx, 16)

            def b0_store_state(i):
                b0_vd.wait(sp, i)
                sp.dma_start(node_part(state[0])[:, bass.ds(i * W, W)], flat(hnew[:, 0:G, :])).then_inc(b0_sts, 16)

            def b0_arrived(s, n):
                if not isinstance(n, int) or n > 0:
                    sp.wait_ge(s, 16 * n)
                    hold(sp)

            pipeline(sp, NG, [(0, lambda i: b0_arrived(b0_ld, i)), (0, b0_load),
                              (2, lambda i: b0_arrived(b0_sth, i)), (2, b0_store_h0),
                              (4, lambda i: b0_arrived(b0_stx, i)), (4, b0_store_x1),
                              (5, lambda i: b0_arrived(b0_sts, i)), (5, b0_store_state)], back=7)

            with sp.Fori(DR, ET // CH) as r:
                sp.wait_ge(s_same, 2 * (r - DR) + 2)
                hold(sp)
                rows_in(r).then_inc(s_drow, 16)
                sp.wait_ge(s_drow, 16 * (r - DR + 1))
                hold(sp)

            V = Q * D

            def a0_load(i):
                b0_arrived(a0_ea, i)
                a0_he.wait(sp, i - 4)
                sp.dma_start(nring[:, bass.ds((i % 4) * V, V)], edge_attr[:, bass.ds(i * V, V)]).then_inc(a0_ea, 16)

            def a0_store_x1(i):
                a0_upd.wait(sp, i, 5)
                sp.dma_start(slot_part(x1_tab)[:, bass.ds(i * V, V)], flat(x1b[:, 0:Q, :])).then_inc(a0_stx, 16)
                sp.wait_ge(a0_stx, 16 * (i + 1))
                hold(sp)

            def a0_store(i):
                a0_vd.wait(sp, i)
                sp.dma_start(slot_part(state[0])[:, bass.ds(i * V, V)], h_slot[:, bass.ds(i * V, V)]).then_inc(a0_sts, 16)
                sp.wait_ge(a0_sts, 16 * (i + 1))
                hold(sp)

            sp.wait_ge(b0_sth, 16 * NG)
            b0_vd.wait(sp, NG - 1)
            pipeline(sp, NQ, [(0, a0_load), (4, a0_store_x1), (5, a0_store)], back=5)

            for k in range(STEPS):
                last = k == STEPS - 1
                src_t = node_part(state[k])
                dst_t = node_part(out if last else state[k + 1])
                if k == 0:
                    a0_he.wait(sp, NQ - 1)
                    sp.wait_ge(b0_sts, 16 * NG)
                    sp.wait_ge(b0_stx, 16 * NG)

                def cols(i):
                    w = (HL if isinstance(i, int) and i == NQ - 1 else H) * D
                    return bass.ds(i * H * D, w), w

                def b_load(i):
                    it = i + k * NQ
                    b_new.wait(sp, it - 4)
                    hold(sp)
                    c, w = cols(i)
                    sp.dma_start(nring[:, bass.ds((it % 4) * H * D, w)], src_t[:, c]).then_inc(b_ld, 16)
                    if last:
                        if not isinstance(i, int) or i >= 4:
                            sp.wait_ge(b_fin, i - 3)
                        sp.dma_start(xring_b[:, bass.ds((it % 4) * H * D, w)], node_part(x1_tab)[:, c]).then_inc(b_ld1, 16)
                        sp.wait_ge(b_ld1, 16 * (i + 1))
                    sp.wait_ge(b_ld, 16 * (it + 1))
                    hold(sp)

                def b_store(i):
                    it = i + k * NQ
                    if last:
                        sp.wait_ge(b_fin, i + 1)
                    else:
                        b_new.wait(sp, it)
                    c, w = cols(i)
                    sp.dma_start(dst_t[:, c], flat((fin if last else hnew)[:, :, :])[:, 0:w]).then_inc(b_st, 16)
                    sp.wait_ge(b_st, 16 * (it + 1))
                    hold(sp)

                def a_store(i):
                    it = i + k * NQ
                    a_new.wait(sp, it)
                    sp.dma_start(slot_part(state[k + 1])[:, bass.ds(i * V, V)],
                                 h_slot[:, bass.ds(i * V, V)]).then_inc(a_st, 16)
                    sp.wait_ge(a_st, 16 * (it + 1))
                    hold(sp)

                pipeline(sp, NQ, [(0, b_load), (3, b_store)] + ([] if last else [(5, a_store)]), back=6, tail=1)

            def f_load(i):
                if not isinstance(i, int):
                    sp.wait_ge(f_v, i - 3)
                sp.dma_start(nring[:, bass.ds((i % 4) * V, V)], slot_part(x1_tab)[:, bass.ds(i * V, V)]).then_inc(f_ld, 16)
                sp.wait_ge(f_ld, 16 * (i + 1))
                hold(sp)

            for i in range(4):
                f_load(i)
            with sp.Fori(4, NQ) as i:
                f_load(i)
            for q in range(R):
                sp.wait_ge(f_sc[q], 16 * Q * NR)

        @block.gpsimd
        def _(pool):
            setup = [0]

            def mark(ins):
                setup[0] += 1
                ins.then_inc(s_setup, 1)
                pool.wait_ge(s_setup, setup[0])

            mark(pool.memset(ident[:, :], 0.0))
            mark(pool.memset(eps[:, :], EPS))
            mark(pool.memset(wa2[:, :], 0.0))
            mark(pool.memset(wg[:, :], 0.0))
            mark(pool.memset(wh[:, :], 0.0))
            mark(pool.memset(wa1[:, :], 0.0))
            mark(pool.memset(wl[:, :], 0.0))
            mark(pool.memset(bias3[:, :], 0.0))
            mark(pool.memset(hT[D:2 * D, :], 0.0))
            mark(pool.memset(brow_i[:, :], 0.0))
            mark(pool.memset(brow_h[:, :], 0.0))
            mark(pool.memset(b3f[:, :, :], 0.0))
            mark(pool.memset(ones3[:, :], 0.0))
            mark(pool.memset(ones3[0:3, :], 1.0))
            mark(pool.memset(hT[D:D + 1, :], 1.0))
            mark(pool.memset(parts[:, :, :, :], 0.0))
            mark(pool.memset(tail_now[:, :], 0))
            mark(pool.iota(slot_row[:, :], pattern=[[1, ET]], base=NB, channel_multiplier=ET))
            mark(pool.iota(node_ids[:, :], pattern=[[1, BT]], base=0, channel_multiplier=BT))
            mark(pool.iota(tail_rows[:, :], pattern=[[0, 1]], base=NB + TAIL_P * ET + ET - 1, channel_multiplier=ET))
            mark(pool.iota(cand[:, :], pattern=[[0, 1]], base=NB - TAIL_P, channel_multiplier=1))
            mark(pool.affine_select(out=ident[:, :], in_=ident[:, :], compare_op=ALU.not_equal, fill=1.0,
                                    base=0, pattern=[[-1, P]], channel_multiplier=1))
            mark(pool.memset(wa2[D:D + 1, D:D + 1], 1.0))
            mark(pool.memset(parts[:, 0, :, D:D + 1], 1.0))

            T = R * Q
            pool.wait_ge(s_prep, 9)
            pool.wait_ge(s_minit, 32)

            def step(ins):
                ins.then_inc(s_pool, 1)

            with pool.Fori(0, NR) as r:
                step(pool.tensor_copy(idx_st[:, 0, :], own_idx[:, bass.ds(r * T, T)]))
                step(pool.tensor_copy(val_st[:, :], slot_row[:, bass.ds(r * T, T)]))
                pool.wait_ge(s_pool, 2 * r + 2)
                hold(pool)
                for t in range(T):
                    pool.indirect_dma_start(out=node_row[:, :],
                                            out_offset=bass.IndirectOffsetOnAxis(ap=idx_st[:, 0, t:t + 1], axis=0),
                                            in_=val_st[:, t:t + 1], in_offset=None,
                                            bounds_check=N - 1, oob_is_err=False).then_inc(s_mset, 16)
                pool.wait_ge(s_mset, 16 * T * (r + 1))
                hold(pool)
            def rows_of_sources(r, done):
                step(pool.tensor_copy(idx_st[:, 0, :], src_i[:, bass.ds(r * T, T)]))
                pool.wait_ge(s_pool, done + 1)
                hold(pool)
                for t in range(T):
                    pool.indirect_dma_start(out=val_st[:, t:t + 1], out_offset=None, in_=node_row[:, :],
                                            in_offset=bass.IndirectOffsetOnAxis(ap=idx_st[:, 0, t:t + 1], axis=0)
                                            ).then_inc(s_mget, 16)
                pool.wait_ge(s_mget, 16 * T * (r + 1))
                step(pool.tensor_copy(src_row[:, bass.ds(r * T, T)], val_st[:, :]))
                pool.wait_ge(s_pool, done + 2)
                hold(pool)

            with pool.Fori(0, EARLY) as r:
                rows_of_sources(r, 2 * NR + 2 * r)
            pool.dma_start(tail_now[TAIL_P:TAIL_P + TAIL, :], node_row[NB:N, :]).then_inc(s_tailnow, 16)

            pool.wait_ge(b0_sth, 16 * NG)
            pool.wait_ge(s_tail, 32)
            done = 2 * NR + 2 * EARLY

            def a0_quad_in(r, q):
                i = r * R + q
                for j in range(Q):
                    t = q * Q + j
                    pool.indirect_dma_start(out=xring[:, t * D:(t + 1) * D], out_offset=None, in_=x[:, :],
                                            in_offset=bass.IndirectOffsetOnAxis(ap=idx_st[:, 0, t:t + 1], axis=0)
                                            ).then_inc(a0_g[q], 16)
                    pool.indirect_dma_start(out=ring[:, t * D:(t + 1) * D], out_offset=None, in_=h0_tab[:, :],
                                            in_offset=bass.IndirectOffsetOnAxis(ap=idx_st[:, 1, t:t + 1], axis=0)
                                            ).then_inc(a0_g[q], 16)

            def forward(sems, q, r, per, quad_sem):
                pool.wait_ge(sems[q], per * (r + 1))
                pool.sem_inc(quad_sem, 1)

            def a0_round(r):
                step(pool.tensor_copy(idx_st[:, 0, :], slot_i[:, bass.ds(r * T, T)]))
                step(pool.tensor_copy(idx_st[:, 1, :], src_i[:, bass.ds(r * T, T)]))
                pool.wait_ge(s_pool, done + 2 * r + 2)
                hold(pool)
                for q in range(R):
                    if not isinstance(r, int):
                        a0_upd.wait(pool, (r - 1) * R + q)
                        hold(pool)
                    a0_quad_in(r, q)
                    if q:
                        forward(a0_g, q - 1, r, 32 * Q, a0_quad)
                forward(a0_g, R - 1, r, 32 * Q, a0_quad)

            a0_round(0)
            with pool.Fori(1, NR) as r:
                a0_round(r)
            done += 2 * NR

            pool.wait_ge(b0_sts, 16 * NG)
            for k in range(STEPS):
                if k == 0:
                    pool.wait_ge(a0_sts, 16 * NQ)
                else:
                    pool.wait_ge(a_st, 16 * NQ * k)
                    pool.wait_ge(b_st, 16 * NQ * k)

                def a_round(r, done):
                    step(pool.tensor_copy(idx_st[:, 0, :], src_row[:, bass.ds(r * T, T)]))
                    pool.wait_ge(s_pool, done + 1)
                    for q in range(R):
                        it = r * R + q + k * NQ
                        a_stg.wait(pool, it - R)
                        hold(pool)
                        for j in range(Q):
                            t = q * Q + j
                            pool.indirect_dma_start(out=ring[:, t * D:(t + 1) * D], out_offset=None, in_=state[k][:, :],
                                                    in_offset=bass.IndirectOffsetOnAxis(ap=idx_st[:, 0, t:t + 1], axis=0)
                                                    ).then_inc(a_g[q], 16)
                        if q:
                            forward(a_g, q - 1, r + k * NR, 16 * Q, a_quad)
                    forward(a_g, R - 1, r + k * NR, 16 * Q, a_quad)

                first = 1
                if k == 0:
                    first = NR - EARLY
                    for r in range(first):
                        a_round(r, done + 3 * r)
                        rows_of_sources(r + EARLY, done + 3 * r + 1)
                    done += 2 * first
                else:
                    a_round(0, done)
                with pool.Fori(first, NR) as r:
                    a_round(r, done + r)
                done += NR

            pool.wait_ge(b_st, 16 * NQ * STEPS)

            def f_round(r):
                step(pool.tensor_copy(idx_st[:, 0, :], own_idx[:, bass.ds(r * T, T)]))
                pool.wait_ge(s_pool, done + r + 1)
                for q in range(R):
                    pool.wait_ge(f_v, r * R + q + 1)
                    hold(pool)
                    for j in range(Q):
                        t = q * Q + j
                        pool.indirect_dma_start(out=out[:, :],
                                                out_offset=bass.IndirectOffsetOnAxis(ap=idx_st[:, 0, t:t + 1], axis=0),
                                                in_=ring[:, t * D:(t + 1) * D], in_offset=None,
                                                bounds_check=N - 1, oob_is_err=False).then_inc(f_sc[q], 16)

            f_round(0)
            with pool.Fori(1, NR) as r:
                for q in range(R):
                    pool.wait_ge(f_sc[q], 16 * Q * r)
                f_round(r)
            for q in range(R):
                pool.wait_ge(f_sc[q], 16 * Q * NR)

        @block.scalar
        def _(act):
            def copy(out_, in_):
                return nc.scalar.activation(out_, in_, ACT.Copy)

            def root(u, n, p=P):
                return nc.scalar.activation(ln_s[0:p, u, 3, 0:n], ln_s[0:p, u, 2, 0:n], ACT.Sqrt,
                                            bias=eps[0:p, :], scale=1.0 / D)

            act.wait_ge(s_setup, 24)
            act.wait_ge(s_prep, 5)
            root(0, 1, TAIL).then_inc(s_tailc, 1)

            def square(u, n):
                return nc.scalar.activation(ln_q[:, u, 0:n, :], ln_c[:, u, 0:n, :], ACT.Square)

            def one(steps, it, ins):
                steps.begin(act, it)
                steps.mark(ins())
                steps.end()

            def b0_root1(i):
                b0_vd.wait(act, i, 1)
                one(b0_rt1, i, lambda: root(1, G))

            def b0_root0(i):
                b0_vb.wait(act, i, 1)
                one(b0_rt0, i, lambda: root(0, G))

            def b0_copy(i):
                b0_tr.wait(act, i)
                b0_mm.wait(act, i - 1)
                b0_ev.begin(act, i)
                b0_ev.mark(copy(hT[0:D, 0:3 * P], ps[0:D, 0, 0:3 * P]))
                b0_ev.mark(copy(hT[0:D, 3 * P:6 * P], ps[0:D, 1, 0:3 * P]))
                b0_ev.end()

            def b0_square1(i):
                b0_vc.wait(act, i)
                b0_vd.wait(act, i - 1, 1)
                one(b0_sq1, i, lambda: square(1, G))

            def b0_square0(i):
                b0_va.wait(act, i)
                b0_vb.wait(act, i - 1, 1)
                one(b0_sq0, i, lambda: square(0, G))

            pipeline(act, NG, [(4, b0_root1), (1, b0_root0), (2, b0_copy), (3, b0_square1), (0, b0_square0)])

            b0_vd.wait(act, NG - 1)
            act.wait_ge(b0_stx, 16 * NG)
            V = Q * D

            def a0_he_in(i):
                a0_he.begin(act, i)
                act.wait_ge(a0_quad, i + 1)
                a0_p0.wait(act, i - 1)
                a0_he.mark(copy(he[:, :, 0:D], tiles(ring[:, bass.ds((i % R) * V, V)], Q)))
                act.wait_ge(a0_ea, 16 * (i + 1))
                a0_he.mark(copy(he[:, :, D:2 * D], tiles(nring[:, bass.ds((i % 4) * V, V)], Q)))
                a0_he.end()

            def a0_copy(i):
                a0_p0.wait(act, i)
                a0_p1.wait(act, i - 1)
                one(a0_ev, i, lambda: copy(heT, ps[:, 0, :]))

            def a0_hi(i):
                a0_msg.wait(act, i, 1)
                a0_p2.wait(act, i - 1)
                a0_cut.begin(act, i)
                a0_cut.mark(copy(parts[:, 0, :, 0:D], m[:, :, :]))

            def a0_mid(i):
                a0_msg.wait(act, i, 2)
                a0_cut.mark(copy(parts[:, 1, :, 0:D], mres[:, :, :]))
                a0_cut.end()

            def a0_root0(i):
                a0_vb.wait(act, i, 1)
                one(a0_rt0, i, lambda: root(0, Q))

            def a0_copy_h(i):
                a0_p2.wait(act, i, 1)
                a0_p3.wait(act, i - 1)
                one(a0_evh, i, lambda: copy(hT[0:D, 0:Q * P], ps[0:D, 1, :]))

            def a0_root1(i):
                a0_vd.wait(act, i, 1)
                one(a0_rt1, i, lambda: root(1, Q))

            def a0_square0(i):
                a0_va.wait(act, i)
                a0_vb.wait(act, i - 1, 1)
                one(a0_sq0, i, lambda: square(0, Q))

            def a0_square1(i):
                a0_upd.wait(act, i)
                a0_vd.wait(act, i - 1, 1)
                one(a0_sq1, i, lambda: square(1, Q))

            pipeline(act, NQ, [(0, a0_he_in), (1, a0_hi), (4, a0_root1), (1, a0_root0), (1, a0_mid), (0, a0_copy),
                               (0, a0_square0), (2, a0_copy_h), (3, a0_square1)])

            a0_vd.wait(act, NQ - 1)
            for k in range(STEPS):
                at = lambda i: i + k * NQ

                def stage_nodes(i):
                    act.wait_ge(b_ld, 16 * (at(i) + 1))
                    b_tr.wait(act, at(i) - 1)
                    one(b_stg, at(i), lambda: copy(flat(stage_b), nring[:, bass.ds((at(i) % 4) * H * D, H * D)]))

                def copy_nodes(u):
                    def body(i):
                        b_tr.wait(act, at(i), u + 1)
                        b_gate.wait(act, at(i) - 1, u + 1)
                        if u == 0:
                            b_ev.begin(act, at(i))
                        b_ev.mark(copy(hT_b[0:D, u * Q * P:(u + 1) * Q * P], ps[0:D, 0, :]))
                    return body

                def sigmoid_nodes(u):
                    def body(i):
                        b_gate.wait(act, at(i), u + 1)
                        if u == 0:
                            b_sig.begin(act, at(i))
                            b_new.wait(act, at(i) - 1, 2)
                        b_sig.mark(nc.scalar.activation(rz_b[:, u * Q:(u + 1) * Q, :], gates_b()[:, :, 0:2 * D], ACT.Sigmoid))
                    return body

                def tanh_nodes(i):
                    b_pre.wait(act, at(i))
                    b_new.wait(act, at(i) - 1)
                    one(b_tanh, at(i), lambda: nc.scalar.activation(flat(cn_b), flat(pre_b), ACT.Tanh))

                def stage_src(i):
                    act.wait_ge(a_quad, at(i) + 1)
                    a_tr.wait(act, at(i) - 1)
                    one(a_stg, at(i), lambda: copy(flat(stage[:, 0:Q, :]), ring[:, bass.ds((i % R) * V, V)]))

                def copy_src(i):
                    a_tr.wait(act, at(i))
                    a_mm.wait(act, at(i) - 1)
                    one(a_ev, at(i), lambda: copy(hT[0:D, 0:Q * P], ps[0:D, 0, :]))

                def type0(i):
                    a_mm.wait(act, at(i))
                    a_res.wait(act, at(i) - 1)
                    one(a_m0, at(i), lambda: copy(m[:, :, :], psf[:, 512:1536].rearrange("p (a t d) -> p a t d", t=NT, d=D)[:, :, 0, :]))

                def hi(i):
                    a_msg.wait(act, at(i))
                    a_agg.wait(act, at(i) - 1)
                    a_cut.begin(act, at(i))
                    a_cut.mark(copy(parts[:, 0, :, 0:D], m[:, :, :]))

                def mid(i):
                    a_res.wait(act, at(i), 1)
                    a_cut.mark(copy(parts[:, 1, :, 0:D], mres[:, :, :]))
                    a_cut.end()

                def stage_slots(i):
                    a_trh.wait(act, at(i) - 1)
                    one(a_stgh, at(i), lambda: copy(flat(stage2[:, :, :]), h_slot[:, bass.ds(i * V, V)]))

                def copy_slots(i):
                    a_trh.wait(act, at(i))
                    a_gate.wait(act, at(i) - 1)
                    one(a_evh, at(i), lambda: copy(stack[D:2 * D, :], ps[0:D, 0, :]))

                def sigmoid_slots(i):
                    a_gate.wait(act, at(i))
                    a_new.wait(act, at(i) - 1)
                    one(a_sig, at(i), lambda: nc.scalar.activation(rz[:, :, :], gates_a()[:, :, 0:2 * D], ACT.Sigmoid))

                def tanh_slots(i):
                    a_pre.wait(act, at(i))
                    one(a_tanh, at(i), lambda: nc.scalar.activation(flat(cn[:, :, :]), flat(pre[:, :, :]), ACT.Tanh))

                pipeline(act, NQ, [(2, stage_slots), (2, tanh_nodes), (2, hi), (0, stage_nodes), (2, copy_slots), (2, mid), (3, sigmoid_slots),
                                   (1, sigmoid_nodes(0)), (0, copy_nodes(0)), (0, stage_src), (3, tanh_slots), (1, type0),
                                   (0, copy_src), (1, sigmoid_nodes(1)), (0, copy_nodes(1))])

        @block.vector
        def _(dve):
            count = [0]

            def link(ins):
                count[0] += 1
                ins.then_inc(s_prep, 1)
                dve.wait_ge(s_prep, count[0])

            def ln_head(st, u, src, n, p=P):
                wide = lambda a: a.rearrange("p (n o) -> p n o", o=1).to_broadcast([p, n, D])
                st(nc.vector.tensor_reduce(ln_s[0:p, u, 0, 0:n], src, axis=AX.X, op=ALU.add))
                st(nc.vector.tensor_scalar(ln_s[0:p, u, 1, 0:n], ln_s[0:p, u, 0, 0:n], -1.0 / D, None, ALU.mult))
                st(nc.vector.tensor_tensor(ln_c[0:p, u, 0:n, :], src, wide(ln_s[0:p, u, 1, 0:n]), ALU.add))
                st(nc.vector.tensor_tensor(ln_q[0:p, u, 0:n, :], ln_c[0:p, u, 0:n, :], ln_c[0:p, u, 0:n, :], ALU.mult))

            def ln_sum(u, n, p=P):
                return nc.vector.tensor_reduce(ln_s[0:p, u, 2, 0:n], ln_q[0:p, u, 0:n, :], axis=AX.X, op=ALU.add)

            def ln_inv(u, n, p=P):
                return nc.vector.reciprocal(ln_s[0:p, u, 4, 0:n], ln_s[0:p, u, 3, 0:n])

            def ln_out(u, dst, n, p=P):
                wide = ln_s[0:p, u, 4, 0:n].rearrange("p (n o) -> p n o", o=1).to_broadcast([p, n, D])
                return nc.vector.scalar_tensor_tensor(dst, ln_c[0:p, u, 0:n, :], 0.0, wide, ALU.max, ALU.mult)

            dve.wait_ge(s_tail, 16)
            ln_head(link, 0, x1b[0:TAIL, 0:1, :], 1, TAIL)
            link(ln_sum(0, 1, TAIL))
            dve.wait_ge(s_tailc, 1)
            link(ln_inv(0, 1, TAIL))
            link(ln_out(0, hnew[0:TAIL, 0:1, :], 1, TAIL))
            dve.wait_ge(s_const, 16 * len(consts))
            link(nc.vector.tensor_tensor(last_f[:, :], dst_i[:, :], dstn_i[:, :], ALU.is_equal))
            link(nc.vector.scalar_tensor_tensor(own_idx[:, :], last_f[:, :], float(SKIP), dst_i[:, :], ALU.mult, ALU.add))
            link(nc.vector.tensor_copy(dst_f[:, :], dst_i[:, :]))
            link(nc.vector.tensor_copy(prev_f[:, :], prev_i[:, :]))
            for t in range(3):
                link(nc.vector.tensor_scalar(tmask[:, t, :], type_i[:, :], float(t + 1), None, ALU.is_equal))
            dve.wait_ge(s_setup, 24)
            link(nc.vector.tensor_tensor(wh[D:D + 1, :], brow_i[D:D + 1, 0:3 * D], brow_h[D:D + 1, 0:3 * D], ALU.add))
            link(nc.vector.tensor_tensor(b3acc[:, 0, :], b3f[:, 0, :], b3f[:, 1, :], ALU.add))
            link(nc.vector.tensor_copy(b3part[:, 0, :], b3acc[:, 0, :]))
            link(nc.vector.tensor_tensor(b3acc[:, 1, :], b3acc[:, 0, :], b3part[:, 0, :], ALU.subtract))
            link(nc.vector.tensor_copy(b3part[:, 1, :], b3acc[:, 1, :]))
            link(nc.vector.tensor_tensor(b3acc[:, 0, :], b3acc[:, 1, :], b3part[:, 1, :], ALU.subtract))
            link(nc.vector.tensor_scalar(b3acc[:, 1, :], b3part[:, 0, :], ident[0:3, 0:1], None, ALU.mult))
            link(nc.vector.scalar_tensor_tensor(b3acc[:, 1, :], b3part[:, 1, :], ident[0:3, 1:2], b3acc[:, 1, :], ALU.mult, ALU.add))
            link(nc.vector.scalar_tensor_tensor(bias3[0:3, :], b3acc[:, 0, :], ident[0:3, 2:3], b3acc[:, 1, :], ALU.mult, ALU.add))
            dve.wait_ge(s_tail, 32)

            W = G * D

            def ln_centre(st, u, src, n, step, it):
                if step:
                    st.wait(dve, it, st.done)
                if step == 0:
                    st.mark(nc.vector.tensor_reduce(ln_s[:, u, 0, 0:n], src, axis=AX.X, op=ALU.add))
                elif step == 1:
                    st.mark(nc.vector.tensor_scalar(ln_s[:, u, 1, 0:n], ln_s[:, u, 0, 0:n], -1.0 / D, None, ALU.mult))
                else:
                    wide = ln_s[:, u, 1, 0:n].rearrange("p (n o) -> p n o", o=1).to_broadcast([P, n, D])
                    st.mark(nc.vector.tensor_tensor(ln_c[:, u, 0:n, :], src, wide, ALU.add))

            def xs(i):
                return tiles(nring[:, bass.ds((i % X_RING) * W, W)], G)

            def stored(s, i):
                if not isinstance(i, int) or i > 0:
                    dve.wait_ge(s, 16 * i)

            def b0_sum1(i):
                b0_vd.begin(dve, i)
                b0_sq1.wait(dve, i)
                b0_vd.mark(ln_sum(1, G))

            def b0_sum0(i):
                b0_vb.begin(dve, i)
                b0_sq0.wait(dve, i)
                b0_vb.mark(ln_sum(0, G))

            def b0_x1(i):
                b0_vc.begin(dve, i)
                b0_mm.wait(dve, i)
                stored(b0_stx, i)
                b0_vc.mark(nc.vector.scalar_tensor_tensor(x1b, tiles(ps[:, 2, 0:W], G), 0.0, xs(i), ALU.max, ALU.add))

            def b0_inv1(i):
                b0_rt1.wait(dve, i)
                b0_vd.mark(ln_inv(1, G))

            def b0_out1(i):
                b0_vd.wait(dve, i, 2)
                stored(b0_sts, i)
                b0_vd.mark(ln_out(1, hnew[:, 0:G, :], G))
                b0_vd.end()

            def b0_inv0(i):
                b0_rt0.wait(dve, i)
                b0_vb.mark(ln_inv(0, G))

            def b0_out0(i):
                b0_vb.wait(dve, i, 2)
                b0_tr.wait(dve, i - 1)
                stored(b0_sth, i)
                b0_vb.mark(ln_out(0, stage[:, :, :], G))
                b0_vb.end()

            def b0_centre1(step):
                def body(i):
                    if step == 2:
                        b0_vd.wait(dve, i - 1)
                        b0_sq1.wait(dve, i - 1)
                    ln_centre(b0_vc, 1, x1b, G, step, i)
                return body

            def b0_centre0(step):
                def body(i):
                    if step == 0:
                        b0_va.begin(dve, i)
                        dve.wait_ge(b0_ld, 16 * (i + 1))
                    if step == 2:
                        b0_vb.wait(dve, i - 1)
                    ln_centre(b0_va, 0, xs(i), G, step, i)
                return body

            pipeline(dve, NG, [(4, b0_sum1), (1, b0_sum0), (3, b0_x1), (4, b0_inv1), (1, b0_inv0), (4, b0_out1), (1, b0_out0),
                               (3, b0_centre1(0)), (0, b0_centre0(0)), (3, b0_centre1(1)), (0, b0_centre0(1)),
                               (3, b0_centre1(2)), (0, b0_centre0(2))])

            def build(r):
                rows = drow[:, bass.ds((r % DR) * CH * P, CH * P)].rearrange("p (t e) -> p t e", e=P)

                def wide(v, p):
                    return v[:, bass.ds(r * CH, CH)].rearrange("p (t o) -> p t o", o=1).to_broadcast([p, CH, P])

                def tile_block(v):
                    return v[:, bass.ds(r * CH * P, CH * P)].rearrange("p (t e) -> p t e", e=P)

                nc.vector.tensor_tensor(tile_block(same), rows, wide(dst_f, P), ALU.is_equal).then_inc(s_same, 1)
                nc.vector.tensor_tensor(tile_block(cont), rows[0:D + 1], wide(prev_f, D + 1), ALU.is_equal).then_inc(s_same, 1)

            dve.wait_ge(s_drow0, 16 * DR)
            with dve.Fori(0, DR) as r:
                build(r)
            with dve.Fori(DR, ET // CH) as r:
                dve.wait_ge(s_drow, 16 * (r - DR + 1))
                build(r)
            dve.wait_ge(s_same, 2 * ET // CH)

            V = Q * D
            dve.wait_ge(b0_stx, 16 * NG)
            dve.wait_ge(b0_sts, 16 * NG)
            link(nc.vector.memset(aggT, 0.0))
            link(nc.vector.memset(stack[:, :], 0.0))

            def xq(i):
                return tiles(xring[:, bass.ds((i % R) * V, V)], Q)

            def a0_sum1(i):
                a0_vd.begin(dve, i)
                a0_sq1.wait(dve, i)
                a0_vd.mark(ln_sum(1, Q))

            def a0_sum0(i):
                a0_vb.begin(dve, i)
                a0_sq0.wait(dve, i)
                a0_vb.mark(ln_sum(0, Q))

            def a0_m(i):
                a0_msg.begin(dve, i)
                a0_p1.wait(dve, i)
                a0_cut.wait(dve, i - 1)
                bias = bm_all[:, :].rearrange("p (o d) -> p o d", o=1).to_broadcast([P, Q, D])
                a0_msg.mark(nc.vector.tensor_tensor(m[:, :, :], tiles(ps[:, 2, 0:V], Q), bias, ALU.add))

            def a0_inv1(i):
                a0_rt1.wait(dve, i)
                a0_vd.mark(ln_inv(1, Q))

            def a0_out1(i):
                a0_vd.wait(dve, i, 2)
                a0_vd.mark(ln_out(1, tiles(h_slot[:, bass.ds(i * V, V)], Q), Q))
                a0_vd.end()

            def a0_rest(i):
                a0_cut.wait(dve, i, 1)
                a0_msg.mark(nc.vector.tensor_tensor(mres[:, :, :], m[:, :, :], parts[:, 0, :, 0:D], ALU.subtract))

            def a0_inv0(i):
                a0_rt0.wait(dve, i)
                a0_vb.mark(ln_inv(0, Q))

            def a0_out0(i):
                a0_vb.wait(dve, i, 2)
                a0_p2.wait(dve, i - 1, 1)
                a0_vb.mark(ln_out(0, stage[:, 0:Q, :], Q))
                a0_vb.end()

            def a0_low(i):
                a0_cut.wait(dve, i, 2)
                a0_msg.mark(nc.vector.tensor_tensor(parts[:, 2, :, 0:D], mres[:, :, :], parts[:, 1, :, 0:D], ALU.subtract))
                a0_msg.end()

            def a0_update(step):
                def body(i):
                    agg = ps[:, 5, 0:Q * (D + 1)].rearrange("p (a b) -> p a b", b=D + 1)
                    if step == 0:
                        a0_upd.begin(dve, i)
                        a0_p3.wait(dve, i)
                        a0_upd.mark(nc.vector.tensor_scalar(rdeg[:, 0, :], agg[:, :, D], 1.0, None, ALU.max))
                        return
                    if step < 5:
                        a0_upd.wait(dve, i, step)
                    if step == 1:
                        a0_upd.mark(nc.vector.reciprocal(rdeg[:, 1, :], rdeg[:, 0, :]))
                    elif step == 2:
                        wide = rdeg[:, 1, :].rearrange("p (n o) -> p n o", o=1).to_broadcast([P, Q, D])
                        a0_upd.mark(nc.vector.tensor_tensor(fin[:, 0:Q, :], agg[:, :, 0:D], wide, ALU.mult))
                    elif step == 3:
                        a0_upd.mark(nc.vector.tensor_tensor(fin[:, 0:Q, :], tiles(ps[:, 6, 0:V], Q), fin[:, 0:Q, :], ALU.add))
                    elif step == 4:
                        stored(a0_stx, i)
                        a0_upd.mark(nc.vector.scalar_tensor_tensor(x1b[:, 0:Q, :], fin[:, 0:Q, :], 0.0, xq(i), ALU.max, ALU.add))
                    else:
                        if step == 5:
                            a0_upd.wait(dve, i, 5)
                        if step == 7:
                            a0_vd.wait(dve, i - 1)
                        ln_centre(a0_upd, 1, x1b[:, 0:Q, :], Q, step - 5, i)
                return body

            def a0_run(j):
                def body(i):
                    if j == 0:
                        a0_sum.begin(dve, i)
                        a0_p2.wait(dve, i)
                        a0_p3.wait(dve, i - 1)
                    else:
                        a0_sum.wait(dve, i, j)
                    before = (j + Q - 1) % Q * P + P - 1
                    c = slice(j * P, (j + 1) * P)
                    a0_sum.mark(nc.vector.scalar_tensor_tensor(
                        aggT[0:D + 1, c], cont[:, bass.ds((i * Q + j) * P, P)], aggT[0:D + 1, before:before + 1],
                        ps[0:D + 1, 4, c], ALU.mult, ALU.add))
                return body

            def a0_centre0(step):
                def body(i):
                    if step == 0:
                        a0_va.begin(dve, i)
                        dve.wait_ge(a0_quad, i + 1)
                    if step == 2:
                        a0_vb.wait(dve, i - 1)
                    ln_centre(a0_va, 0, xq(i), Q, step, i)
                return body

            pipeline(dve, NQ, [(1, a0_m), (4, a0_sum1), (1, a0_sum0), (1, a0_rest), (4, a0_inv1), (4, a0_out1), (1, a0_low),
                               (1, a0_inv0), (0, a0_centre0(0)), (1, a0_out0), (0, a0_centre0(1)), (3, a0_update(0)),
                               (0, a0_centre0(2)), (3, a0_update(1)), (2, a0_run(0)), (3, a0_update(2)), (2, a0_run(1)),
                               (3, a0_update(3)), (2, a0_run(2)), (3, a0_update(4)), (2, a0_run(3)),
                               (3, a0_update(5)), (3, a0_update(6)), (3, a0_update(7))])

            dve.wait_ge(s_tailnow, 16)
            link(nc.vector.tensor_tensor(tail_f[:, 0:1], tail_now[:, :], slot_row[:, ET - 1:ET], ALU.is_equal))
            link(nc.vector.tensor_scalar(tail_f[:, 1:2], cand[:, :], -float(SKIP), None, ALU.add))
            link(nc.vector.tensor_tensor(tail_f[:, 2:3], tail_f[:, 0:1], tail_f[:, 1:2], ALU.mult))
            link(nc.vector.tensor_scalar(tail_f[:, 3:4], tail_f[:, 2:3], float(SKIP), None, ALU.add))
            link(nc.vector.tensor_tensor(own_idx[:, ET - 1:ET], own_idx[:, ET - 1:ET], tail_f[:, 3:4], ALU.min))

            link(nc.vector.memset(hT_b[D:2 * D, :], 0.0))
            nc.vector.memset(hT_b[D:D + 1, :], 1.0).then_inc(s_ones, 1)
            for k in range(STEPS):
                last = k == STEPS - 1
                at = lambda i: i + k * NQ
                if k:
                    a_gate.wait(dve, k * NQ - 1)
                link(nc.vector.memset(stack[0:D, Q * P - 1:Q * P], 0.0))

                def rest(i):
                    a_res.begin(dve, at(i))
                    a_cut.wait(dve, at(i), 1)
                    a_res.link(nc.vector.tensor_tensor(mres[:, :, :], m[:, :, :], parts[:, 0, :, 0:D], ALU.subtract))

                def low(i):
                    a_cut.wait(dve, at(i), 2)
                    a_res.mark(nc.vector.tensor_tensor(parts[:, 2, :, 0:D], mres[:, :, :], parts[:, 1, :, 0:D], ALU.subtract))
                    a_res.end()

                def blend_nodes(i):
                    b_new.begin(dve, at(i))
                    h = tiles(nring[:, bass.ds((at(i) % 4) * H * D, H * D)], H)
                    b_tanh.wait(dve, at(i))
                    b_new.mark(nc.vector.tensor_tensor(blend_b[:, :, :], h, cn_b, ALU.subtract))

                def blend_nodes2(i):
                    b_new.wait(dve, at(i), 1)
                    b_new.mark(nc.vector.tensor_tensor(blend_b[:, :, :], blend_b[:, :, :], rz_b[:, :, D:2 * D], ALU.mult))

                def blend_nodes3(i):
                    b_new.wait(dve, at(i), 2)
                    stored(b_st, at(i))
                    b_new.mark(nc.vector.tensor_tensor(hnew[:, :, :], blend_b[:, :, :], cn_b, ALU.add))
                    b_new.end()
                    if last:
                        b_new.wait(dve, at(i))
                        dve.wait_ge(b_ld1, 16 * (i + 1))
                        x1 = tiles(xring_b[:, bass.ds((at(i) % 4) * H * D, H * D)], H)
                        nc.vector.tensor_tensor(fin[:, :, :], hnew[:, :, :], x1, ALU.add).then_inc(b_fin, 1)

                def pre_slots(i):
                    a_pre.begin(dve, at(i))
                    a_sig.wait(dve, at(i))
                    a_pre.mark(nc.vector.tensor_tensor(pre[:, :, :], gates_a()[:, :, 2 * D:3 * D], rz[:, :, 0:D], ALU.mult))

                def pre_slots2(i):
                    a_pre.wait(dve, at(i), 1)
                    a_pre.mark(nc.vector.tensor_tensor(pre[:, :, :], gates_a()[:, :, 3 * D:4 * D], pre[:, :, :], ALU.add))
                    a_pre.end()

                def run_sum(j):
                    def body(i):
                        if j == 0:
                            a_sum.begin(dve, at(i))
                            a_agg.wait(dve, at(i))
                            a_gate.wait(dve, at(i) - 1)
                        else:
                            a_sum.wait(dve, at(i), j)
                        before = (j + Q - 1) % Q * P + P - 1
                        c = slice(j * P, (j + 1) * P)
                        a_sum.mark(nc.vector.scalar_tensor_tensor(
                            stack[0:D, c], cont[0:D, bass.ds((i * Q + j) * P, P)], stack[0:D, before:before + 1],
                            ps[0:D, 3, c], ALU.mult, ALU.add))
                    return body

                def blend_slots(step):
                    def body(i):
                        h = tiles(h_slot[:, bass.ds(i * V, V)], Q)
                        if step == 0:
                            a_new.begin(dve, at(i))
                            a_tanh.wait(dve, at(i))
                            a_new.mark(nc.vector.tensor_tensor(blend[:, :, :], h, cn[:, :, :], ALU.subtract))
                        else:
                            a_new.wait(dve, at(i), step)
                            if step == 1:
                                a_new.mark(nc.vector.tensor_tensor(blend[:, :, :], blend[:, :, :], rz[:, :, D:2 * D], ALU.mult))
                            else:
                                a_new.mark(nc.vector.tensor_tensor(h, blend[:, :, :], cn[:, :, :], ALU.add))
                    return body

                def pre_nodes(u):
                    def body(i):
                        if u == 0:
                            b_pre.begin(dve, at(i))
                        half = slice(u * Q, (u + 1) * Q)
                        b_sig.wait(dve, at(i), u + 1)
                        b_tanh.wait(dve, at(i) - 1)
                        b_pre.mark(nc.vector.tensor_tensor(pre_b[:, half, :], gates_b()[:, :, 2 * D:3 * D],
                                                           rz_b[:, half, 0:D], ALU.mult))
                    return body

                def pre_nodes_bias(u):
                    def body(i):
                        half = slice(u * Q, (u + 1) * Q)
                        b_pre.wait(dve, at(i), 2 * u + 1)
                        b_pre.mark(nc.vector.tensor_tensor(pre_b[:, half, :], pre_b[:, half, :],
                                                           bin_all[:, :].rearrange("p (o d) -> p o d", o=1).to_broadcast([P, Q, D]), ALU.add))
                    return body

                def by_type(t):
                    def body(i):
                        if t == 0:
                            a_msg.begin(dve, at(i))
                            a_msg.mark(nc.vector.tensor_copy(tm_st[:, :, :], tmask[:, :, bass.ds(i * Q, Q)]))
                            return
                        if t == 1:
                            a_m0.wait(dve, at(i))
                        a_msg.wait(dve, at(i), t)
                        hold(dve)
                        all_t = psf[:, 512:1536].rearrange("p (a t d) -> p a t d", t=NT, d=D)
                        mask = tm_st[:, t - 1, :].rearrange("p (n o) -> p n o", o=1).to_broadcast([P, Q, D])
                        a_msg.mark(nc.vector.copy_predicated(m[:, :, :], mask, all_t[:, :, t, :]))
                    return body

                pipeline(dve, NQ, [(2, blend_nodes), (2, rest), (2, blend_nodes2), (2, low), (2, blend_nodes3), (3, pre_slots),
                                   (1, pre_nodes(0)), (3, pre_slots2), (1, pre_nodes_bias(0)), (2, run_sum(0)), (2, run_sum(1)),
                                   (3, blend_slots(0)), (2, run_sum(2)), (3, blend_slots(1)), (2, run_sum(3)),
                                   (3, blend_slots(2)), (1, by_type(0)), (1, by_type(1)), (1, pre_nodes(1)),
                                   (1, by_type(2)), (1, pre_nodes_bias(1)), (1, by_type(3))])

            def f_add(i, ring_free):
                dve.wait_ge(f_ld, 16 * (i + 1))
                slot = (i % R) * V
                nc.vector.tensor_tensor(ring[:, bass.ds(slot, V)], h_slot[:, bass.ds(i * V, V)],
                                        nring[:, bass.ds((i % 4) * V, V)], ALU.add).then_inc(f_v, 1)

            a_new.wait(dve, NQ * STEPS - 1)
            a_stg.wait(dve, NQ * STEPS - 1)
            for q in range(R):
                f_add(q, None)
            with dve.Fori(1, NR) as r:
                for q in range(R):
                    dve.wait_ge(f_sc[q], 16 * Q * r)
                    f_add(r * R + q, None)

        @block.tensor
        def _(pe):
            pe.wait_ge(s_setup, 24)
            pe.wait_ge(s_const, 16 * len(consts))
            pe.wait_ge(s_prep, 23)

            def transposes(src, n, bank):
                hold(pe)
                for j in range(n):
                    b, c = (bank + j // 3, j % 3) if n == G else (bank, j)
                    last = nc.tensor.transpose(ps[0:D, b, c * P:(c + 1) * P], src[:, j, :], ident[:, :])
                return last

            def b0_transpose(i):
                b0_vb.wait(pe, i)
                b0_ev.wait(pe, i - 1)
                b0_tr.begin(pe, i)
                b0_tr.mark(transposes(stage, G, 0))

            def b0_own(i):
                b0_ev.wait(pe, i)
                b0_vc.wait(pe, i - 1, 1)
                for j in range(G):
                    last = nc.tensor.matmul(ps[:, 2, j * D:(j + 1) * D], hT[:, j * P:(j + 1) * P], wa1[:, :], start=True, stop=True)
                b0_mm.begin(pe, i)
                b0_mm.mark(last)

            pipeline(pe, NG, [(3, b0_own), (2, b0_transpose)])

            def a0_0(i):
                a0_p0.begin(pe, i)
                a0_he.wait(pe, i)
                a0_ev.wait(pe, i - 1)
                for j in range(Q):
                    last = nc.tensor.transpose(ps[:, 0, j * P:(j + 1) * P], he[:, j, :], ident[:, :])
                a0_p0.mark(last)

            def a0_1(i):
                a0_p1.begin(pe, i)
                a0_ev.wait(pe, i)
                a0_msg.wait(pe, i - 1, 1)
                for j in range(Q):
                    last = nc.tensor.matmul(ps[:, 2, j * D:(j + 1) * D], heT[:, j * P:(j + 1) * P], wm[:, :], start=True, stop=True)
                a0_p1.mark(last)

            def sums(i, wide, bank):
                for j in range(Q):
                    for part in range(3):
                        last = nc.tensor.matmul(ps[0:wide, bank, j * P:(j + 1) * P], parts[:, part, j, 0:wide],
                                                same[:, bass.ds((i * Q + j) * P, P)], start=part == 0, stop=part == 2)
                return last

            def a0_2(i):
                a0_p2.begin(pe, i)
                a0_vb.wait(pe, i)
                a0_evh.wait(pe, i - 1)
                a0_p2.mark(transposes(stage, Q, 1))

            def a0_2s(i):
                a0_msg.wait(pe, i)
                a0_sum.wait(pe, i - 1)
                a0_p2.mark(sums(i, D + 1, 4))
                a0_p2.end()

            def a0_3(i):
                a0_p3.begin(pe, i)
                a0_sum.wait(pe, i)
                a0_evh.wait(pe, i)
                a0_upd.wait(pe, i - 1, 4)
                for j in range(Q):
                    nc.tensor.matmul(ps[:, 5, j * (D + 1):(j + 1) * (D + 1)], aggT[:, j * P:(j + 1) * P], wa2[:, :], start=True, stop=True)
                for j in range(Q):
                    last = nc.tensor.matmul(ps[:, 6, j * D:(j + 1) * D], hT[:, j * P:(j + 1) * P], wa1[:, :], start=True, stop=True)
                a0_p3.mark(last)

            pe.wait_ge(s_same, 2 * ET // CH)
            pipeline(pe, NQ, [(1, a0_1), (2, a0_2), (2, a0_2s), (3, a0_3), (0, a0_0)])

            a0_vd.wait(pe, NQ - 1)
            pe.wait_ge(s_ones, 1)
            for k in range(STEPS):
                at = lambda i: i + k * NQ

                def one(steps, it, last):
                    steps.begin(pe, it)
                    steps.mark(last)

                def transpose_slots(i):
                    a_stgh.wait(pe, at(i))
                    if isinstance(i, int) and i == NQ - 1:
                        a_evh.wait(pe, at(i) - 1)
                    else:
                        b_ev.wait(pe, at(i) + 1)
                    one(a_trh, at(i), transposes(stage2, Q, 0))

                def transpose_nodes(u):
                    def body(i):
                        if u == 0:
                            b_stg.wait(pe, at(i))
                            a_evh.wait(pe, at(i) - 2)
                            if isinstance(i, int) and i == 1:
                                b_ev.wait(pe, at(0))
                            b_tr.begin(pe, at(i))
                        else:
                            a_ev.wait(pe, at(i))
                        b_tr.mark(transposes(stage_b[:, u * Q:(u + 1) * Q, :], Q, 0))
                    return body

                def transpose_src(i):
                    a_stg.wait(pe, at(i))
                    b_ev.wait(pe, at(i), 1)
                    one(a_tr, at(i), transposes(stage, Q, 0))

                def messages(i):
                    a_ev.wait(pe, at(i))
                    a_msg.wait(pe, at(i) - 1)
                    for j in range(Q):
                        last = nc.tensor.matmul(psf[:, 512 + j * 256:768 + j * 256], hT[:, j * P:(j + 1) * P], wl[:, :],
                                                start=True, stop=True)
                    one(a_mm, at(i), last)

                def tile_sums(i):
                    a_res.wait(pe, at(i))
                    a_sum.wait(pe, at(i) - 1)
                    one(a_agg, at(i), sums(i, D, 3))

                def gates_slots(i):
                    a_sum.wait(pe, at(i))
                    a_evh.wait(pe, at(i))
                    a_pre.wait(pe, at(i) - 1)
                    for j in range(Q):
                        o = gates_a()[:, j, :]
                        nc.tensor.matmul(o, stack[:, j * P:(j + 1) * P], wg[:, :], start=True, stop=False)
                        last = nc.tensor.matmul(o, ones3[:, :], bias3[:, :], start=False, stop=True)
                    one(a_gate, at(i), last)

                def gates_nodes(u):
                    def body(i):
                        b_ev.wait(pe, at(i), u + 1)
                        if u == 0:
                            b_pre.wait(pe, at(i) - 1, 3)
                            b_gate.begin(pe, at(i))
                        else:
                            b_pre.wait(pe, at(i), 1)
                        for j in range(Q):
                            last = nc.tensor.matmul(gates_b()[:, j, 0:3 * D], hT_b[:, (u * Q + j) * P:(u * Q + j + 1) * P],
                                                    wh[:, :], start=True, stop=True)
                        b_gate.mark(last)
                    return body

                pipeline(pe, NQ, [(3, gates_slots), (2, transpose_slots), (1, gates_nodes(0)), (0, transpose_nodes(0)),
                                  (2, tile_sums), (1, messages), (0, transpose_src), (1, gates_nodes(1)), (0, transpose_nodes(1))], back=3)


def kernel(x, src, dst, edge_attr_64, edge_type_4, L0_gnn_W_msg_w, L0_gnn_W_msg_b, L0_gnn_W_apply_w,
           L0_gnn_W_apply_b, L1_gnn_W, L1_gnn_b, L1_gnn_w_ih, L1_gnn_w_hh, L1_gnn_b_ih, L1_gnn_b_hh):
    import numpy as np
    import concourse.bacc as bacc
    from concourse.bass_utils import run_bass_kernel_spmd

    slots = P * ET
    pads = slots - E

    def columns(v, pad):
        v = np.concatenate([np.asarray(v), np.asarray(pad, np.int32)])
        return np.ascontiguousarray(v.reshape(ET, P).T)

    dst, src, kind = np.asarray(dst), np.asarray(src), np.asarray(edge_type_4)
    none = np.full(pads, -1, np.int32)
    tail = np.concatenate([np.arange(NB, N, dtype=np.int32), np.zeros(pads - TAIL, np.int32)])
    ea = np.concatenate([np.asarray(edge_attr_64), np.zeros((pads, D), np.float32)])
    arrays = {
        "x": np.asarray(x),
        "edge_attr": np.ascontiguousarray(ea.reshape(ET, P, D).transpose(1, 0, 2).reshape(P, ET * D)),
        "dst_col": columns(dst, none),
        "dst_next": columns(dst[1:], np.full(pads + 1, -1, np.int32)),
        "dst_row": np.concatenate([dst, np.full(pads, -2, np.int32)]).reshape(1, slots),
        "prev_last": np.concatenate([np.full(1, -3, np.int32), dst[P - 1::P][:ET - 1]]).reshape(1, ET),
        "src_col": columns(src, np.zeros(pads, np.int32)),
        "slot_node": columns(dst, tail),
        "type_col": columns(kind, np.zeros(pads, np.int32)),
        "wm_t": np.ascontiguousarray(np.asarray(L0_gnn_W_msg_w).T),
        "bm": np.asarray(L0_gnn_W_msg_b),
        "wa_t": np.ascontiguousarray(np.asarray(L0_gnn_W_apply_w).T),
        "ba": np.asarray(L0_gnn_W_apply_b),
        "wl_t": np.ascontiguousarray(np.asarray(L1_gnn_W).transpose(2, 0, 1).reshape(D, NT * D)),
        "bl": np.asarray(L1_gnn_b),
        "wih_t": np.ascontiguousarray(np.asarray(L1_gnn_w_ih).T),
        "whh_t": np.ascontiguousarray(np.asarray(L1_gnn_w_hh).T),
        "bih": np.asarray(L1_gnn_b_ih),
        "bhh": np.asarray(L1_gnn_b_hh),
    }
    nc = bacc.Bacc("TRN2", target_bir_lowering=False, num_devices=1)
    args = [nc.dram_tensor(f"in_{name}", a.shape, mybir.dt.from_np(a.dtype), kind="ExternalInput").ap()
            for name, a in arrays.items()]
    out = nc.dram_tensor("out", [N, D], F32, kind="ExternalOutput").ap()
    program(nc, *args, out)
    r = run_bass_kernel_spmd(nc, [{f"in_{name}": a for name, a in arrays.items()}], core_ids=[0])
    return r.results[0]["out"]
```
